# Optimizing a Trainium2 kernel written in Bass

```python
import numpy as np
import jax
import jax.numpy as jnp

def _softmax(x, axis=-1):
    return jax.nn.softmax(x, axis=axis)

def _gelu(x):
    return jax.nn.gelu(x, approximate=True)

def _silu(x):
    return jax.nn.silu(x)

def _sigmoid(x):
    return jax.nn.sigmoid(x)

def _layernorm(x, axis=-1, eps=1e-05):
    m = jnp.mean(x, axis=axis, keepdims=True)
    v = jnp.var(x, axis=axis, keepdims=True)
    return (x - m) / jnp.sqrt(v + eps)

def _scatter_add(tgt, idx, src, axis=0):
    return tgt.at[idx].add(src)

def _segment_sum(src, seg, n):
    return jax.ops.segment_sum(src, seg, n)
kernel_name = 'mk_early_fusion_d2_tok_img1024_r4_3d11f0'

def setup_inputs(seed: int=0):
    np.random.seed(seed)
    _w = jnp.asarray

    def _rec_inputs():
        import jax
        import jax.numpy as jnp
        _rk = jax.random.key(seed)
        x = -4.65018e-05 + 0.999886 * jax.random.normal(jax.random.fold_in(_rk, 1), (16, 3, 128, 128), jnp.float32)
        txt = 0.419162 + 1.15059 * jax.random.normal(jax.random.fold_in(_rk, 2), (16, 77, 256), jnp.float32)
        return (x, txt)
    x, txt = _rec_inputs()

    def _L0_tok_setup():
        import jax, jax.numpy as jnp
        import numpy as np
        IMG_H = 128
        IMG_W = 128
        C = 3
        PH = 16
        PW = 16
        HID = 256
        NH = IMG_H // PH
        NW = IMG_W // PW
        PD = C * PH * PW
        BATCH = 64

        def sinusoidal_pos_embed(embed_dim, grid_size_x, grid_size_y):
            gh = jnp.arange(grid_size_y)
            gw = jnp.arange(grid_size_x)
            grid = jnp.stack(jnp.meshgrid(gh, gw, indexing='ij'), axis=0)
            h_pos = grid[0].reshape(-1).astype(jnp.float32)
            w_pos = grid[1].reshape(-1).astype(jnp.float32)
            quarter = embed_dim // 4
            factor = 10000.0 ** (jnp.arange(quarter, dtype=jnp.float32) / quarter)
            h = h_pos[:, None] / factor
            w = w_pos[:, None] / factor
            return jnp.concatenate([jnp.sin(h), jnp.cos(h), jnp.sin(w), jnp.cos(w)], axis=-1)
        key = jax.random.key(seed)
        k1, k2 = jax.random.split(key, 2)
        x = jax.random.normal(k1, (BATCH, C, IMG_H, IMG_W), dtype=jnp.float32)
        Wp = jax.random.normal(k2, (HID, PD), dtype=jnp.float32) * (1.0 / np.sqrt(PD))
        b = jnp.zeros((HID,), dtype=jnp.float32)
        return {'x': x, 'Wp': Wp, 'b': b}
    _L0_tok_all = _L0_tok_setup()
    _L0_tok_in = {k: v for k, v in _L0_tok_all.items() if k in ('Wp', 'b')}
    del _L0_tok_all

    def _L0_attn_setup():
        import jax, jax.numpy as jnp
        import numpy as np
        EPS = 1e-06
        HEADS = 8
        DIM_HEAD = 64
        SCALE = 16.0
        DIM = 256
        INNER = HEADS * DIM_HEAD

        def _l2norm(t):
            return t / jnp.clip(jnp.linalg.norm(t, axis=-1, keepdims=True), 1e-12)
        key = jax.random.key(seed)
        k1, k2, k3, k4 = jax.random.split(key, 4)
        b, n = (2, 1024)
        x = jax.random.normal(k1, (b, n, DIM), dtype=jnp.float32)
        Wq = jax.random.normal(k2, (DIM, INNER), dtype=jnp.float32) * 0.02
        Wkv = jax.random.normal(k3, (DIM, 2 * INNER), dtype=jnp.float32) * 0.02
        Wo = jax.random.normal(k4, (INNER, DIM), dtype=jnp.float32) * 0.02
        return {'x': x, 'Wq': Wq, 'Wkv': Wkv, 'Wo': Wo}
    _L0_attn_all = _L0_attn_setup()
    _L0_attn_in = {k: v for k, v in _L0_attn_all.items() if k in ('Wq', 'Wkv', 'Wo')}
    del _L0_attn_all

    def _L0_ffn_setup():
        import jax, jax.numpy as jnp
        import numpy as np
        B, S, D = (2, 512, 256)
        F = 1024
        E, K = (8, 2)
        EPS = 1e-09
        key = jax.random.key(seed)
        k1, k2, k3, k4 = jax.random.split(key, 4)
        x = jax.random.normal(k1, (B, S, D), dtype=jnp.float32)
        w_gate = jax.random.normal(k2, (D, E), dtype=jnp.float32) * 0.02
        w_gate_up = jax.random.normal(k3, (E, D, 2 * F), dtype=jnp.float32) * 0.02
        w_down = jax.random.normal(k4, (E, F, D), dtype=jnp.float32) * 0.02
        return {'x': x, 'w_gate': w_gate, 'w_gate_up': w_gate_up, 'w_down': w_down}
    _L0_ffn_all = _L0_ffn_setup()
    _L0_ffn_in = {k: v for k, v in _L0_ffn_all.items() if k in ('w_gate', 'w_gate_up', 'w_down')}
    del _L0_ffn_all

    def _L1_attn_setup():
        import jax, jax.numpy as jnp
        import numpy as np
        import math
        DIM = 256
        HEADS = 16
        DIM_K = DIM // HEADS
        SEQ = 512

        def _rope_tables(seq_len, dim):
            pos = jnp.arange(seq_len, dtype=jnp.float32)[:, None]
            freqs = jnp.exp(jnp.arange(0, dim, 2, dtype=jnp.float32) * (-math.log(10000.0) / dim))
            ang = pos * freqs
            return (jnp.cos(ang), jnp.sin(ang))

        def _apply_rope(x, cos, sin):
            even = x[..., ::2]
            odd = x[..., 1::2]
            return jnp.concatenate([even * cos - odd * sin, even * sin + odd * cos], axis=-1)
        key = jax.random.key(seed)
        ks = jax.random.split(key, 6)
        B, S, D = (2, SEQ, DIM)
        scale = 1.0 / math.sqrt(D)
        return {'x': jax.random.normal(ks[0], (B, S, D), dtype=jnp.float32), 'wq': jax.random.normal(ks[1], (D, D), dtype=jnp.float32) * scale, 'wk': jax.random.normal(ks[2], (D, D), dtype=jnp.float32) * scale, 'wv': jax.random.normal(ks[3], (D, D), dtype=jnp.float32) * scale, 'wo_w': jax.random.normal(ks[4], (D, D), dtype=jnp.float32) * scale, 'wo_b': jax.random.normal(ks[5], (D,), dtype=jnp.float32) * 0.01}
    _L1_attn_all = _L1_attn_setup()
    _L1_attn_in = {k: v for k, v in _L1_attn_all.items() if k in ('wq', 'wk', 'wv', 'wo_w', 'wo_b')}
    del _L1_attn_all

    def _L1_ffn_setup():
        import jax, jax.numpy as jnp
        import numpy as np
        S, B, D, H, DH = (1024, 8, 256, 16, 64)

        def _forward(x, Wg, Wq, bq, Wkv, bkv, Wo, bo, ln_g, ln_b):
            s_len, bsz, d_model = x.shape
            n_head, _, d_head = Wq.shape
            cap = s_len // n_head
            scale = 1.0 / d_head ** 0.5
            h = jnp.transpose(x, (1, 0, 2))
            t = h
            probs = jax.nn.softmax(h @ Wg, axis=-1)
            scores = jnp.transpose(probs, (0, 2, 1))
            _, idx = jax.lax.top_k(scores, cap)
            idx = jnp.sort(idx, axis=-1)
            hg = jnp.take_along_axis(h[:, None, :, :], idx[..., None], axis=2)
            hg = jnp.transpose(hg, (1, 0, 2, 3))
            q = jnp.einsum('hbcd,hde->hbce', hg, Wq) + bq[:, None, None, :]
            kv = jnp.einsum('hbcd,hde->hbce', hg, Wkv) + bkv[:, None, None, :]
            k, v = jnp.split(kv, 2, axis=-1)
            att = jnp.einsum('hbid,hbjd->hbij', q, k) * scale
            p = jax.nn.softmax(att, axis=1)
            av = jnp.einsum('hbij,hbjd->hbid', p, v)
            ao = jnp.einsum('hbid,hde->hbie', av, Wo) + bo
            tok = jnp.transpose(idx, (1, 0, 2))
            b_ids = jnp.arange(bsz)[None, :, None]
            outs = jnp.zeros_like(t).at[b_ids, tok].add(ao)
            y = t + outs
            mu = jnp.mean(y, axis=-1, keepdims=True)
            var = jnp.var(y, axis=-1, keepdims=True)
            yn = (y - mu) * jax.lax.rsqrt(var + 1e-05) * ln_g + ln_b
            return jnp.transpose(yn, (1, 0, 2))
        key = jax.random.key(seed)
        ks = jax.random.split(key, 6)
        s = 0.02
        return {'x': jax.random.normal(ks[0], (S, B, D), jnp.float32), 'attn_mask': jnp.zeros((S, S), jnp.bool_), 'Wg': jax.random.normal(ks[1], (D, H), jnp.float32) * s, 'Wq': jax.random.normal(ks[2], (H, D, DH), jnp.float32) * s, 'bq': jnp.zeros((H, DH), jnp.float32), 'Wkv': jax.random.normal(ks[3], (H, D, 2 * DH), jnp.float32) * s, 'bkv': jnp.zeros((H, 2 * DH), jnp.float32), 'Wo': jax.random.normal(ks[4], (H, DH, D), jnp.float32) * s, 'bo': jnp.zeros((D,), jnp.float32), 'ln_g': jnp.ones((D,), jnp.float32), 'ln_b': jnp.zeros((D,), jnp.float32)}
    _L1_ffn_all = _L1_ffn_setup()
    _L1_ffn_in = {k: v for k, v in _L1_ffn_all.items() if k in ('attn_mask', 'Wg', 'Wq', 'bq', 'Wkv', 'bkv', 'Wo', 'bo', 'ln_g', 'ln_b')}
    del _L1_ffn_all
    return {'x': x, 'txt': txt, 'L0_tok_Wp': _L0_tok_in['Wp'], 'L0_tok_b': _L0_tok_in['b'], 'L0_attn_Wq': _L0_attn_in['Wq'], 'L0_attn_Wkv': _L0_attn_in['Wkv'], 'L0_attn_Wo': _L0_attn_in['Wo'], 'L0_ffn_w_gate': _L0_ffn_in['w_gate'], 'L0_ffn_w_gate_up': _L0_ffn_in['w_gate_up'], 'L0_ffn_w_down': _L0_ffn_in['w_down'], 'L1_attn_wq': _L1_attn_in['wq'], 'L1_attn_wk': _L1_attn_in['wk'], 'L1_attn_wv': _L1_attn_in['wv'], 'L1_attn_wo_w': _L1_attn_in['wo_w'], 'L1_attn_wo_b': _L1_attn_in['wo_b'], 'L1_ffn_attn_mask': _L1_ffn_in['attn_mask'], 'L1_ffn_Wg': _L1_ffn_in['Wg'], 'L1_ffn_Wq': _L1_ffn_in['Wq'], 'L1_ffn_bq': _L1_ffn_in['bq'], 'L1_ffn_Wkv': _L1_ffn_in['Wkv'], 'L1_ffn_bkv': _L1_ffn_in['bkv'], 'L1_ffn_Wo': _L1_ffn_in['Wo'], 'L1_ffn_bo': _L1_ffn_in['bo'], 'L1_ffn_ln_g': _L1_ffn_in['ln_g'], 'L1_ffn_ln_b': _L1_ffn_in['ln_b']}

def reference(x, txt, L0_tok_Wp, L0_tok_b, L0_attn_Wq, L0_attn_Wkv, L0_attn_Wo, L0_ffn_w_gate, L0_ffn_w_gate_up, L0_ffn_w_down, L1_attn_wq, L1_attn_wk, L1_attn_wv, L1_attn_wo_w, L1_attn_wo_b, L1_ffn_attn_mask, L1_ffn_Wg, L1_ffn_Wq, L1_ffn_bq, L1_ffn_Wkv, L1_ffn_bkv, L1_ffn_Wo, L1_ffn_bo, L1_ffn_ln_g, L1_ffn_ln_b):
    import jax
    import jax.numpy as jnp

    def _L0_tok_ref(x, Wp, b):
        import jax, jax.numpy as jnp
        import numpy as np
        IMG_H = 128
        IMG_W = 128
        C = 3
        PH = 16
        PW = 16
        HID = 256
        NH = IMG_H // PH
        NW = IMG_W // PW
        PD = C * PH * PW
        BATCH = 64

        def sinusoidal_pos_embed(embed_dim, grid_size_x, grid_size_y):
            gh = jnp.arange(grid_size_y)
            gw = jnp.arange(grid_size_x)
            grid = jnp.stack(jnp.meshgrid(gh, gw, indexing='ij'), axis=0)
            h_pos = grid[0].reshape(-1).astype(jnp.float32)
            w_pos = grid[1].reshape(-1).astype(jnp.float32)
            quarter = embed_dim // 4
            factor = 10000.0 ** (jnp.arange(quarter, dtype=jnp.float32) / quarter)
            h = h_pos[:, None] / factor
            w = w_pos[:, None] / factor
            return jnp.concatenate([jnp.sin(h), jnp.cos(h), jnp.sin(w), jnp.cos(w)], axis=-1)
        B = x.shape[0]
        p = x.reshape(B, C, NH, PH, NW, PW)
        p = p.transpose(0, 2, 4, 3, 5, 1)
        p = p.reshape(B, NH * NW, PH * PW * C)
        out = jnp.einsum('bnd,hd->bnh', p, Wp) + b
        pos = sinusoidal_pos_embed(HID, NW, NH)
        return out + pos

    def _L0_attn_ref(x, Wq, Wkv, Wo):
        import jax, jax.numpy as jnp
        import numpy as np
        EPS = 1e-06
        HEADS = 8
        DIM_HEAD = 64
        SCALE = 16.0
        DIM = 256
        INNER = HEADS * DIM_HEAD

        def _l2norm(t):
            return t / jnp.clip(jnp.linalg.norm(t, axis=-1, keepdims=True), 1e-12)
        b, n, _ = x.shape
        q = (x @ Wq).reshape(b, n, HEADS, DIM_HEAD).transpose(0, 2, 1, 3)
        kv = x @ Wkv
        k = kv[..., :INNER].reshape(b, n, HEADS, DIM_HEAD).transpose(0, 2, 1, 3)
        v = kv[..., INNER:].reshape(b, n, HEADS, DIM_HEAD).transpose(0, 2, 1, 3)
        q = _l2norm(q)
        k = _l2norm(k)
        logits = jnp.einsum('bhid,bhjd->bhij', q, k) * SCALE - SCALE
        p = jnp.exp(logits)
        row_sums = jnp.clip(p.sum(axis=-1, keepdims=True), EPS)
        out = jnp.einsum('bhij,bhjd->bhid', p, v) / row_sums
        out = out.transpose(0, 2, 1, 3).reshape(b, n, INNER)
        return out @ Wo

    def _L0_ffn_ref(x, w_gate, w_gate_up, w_down):
        import jax, jax.numpy as jnp
        import numpy as np
        B, S, D = (2, 512, 256)
        F = 1024
        E, K = (8, 2)
        EPS = 1e-09
        gate_logits = x @ w_gate
        gate_probs = jax.nn.softmax(gate_logits, axis=-1)
        topk_vals, topk_idx = jax.lax.top_k(gate_probs, K)
        masked = jnp.sum(jax.nn.one_hot(topk_idx, E, dtype=gate_probs.dtype) * topk_vals[..., None], axis=-2)
        denom = jnp.maximum(jnp.sum(masked, axis=-1, keepdims=True), EPS)
        gate_probs = masked / denom
        gu = jnp.einsum('bsd,edh->ebsh', x, w_gate_up)
        g, u = jnp.split(gu, 2, axis=-1)
        act = jax.nn.silu(g) * u
        expert_out = jnp.einsum('ebsf,efd->ebsd', act, w_down)
        return jnp.einsum('bse,ebsd->bsd', gate_probs, expert_out)

    def _L1_attn_ref(x, wq, wk, wv, wo_w, wo_b):
        import jax, jax.numpy as jnp
        import numpy as np
        import math
        DIM = 256
        HEADS = 16
        DIM_K = DIM // HEADS
        SEQ = 512

        def _rope_tables(seq_len, dim):
            pos = jnp.arange(seq_len, dtype=jnp.float32)[:, None]
            freqs = jnp.exp(jnp.arange(0, dim, 2, dtype=jnp.float32) * (-math.log(10000.0) / dim))
            ang = pos * freqs
            return (jnp.cos(ang), jnp.sin(ang))

        def _apply_rope(x, cos, sin):
            even = x[..., ::2]
            odd = x[..., 1::2]
            return jnp.concatenate([even * cos - odd * sin, even * sin + odd * cos], axis=-1)
        B, S, D = x.shape
        cos, sin = _rope_tables(S, D)
        Q = _apply_rope(jnp.einsum('bsd,ed->bse', x, wq), cos, sin)
        K = _apply_rope(jnp.einsum('bsd,ed->bse', x, wk), cos, sin)
        V = jnp.einsum('bsd,ed->bse', x, wv)
        Q = Q.reshape(B, S, HEADS, DIM_K).transpose(0, 2, 1, 3)
        K = K.reshape(B, S, HEADS, DIM_K).transpose(0, 2, 1, 3)
        V = V.reshape(B, S, HEADS, DIM_K).transpose(0, 2, 1, 3)
        scores = jnp.einsum('bhqd,bhkd->bhqk', Q, K) / math.sqrt(DIM_K)
        weights = jax.nn.softmax(scores, axis=-1)
        out = jnp.einsum('bhqk,bhkd->bhqd', weights, V)
        out = out.transpose(0, 2, 1, 3).reshape(B, S, D)
        return jnp.einsum('bsd,ed->bse', out, wo_w) + wo_b

    def _L1_ffn_ref(x, attn_mask, Wg, Wq, bq, Wkv, bkv, Wo, bo, ln_g, ln_b):
        import jax, jax.numpy as jnp
        import numpy as np
        S, B, D, H, DH = (1024, 8, 256, 16, 64)

        def _forward(x, Wg, Wq, bq, Wkv, bkv, Wo, bo, ln_g, ln_b):
            s_len, bsz, d_model = x.shape
            n_head, _, d_head = Wq.shape
            cap = s_len // n_head
            scale = 1.0 / d_head ** 0.5
            h = jnp.transpose(x, (1, 0, 2))
            t = h
            probs = jax.nn.softmax(h @ Wg, axis=-1)
            scores = jnp.transpose(probs, (0, 2, 1))
            _, idx = jax.lax.top_k(scores, cap)
            idx = jnp.sort(idx, axis=-1)
            hg = jnp.take_along_axis(h[:, None, :, :], idx[..., None], axis=2)
            hg = jnp.transpose(hg, (1, 0, 2, 3))
            q = jnp.einsum('hbcd,hde->hbce', hg, Wq) + bq[:, None, None, :]
            kv = jnp.einsum('hbcd,hde->hbce', hg, Wkv) + bkv[:, None, None, :]
            k, v = jnp.split(kv, 2, axis=-1)
            att = jnp.einsum('hbid,hbjd->hbij', q, k) * scale
            p = jax.nn.softmax(att, axis=1)
            av = jnp.einsum('hbij,hbjd->hbid', p, v)
            ao = jnp.einsum('hbid,hde->hbie', av, Wo) + bo
            tok = jnp.transpose(idx, (1, 0, 2))
            b_ids = jnp.arange(bsz)[None, :, None]
            outs = jnp.zeros_like(t).at[b_ids, tok].add(ao)
            y = t + outs
            mu = jnp.mean(y, axis=-1, keepdims=True)
            var = jnp.var(y, axis=-1, keepdims=True)
            yn = (y - mu) * jax.lax.rsqrt(var + 1e-05) * ln_g + ln_b
            return jnp.transpose(yn, (1, 0, 2))
        return _forward(x, Wg, Wq, bq, Wkv, bkv, Wo, bo, ln_g, ln_b)
    h = _L0_tok_ref(x, L0_tok_Wp, L0_tok_b)
    h = jnp.concatenate([h, txt], axis=1)
    h = h + _L0_attn_ref(_layernorm(h, axis=-1), L0_attn_Wq, L0_attn_Wkv, L0_attn_Wo)
    h = h + _L0_ffn_ref(_layernorm(h, axis=-1), L0_ffn_w_gate, L0_ffn_w_gate_up, L0_ffn_w_down)
    h = h + _L1_attn_ref(_layernorm(h, axis=-1), L1_attn_wq, L1_attn_wk, L1_attn_wv, L1_attn_wo_w, L1_attn_wo_b)
    h = h + _L1_ffn_ref(_layernorm(h, axis=-1), L1_ffn_attn_mask, L1_ffn_Wg, L1_ffn_Wq, L1_ffn_bq, L1_ffn_Wkv, L1_ffn_bkv, L1_ffn_Wo, L1_ffn_bo, L1_ffn_ln_g, L1_ffn_ln_b)
    return h

_drawn_inputs = setup_inputs


def setup_inputs(seed=0):
    import zlib

    import numpy as np

    out = dict(_drawn_inputs(seed))
    spreads = {'L0_tok_b': (0.0, 0.1),
     'L1_ffn_bq': (0.0, 0.8),
     'L1_ffn_bkv': (0.0, 0.8),
     'L1_ffn_bo': (0.0, 0.1),
     'L1_ffn_ln_g': (1.0, 0.2),
     'L1_ffn_ln_b': (0.0, 0.1)}
    factors = {'L0_ffn_w_gate': 2.944,
     'L1_attn_wo_b': 6.25,
     'L1_ffn_Wq': 8.0,
     'L1_ffn_Wkv': 8.0,
     'L1_ffn_Wo': 8.0}
    for name, (base, spread) in spreads.items():
        noise = np.random.default_rng([zlib.crc32(name.encode()), seed]).standard_normal(out[name].shape)
        drawn = base * np.exp(spread * noise) if base else spread * noise
        out[name] = jnp.asarray(drawn.astype(out[name].dtype))
    for name, factor in factors.items():
        out[name] = (out[name] * factor).astype(out[name].dtype)
    return out
```

```python
import concourse.bass as bass
from concourse import mybir
from contextlib import ExitStack

IMAGES = 16
PATCHES = 64
TEXT = 77
SEQ = PATCHES + TEXT
D = 256
P = 128
KC = D // P
TILES = -(-IMAGES * SEQ // P)
ROWS = TILES * P
REST = SEQ - P
PK = 768 // P
H0, DH0 = 8, 64
INNER = H0 * DH0
V0 = DH0 + 1
H1, DH1 = 16, 16
V1 = DH1 + 1
HG = P // DH1
EXPERTS = 8
F = 1024
FK = F // P
SLOT_TILES = 44
SLOTS = SLOT_TILES * P
HF, DHF = 16, 64
POS = ROWS // IMAGES
GB = P // IMAGES
PAIRS = HF // 2
EXPW = KC * 2 * F + FK * D
assert SLOT_TILES >= (2 * ROWS + EXPERTS * (P - 1)) // P and POS >= SEQ and TILES % 2 == 0
C_IDENT, C_TRI, C_BLOCK, C_HEAD, C_IOTA, C_TILE, C_Q128 = 0, 128, 256, 384, 392, 408, 452
C_WIDTH = 470


class Count:

    def __init__(self):
        self.n, self.off = 0, 0

    def next(self, k=1):
        self.n += k
        return self.off + self.n

    def enter(self, i, per):
        self.mark, self.per, self.off = self.n, per, i * per

    def leave(self, turns):
        assert self.n - self.mark == self.per, (self.n - self.mark, self.per)
        self.n, self.off = self.mark + self.per * turns, 0


def ds(start, size):
    return bass.ds(start, size)


def load_expert(nc, S, wexp, w_gu, w_down, e):
    at = (e % 2) * EXPW
    nc.gpsimd.dma_start(wexp[:, at:at + KC * 2 * F], w_gu[e, :, :]).then_inc(S(f"wexp_ld{e % 2}"), 16)
    nc.gpsimd.dma_start(wexp[:, at + KC * 2 * F:at + EXPW], w_down[e, :, :]).then_inc(S(f"wexp_ld{e % 2}"), 16)
def fusion_kernel(nc, patches, txt, pos_table, row_vectors, w_tok, w_qkv0, w_o0, w_gate, w_gu, w_down,
                  w_qkv1, w_o1, rope, w_router, w_qkvf, b_qkvf, w_of, constants, out):
    f32, i32 = mybir.dt.float32, mybir.dt.int32
    ALU, ACT, X = mybir.AluOpType, mybir.ActivationFunctionType, mybir.AxisListType.X
    ctx = ExitStack()
    with ctx:
        def sb(name, shape, dt=f32):
            return ctx.enter_context(nc.sbuf_tensor(name, shape, dt))

        def dram(name, shape):
            return nc.dram_tensor(name, shape, f32).ap()

        h0_d = dram("h0_scratch", [ROWS, D])
        v0_d = dram("v0_scratch", [ROWS, H0 * V0])
        ao0_d = dram("attn0_scratch", [ROWS, INNER])
        xs_d = dram("slot_in_scratch", [SLOTS, D])
        ys_d = dram("slot_out_scratch", [SLOTS, D])
        v1_d = dram("v1_scratch", [ROWS, H1 * V1])
        ao1_d = dram("attn1_scratch", [ROWS, D])
        x3_d = dram("x3_scratch", [ROWS, D])
        h3_d = dram("h3_scratch", [ROWS, D])
        aof_d = dram("aof_scratch", [POS * HF, D])

        psum = ctx.enter_context(nc.psum_tensor("psum", [P, 8, 512], f32))

        const = sb("const", [P, C_WIDTH])
        ident = const[:, C_IDENT:C_IDENT + P]
        tri = const[:, C_TRI:C_TRI + P]
        blockones = const[:, C_BLOCK:C_BLOCK + P]
        headmask = const[:, C_HEAD:C_HEAD + 8]
        iota = const[:, C_IOTA:C_IOTA + 16]
        tile_no = const[:, C_TILE:C_TILE + SLOT_TILES]
        q128 = const[:, C_Q128:C_Q128 + TILES]
        rowv = sb("rowv", [P, 5, D])
        ones = sb("ones", [P, P])
        zeros = sb("zeros", [P, D])
        minus16 = sb("minus16", [P, 1])
        h = sb("h", [P, TILES, D])
        wqkv = sb("wqkv", [P, KC * 3 * INNER])
        wo_sb = sb("wo_sb", [P, 4, D])
        wgate_sb = sb("wgate_sb", [P, KC, EXPERTS])
        wrout_sb = sb("wrout_sb", [P, KC, HF])
        big = sb("big", [P, 8 * ROWS])
        wexp = sb("wexp", [P, 2 * EXPW])
        xbuf = sb("xbuf", [P, 2 * D + 2 * D])
        mv = sb("mv", [P, TILES, 2])
        st6 = sb("st6", [P, TILES, 6])
        rstd = sb("rstd", [P, TILES])
        moe_tab = sb("moe_tab", [1, 2, SLOT_TILES], i32)
        end_tab = sb("end_tab", [1, EXPERTS], i32)
        slot = sb("slot", [P, 2, TILES], i32)
        gates = sb("gates", [P, 2, TILES])
        work = sb("work", [P, 10112])

        sems = {}

        def S(name):
            if name not in sems:
                sems[name] = ctx.enter_context(nc.semaphore(name))
            return sems[name]

        def view(base, at, *shape):
            n = 1
            for x in shape:
                n *= x
            v = base[:, at:at + n]
            if len(shape) == 1:
                return v
            names = "abcd"[:len(shape)]
            return v.rearrange(f"p ({' '.join(names)}) -> p {' '.join(names)}", **dict(zip(names, shape)))

        xn = view(xbuf, 0, 2, D)
        xT = view(xbuf, 2 * D, 2, KC, P)
        wqkv_sb = view(wqkv, 0, KC, 3 * INNER)
        wqkv1_sb = view(wqkv, 0, KC, 3 * D)
        wo1_sb = view(wqkv, KC * 3 * D, KC, D)
        wtok_sb = view(big, 0, PK, D)
        pt = view(work, 0, 2, PK, P)
        posb = view(work, 1536, D)
        h0s = view(work, 1792, 2, D)
        qkT = view(big, 0, 8, ROWS)
        vst = view(work, 0, 2, H0, V0)
        sq = view(work, 1040, 1024)
        qkn = view(work, 2064, 2, 1024)
        ssum = view(work, 4112, 2, 16)
        snorm = view(work, 4144, 2, 16)
        qz = view(work, 0, 2, 4, 2, SEQ)
        kz = view(work, 2256, 2, 4, SEQ)
        vm = view(work, 3384, 2, H0, V0)
        vr = view(work, 4424, 2, H0, V0)
        pm = view(work, 5464, 2, H0, SEQ)
        pr = view(work, 7720, 2, H0, SEQ)
        aom = view(xbuf, 0, 2, H0, DH0)
        aor = view(wqkv, 2048, 2, H0, DH0)
        rsum = view(work, 9976, 2, 2, H0)

        aT_in = view(work, 0, 2, INNER)
        aT = view(work, 1024, 2, 4, P)
        xn2 = view(big, 0, TILES, D)
        E8 = TILES * EXPERTS
        lg = view(work, 2048, TILES, EXPERTS)
        oh = view(work, 2048 + E8, 2, TILES, EXPERTS)
        t8 = view(work, 2048 + 3 * E8, TILES, EXPERTS)
        u8 = view(work, 2048 + 4 * E8, TILES, EXPERTS)
        mask = view(work, 2048 + 5 * E8, TILES, EXPERTS)
        ca = view(work, 2048 + 6 * E8, TILES, EXPERTS)
        cb = view(work, 2048 + 7 * E8, TILES, EXPERTS)
        rank = view(work, 2048 + 8 * E8, TILES, EXPERTS)
        RB = 2048 + 9 * E8
        r18 = view(work, RB, TILES)
        s18 = view(work, RB + 18, TILES)
        val = view(work, RB + 36, 2, TILES)
        cmp = view(work, RB + 72, EXPERTS, TILES)
        nt = view(work, RB + 216, EXPERTS)
        endf = view(work, RB + 224, EXPERTS + 1)
        ej = view(work, RB + 240, SLOT_TILES)
        ej2 = view(work, RB + 284, SLOT_TILES)
        cmpj = view(work, RB + 328, SLOT_TILES, EXPERTS)
        posf = view(work, RB + 680, 2, TILES)

        xsl = view(work, 5120, 2, D)
        sil = view(work, 5632, 2, 512)
        hid = view(work, 6656, 2, 512)
        hidT = view(work, 7680, 2, 4, P)
        yst = view(work, 8704, 2, D)
        yg = view(big, 0, 2, TILES, D)
        h0_img = h0_d[0:IMAGES * SEQ, :].rearrange("(b n) d -> b n d", n=SEQ)
        qkT1 = view(big, 2 * TILES * D, 4, ROWS)
        vst1 = view(work, 0, 2, H1, V1)
        rp = view(work, 544, 2, 3, P)
        ra = view(work, 1312, 2, 2, P)
        rb = view(work, 1824, 2, 2, P)
        qkr = view(work, 2336, 2, 4, P)
        kblk = view(wexp, 0, 2, 2, HG, SEQ)
        wts = view(wexp, 4512, 2, HG, SEQ)
        wT = view(wexp, 6768, 2, H1, SEQ)
        q1 = view(work, 3360, 2, 2, SEQ)
        v1m = view(work, 3924, 2, H1, V1)
        v1r = view(work, 4468, 2, H1, V1)
        a1m = view(work, 5012, 2, H1, DH1)
        a1r = view(work, 5524, 2, H1, DH1)
        max1 = view(work, 6036, 2, HG)
        rs1 = view(work, 6052, H1)
        a1T_in = view(work, 6100, 2, D)
        x3 = view(big, 0, TILES, D)
        xg = view(work, 0, 2, D)
        lg3 = view(work, 512, TILES, HF)
        pT = view(work, 800, 3 * P)
        uT = view(work, 1184, 3 * P)
        oT = view(work, 1568, 3 * P)
        m3 = view(work, 1952, 3 * GB)
        sel = view(work, 1980, TILES, HF)
        selb = view(work, 2268, 2, GB, HF)
        sel_all = view(work, 2524, TILES, P)
        hgT = view(big, 2 * TILES * D, KC, HF, POS)
        x3T = view(work, 4828, 2, KC, P)
        wf = view(wexp, 0, 2, KC, 3, 2 * DHF)
        wof = view(wexp, 1536, 2, D)
        bf = view(wexp, 2048, PAIRS, 3)
        hgp = view(wexp, 2072, 2, KC, 2, SEQ)
        qf = view(wexp, 3200, SEQ)
        kf = view(wexp, 3341, SEQ)
        vf = view(wexp, 3482, SEQ)
        ef = view(wexp, 3623, SEQ)
        af = view(wexp, 3764, 2, SEQ)
        mf = view(wexp, 4046, 2)
        rf = view(wexp, 4048, 2)
        aofm = view(wexp, 4052, 2, 2, D)
        aofr = view(wexp, 5076, 2, 2, D)
        aofl = view(wexp, 6100, 2, D)
        xh = view(wexp, 6612, 2, 2, D)
        sel_s = view(wexp, 7636, 2, P)
        ysum = view(big, TILES * D, TILES, D)
        hb = view(wexp, 7892, 2, D)
        o1 = view(wexp, 8404, 2, D)

        LASTB = SEQ - (TILES - 1) * GB

        def by_position(rows_d):
            return bass.AP(rows_d.tensor, 0, [[D, POS], [SEQ * D, IMAGES], [1, D]])

        block = ctx.enter_context(nc.Block())

        @block.sync
        def _(sp):
            sp.dma_start(wtok_sb, w_tok).then_inc(S("wtok_ld"), 16)
            sp.dma_start(posb, pos_table).then_inc(S("tables_ld"), 16)
            sp.dma_start(rowv[:, :, :], row_vectors).then_inc(S("tables_ld"), 16)
            with sp.Fori(0, IMAGES // 4) as i:
                for s in range(2):
                    t = 2 * i + s
                    sp.wait_ge(S("tok_ps"), t + 1)
                    sp.dma_start(pt[:, s, :, :], patches[ds(t, 1), :, :, :].rearrange("o p k n -> p (o k) n")).then_inc(S(f"pt_ld{s}"), 16)
            sp.dma_start(h0_img[:, PATCHES:SEQ, :], txt).then_inc(S("h0_st"), 16)
            sp.wait_ge(S("fills"), 3)
            sp.dma_start(h0_d[IMAGES * SEQ:ROWS, :], zeros[0:ROWS - IMAGES * SEQ, :]).then_inc(S("h0_st"), 16)
            sp.dma_start(const[:, :], constants).then_inc(S("weights_ld"), 16)
            sp.dma_start(wqkv_sb, w_qkv0).then_inc(S("weights_ld"), 16)
            sp.dma_start(wo_sb[:, :, :], w_o0).then_inc(S("weights_ld"), 16)
            sp.dma_start(wgate_sb[:, :, :], w_gate).then_inc(S("weights_ld"), 16)
            sp.dma_start(wrout_sb[:, :, :], w_router).then_inc(S("weights_ld"), 16)
            sp.wait_ge(S("h0_st"), 32)
            for s in range(2):
                sp.wait_ge(S(f"tok_st{s}"), 32 * (IMAGES // 4 + 1))
            sp.dma_start(h[:, :, :], h0_d.rearrange("(t p) d -> p t d", p=P)).then_inc(S("h_ld"), 16)
            sp.dma_start(xs_d.rearrange("(t p) d -> p t d", p=P), zeros[:, :].unsqueeze(1).to_broadcast([P, SLOT_TILES, D])).then_inc(S("zero_st"), 16)
            sp.dma_start(aof_d[SEQ * HF:POS * HF, :], zeros[0:(POS - SEQ) * HF, :]).then_inc(S("zero_st"), 16)
            with sp.Fori(0, TILES // 2) as i:
                for s in range(2):
                    t = 2 * i + s
                    sp.wait_ge(S("v0_ready"), t + 2)
                    sp.dma_start(v0_d[ds(t * P, P), :], vst[:, s, :, :].rearrange("p h v -> p (h v)")).then_inc(S(f"v0_st{s}"), 16)
            for s in range(2):
                sp.wait_ge(S(f"v0_st{s}"), 16 * (TILES // 2 + 1))
            sp.wait_ge(S("qkv_ps"), TILES)
            sp.dma_start(wqkv1_sb, w_qkv1).then_inc(S("weights1_ld"), 16)
            sp.dma_start(wo1_sb, w_o1).then_inc(S("weights1_ld"), 16)
            sp.wait_ge(S("qkT_ready"), 2 * TILES + 2)
            with sp.Fori(0, IMAGES // 2) as i:
                for s in range(2):
                    b = 2 * i + s
                    sp.wait_ge(S("pv0_ps"), 2 * b + 2)
                    sp.dma_start(vm[:, s, :, :], v0_d[ds(b * SEQ, P), :].rearrange("p (h v) -> p h v", h=H0)).then_inc(S(f"v0_ld{s}"), 16)
                    sp.dma_start(vr[0:REST, s, :, :], v0_d[ds(b * SEQ + P, REST), :].rearrange("p (h v) -> p h v", h=H0)).then_inc(S(f"v0_ld{s}"), 16)
            for s in range(2):
                sp.wait_ge(S(f"ao0_st{s}"), 32 * (IMAGES // 2 + 1))
            sp.wait_ge(S("ao0_pad"), 32)
            with sp.Fori(0, TILES // 2) as i:
                for s in range(2):
                    t = 2 * i + s
                    sp.wait_ge(S("aT_ps"), t + 1)
                    sp.dma_start(aT_in[:, s, :], ao0_d[ds(t * P, P), :]).then_inc(S(f"aT_ld{s}"), 16)
            sp.wait_ge(S("xs_st"), 16 * 2 * TILES)
            with sp.Fori(0, SLOT_TILES // 2) as i:
                for s in range(2):
                    j = 2 * i + s
                    sp.wait_ge(S("xsT_ps"), j + 1)
                    sp.dma_start(xsl[:, s, :], xs_d[ds(j * P, P), :]).then_inc(S(f"xsl_ld{s}"), 16)
            with sp.Fori(0, TILES // 2) as i:
                for s in range(2):
                    t = 2 * i + s
                    sp.wait_ge(S("qkr_ready"), t + 1)
                    sp.dma_start(rp[:, s, :, :], rope[:, ds(t, 1), :, :].rearrange("p o k n -> p (o k) n")).then_inc(S(f"rp_ld{s}"), 16)
            for s in range(2):
                sp.wait_ge(S(f"v1_st{s}"), 16 * (TILES // 2 + 1))
            with sp.Fori(0, IMAGES // 2) as i:
                for s in range(2):
                    b = 2 * i + s
                    sp.wait_ge(S("pv1_ps"), 2 * b + 2)
                    sp.dma_start(v1m[:, s, :, :], v1_d[ds(b * SEQ, P), :].rearrange("p (h v) -> p h v", h=H1)).then_inc(S(f"v1_ld{s}"), 16)
                    sp.dma_start(v1r[0:REST, s, :, :], v1_d[ds(b * SEQ + P, REST), :].rearrange("p (h v) -> p h v", h=H1)).then_inc(S(f"v1_ld{s}"), 16)
            for s in range(2):
                sp.wait_ge(S(f"a1_st{s}"), 32 * (IMAGES // 2 + 1))
            sp.wait_ge(S("a1_pad"), 16)
            with sp.Fori(0, TILES // 2) as i:
                for s in range(2):
                    t = 2 * i + s
                    sp.wait_ge(S("a1T_ps"), t + 1)
                    sp.dma_start(a1T_in[:, s, :], ao1_d[ds(t * P, P), :]).then_inc(S(f"a1T_ld{s}"), 16)
            sp.wait_ge(S("h3_ready"), 1)
            sp.dma_start(h3_d.rearrange("(t p) d -> p t d", p=P), h[:, :, :]).then_inc(S("rows3_st"), 16)
            sp.wait_ge(S("x3_ready"), 1)
            sp.dma_start(x3_d.rearrange("(t p) d -> p t d", p=P), x3).then_inc(S("rows3_st"), 16)
            sp.wait_ge(S("rows3_st"), 32)
            x3_bs = by_position(x3_d)
            h3_bs = by_position(h3_d)
            for turn, free in ((0, "x3T_ps"), (1, "hg_ps")):
                if turn:
                    sp.wait_ge(S("x3T_ps"), TILES + 2)
                with sp.Fori(0, TILES // 2) as i:
                    for s in range(2):
                        sp.wait_ge(S(free), 2 * i + s + 1)
                        sp.dma_start(xg[:, s, :], x3_bs[ds((2 * i + s) * GB, GB), :, :]).then_inc(S(f"xg_ld{s}"), 16)
            sp.dma_start(bf, b_qkvf.rearrange("p (a b) -> p a b", a=PAIRS)).then_inc(S("bf_ld"), 16)
            with sp.Fori(0, PAIRS // 2) as i:
                for s in range(2):
                    p_ = 2 * i + s
                    sp.wait_ge(S("aof_ps"), 2 * p_ + 2)
                    sp.dma_start(wf[:, s, :, :, :].rearrange("p k x n -> p (k x n)"), w_qkvf[ds(p_, 1), :, :].rearrange("o p n -> p (o n)")).then_inc(S(f"wf_ld{s}"), 16)
                    sp.dma_start(wof[:, s, :], w_of[ds(p_, 1), :, :].rearrange("o p n -> p (o n)")).then_inc(S(f"wf_ld{s}"), 16)
            for s in range(2):
                sp.wait_ge(S(f"aof_st{s}"), 32 * (PAIRS // 2 + 1))
            sp.wait_ge(S("zero_st"), 32)
            with sp.Fori(0, TILES // 2) as i:
                for s in range(2):
                    t = 2 * i + s
                    sp.wait_ge(S("y_sum"), t + 1)
                    sp.dma_start(aofl[:, s, :], aof_d[ds(t * P, P), :]).then_inc(S(f"aofl_ld{s}"), 16)
                    sp.dma_start(xh[:, s, 0, :], x3_bs[ds(t * GB, GB), :, :]).then_inc(S(f"x3b_ld{s}"), 16)
            with sp.Fori(0, TILES // 2) as i:
                for s in range(2):
                    t = 2 * i + s
                    sp.wait_ge(S("o1_ready"), t + 1)
                    sp.dma_start(xh[:, s, 1, :], h3_bs[ds(t * GB, GB), :, :]).then_inc(S(f"h3b_ld{s}"), 16)

        @block.gpsimd
        def _(pool):
            nc.gpsimd.memset(zeros[:, :], 0.0).then_inc(S("fills"), 1)
            nc.gpsimd.memset(ones[:, :], 1.0).then_inc(S("fills"), 1)
            nc.gpsimd.memset(minus16[:, :], -16.0).then_inc(S("fills"), 1)
            pool.wait_ge(S("h_ld"), 16)
            for e in range(2):
                load_expert(nc, S, wexp, w_gu, w_down, e)
            for s in range(2):
                pool.wait_ge(S(f"v0_st{s}"), 16 * (TILES // 2 + 1))
            pool.wait_ge(S("qkT_ready"), 2 * TILES + 2)
            with pool.Fori(0, IMAGES // 2) as i:
                for s in range(2):
                    b = 2 * i + s
                    pool.wait_ge(S("pv0_ps"), 2 * b + 2)
                    nc.gpsimd.tensor_copy(kz[:, s, :, :], qkT[:, 4:8, ds(b * SEQ, SEQ)])
                    for r in range(2):
                        m = nc.gpsimd.tensor_tensor(qz[:, s, :, r, :], qkT[:, 0:4, ds(b * SEQ, SEQ)],
                                                    blockones[:, 64 * r:64 * r + 1].unsqueeze(2).to_broadcast([P, 4, SEQ]), ALU.mult)
                    m.then_inc(S("qks_ready"), 1)
            pool.sem_inc(S("xn2_kept"), 2)
            pool.wait_ge(S("qks_ready"), IMAGES)
            with pool.Fori(0, TILES // 2) as i:
                for s in range(2):
                    t = 2 * i + s
                    pool.wait_ge(S("xn2_ready"), t + 1)
                    nc.gpsimd.tensor_copy(xn2[:, t, :], xn[:, s, :]).then_inc(S("xn2_kept"), 1)
            pool.wait_ge(S("slots_ready"), 1)
            pool.wait_ge(S("xn2_kept"), TILES + 2)
            pool.wait_ge(S("zero_st"), 32)
            for k in range(2):
                for t in range(TILES):
                    nc.gpsimd.indirect_dma_start(xs_d, bass.IndirectOffsetOnAxis(slot[:, k, t:t + 1], 0), xn2[:, t, :], None).then_inc(S("xs_st"), 16)
            pool.wait_ge(S("tables_ready"), 1)
            for e in range(2):
                pool.wait_ge(S(f"wexp_ld{e}"), 32)
                pool.sem_inc(S("wexp_ready"), 1)
            for e in range(2, EXPERTS):
                done = pool.value_load(end_tab[0:1, e - 2:e - 1], min_val=2, max_val=2 * SLOT_TILES + 2)
                pool.wait_ge(S("dn_ps"), done)
                pool.sem_inc(S("wexp_free"), 1)
                load_expert(nc, S, wexp, w_gu, w_down, e)
                pool.wait_ge(S(f"wexp_ld{e % 2}"), 32 * (e // 2 + 1))
                pool.sem_inc(S("wexp_ready"), 1)
            pool.wait_ge(S("xs_st"), 16 * 2 * TILES)
            for s in range(2):
                pool.wait_ge(S(f"ys_st{s}"), 16 * (SLOT_TILES // 2 + 1))
            for t in range(TILES):
                for k in range(2):
                    nc.gpsimd.indirect_dma_start(yg[:, k, t, :], None, ys_d, bass.IndirectOffsetOnAxis(slot[:, k, t:t + 1], 0)).then_inc(S("yg_ld"), 16)
            pool.wait_ge(S("qkT1_ready"), TILES + 2)
            pool.wait_ge(S("xn1_ready"), TILES)
            nc.gpsimd.tensor_tensor(h[:, :, :], h[:, :, :], rowv[:, 1, :].unsqueeze(1).to_broadcast([P, TILES, D]), ALU.add).then_inc(S("h_bias"), 1)
            with pool.Fori(0, IMAGES // 2) as i:
                for s in range(2):
                    b = 2 * i + s
                    pool.wait_ge(S("pv1_ps"), 2 * b + 2)
                    nc.gpsimd.tensor_copy(q1[:, s, :, :], qkT1[:, 0:2, ds(b * SEQ, SEQ)])
                    for g in range(2):
                        m = nc.gpsimd.tensor_tensor(kblk[:, s, g, :, :], qkT1[:, 2 + g, ds(b * SEQ, SEQ)].unsqueeze(1).to_broadcast([P, HG, SEQ]),
                                                    headmask.unsqueeze(2).to_broadcast([P, HG, SEQ]), ALU.mult)
                    m.then_inc(S("q1_ready"), 1)
            pool.wait_ge(S("hgT_ready"), 2 * TILES + 4)
            with pool.Fori(0, PAIRS // 2) as i:
                for s in range(2):
                    p_ = 2 * i + s
                    pool.wait_ge(S("qkvf_ps"), p_ + 1)
                    nc.gpsimd.tensor_copy(hgp[:, s, :, :, :], hgT[:, :, ds(2 * p_, 2), 0:SEQ]).then_inc(S("hgp_ready"), 1)
            with pool.Fori(0, TILES // 2) as i:
                for s in range(2):
                    t = 2 * i + s
                    pool.wait_ge(S("yf_ps"), t + 1)
                    nc.gpsimd.tensor_copy(sel_s[:, s, :], sel_all[:, t, :]).then_inc(S("sel_ready"), 1)
            with pool.Fori(0, TILES // 2) as i:
                for s in range(2):
                    t = 2 * i + s
                    pool.wait_ge(S(f"h3b_ld{s}"), 16 * (i + 1))
                    pool.wait_ge(S("o1_ready"), t + 1)
                    nc.gpsimd.tensor_tensor(hb[:, s, :], xh[:, s, 1, :], rowv[:, 4, :], ALU.add).then_inc(S("hb_ready"), 1)

        @block.scalar
        def _(act):
            for s in range(2):
                act.sem_inc(S(f"tok_st{s}"), 32)
            with act.Fori(0, IMAGES // 4) as i:
                for s in range(2):
                    t = 2 * i + s
                    act.wait_ge(S("tok_ready"), t + 3)
                    for r in range(2):
                        act.dma_start(h0_img[ds(2 * t + r, 1), 0:PATCHES, :].rearrange("o n d -> (o n) d"),
                                      h0s[64 * r:64 * r + 64, s, :]).then_inc(S(f"tok_st{s}"), 16)
            act.sem_inc(S("xT_ready"), 2)
            act.sem_inc(S("qkT_ready"), 2)
            act.sem_inc(S("v0_ready"), 1)
            for s in range(2):
                act.sem_inc(S(f"v0_st{s}"), 16)
            act.wait_ge(S("ln_stats"), 1)
            nc.scalar.activation(rstd[:, :], mv[:, :, 1], ACT.Sqrt).then_inc(S("ln_root"), 1)

            def keep_qkT(t):
                for a in range(2):
                    act.wait_ge(S("qkT_ps"), 2 * t + a + 5)
                    nc.scalar.activation(qkT[:, 4 * a:4 * a + 4, ds(t * P, P)],
                                         psum[:, 6 + a, :].rearrange("p (k n) -> p k n", k=4), ACT.Copy).then_inc(S("qkT_ready"), 1)

            def qkv_step(t, s, i, first=False):
                act.wait_ge(S("xT_ps"), t + 1)
                nc.scalar.activation(xT[:, s, :, :], psum[:, 5, 0:D].rearrange("p (k n) -> p k n", k=KC), ACT.Copy).then_inc(S("xT_ready"), 1)
                act.wait_ge(S("qkv_ps"), t + 1)
                if not first:
                    act.wait_ge(S("ssum_ready"), t)
                nc.scalar.activation(sq.rearrange("p (a n) -> p a n", a=2), psum[:, 2 * s:2 * s + 2, :], ACT.Square).then_inc(S("sq_ready"), 1)
                act.wait_ge(S(f"v0_st{s}"), 16 * (i + 1))
                act.wait_ge(S("v0_ones"), 1)
                nc.scalar.activation(vst[:, s, :, 0:DH0], psum[:, 4, :].rearrange("p (h v) -> p h v", h=H0), ACT.Copy).then_inc(S("v0_ready"), 1)
                act.wait_ge(S("ssum_ready"), t + 1)
                nc.scalar.activation(snorm[:, s, :], ssum[:, s, :], ACT.Sqrt).then_inc(S("snorm_ready"), 1)
                if not first:
                    keep_qkT(t - 1)

            qkv_step(0, 0, 0, True)
            with act.Fori(0, TILES // 2 - 1) as i:
                qkv_step(2 * i + 1, 1, i)
                qkv_step(2 * i + 2, 0, i + 1)
            qkv_step(TILES - 1, 1, TILES // 2 - 1)
            keep_qkT(TILES - 1)
            for s in range(2):
                act.sem_inc(S(f"ao0_st{s}"), 32)

            def exp0(b, s):
                act.wait_ge(S("pv0_ps"), 2 * b + 2)
                for part, (p_, rows, base) in enumerate(((pm, P, 0), (pr, REST, 3))):
                    act.wait_ge(S("s0_ps"), 2 * b + part + 1)
                    nc.scalar.activation(p_[0:rows, s, 0:6, :].rearrange("p (a c) i -> p a (c i)", c=3),
                                         psum[0:rows, base:base + 2, 0:3 * SEQ], ACT.Exp, bias=minus16[0:rows, :], scale=16.0).then_inc(S("p0_ready"), 1)
                    nc.scalar.activation(p_[0:rows, s, 6:8, :].rearrange("p c i -> p (c i)"),
                                         psum[0:rows, base + 2, 0:2 * SEQ], ACT.Exp, bias=minus16[0:rows, :], scale=16.0).then_inc(S("p0_ready"), 1)

            def store_ao0(b, s):
                act.wait_ge(S("ao0_ready"), 2 * b + 4)
                act.dma_start(ao0_d[ds(b * SEQ, P), :], aom[:, s, :, :].rearrange("p h v -> p (h v)")).then_inc(S(f"ao0_st{s}"), 16)
                act.dma_start(ao0_d[ds(b * SEQ + P, REST), :], aor[0:REST, s, :, :].rearrange("p h v -> p (h v)")).then_inc(S(f"ao0_st{s}"), 16)

            act.dma_start(ao0_d[IMAGES * SEQ:ROWS, 0:D], zeros[0:ROWS - IMAGES * SEQ, :]).then_inc(S("ao0_pad"), 16)
            act.dma_start(ao0_d[IMAGES * SEQ:ROWS, D:INNER], zeros[0:ROWS - IMAGES * SEQ, :]).then_inc(S("ao0_pad"), 16)
            act.wait_ge(S("fills"), 3)
            with act.Fori(0, IMAGES // 2) as i:
                for s in range(2):
                    exp0(2 * i + s, s)
                    store_ao0(2 * i + s, s)
            act.sem_inc(S("aT_ready"), 2)

            def keep_aT(t, s):
                act.wait_ge(S("aT_ps"), t + 3)
                act.wait_ge(S("o0_ps"), t + 1)
                nc.scalar.activation(aT[:, s, :, :], psum[:, s, :].rearrange("p (k n) -> p k n", k=4), ACT.Copy).then_inc(S("aT_ready"), 1)

            with act.Fori(0, TILES // 2) as i:
                for s in range(2):
                    keep_aT(2 * i + s, s)
            act.wait_ge(S("ln_stats"), 2)
            nc.scalar.activation(rstd[:, :], mv[:, :, 1], ACT.Sqrt).then_inc(S("ln_root"), 1)
            act.sem_inc(S("xT2_ready"), 2)
            with act.Fori(0, TILES // 2) as i:
                for s in range(2):
                    t = 2 * i + s
                    act.wait_ge(S("xT2_ps"), t + 3)
                    act.wait_ge(S("gate_ps"), t + 1)
                    nc.scalar.activation(xT[:, s, :, :], psum[:, 4 + s, 0:D].rearrange("p (k n) -> p k n", k=KC), ACT.Copy).then_inc(S("xT2_ready"), 1)
            act.wait_ge(S("lg_ready"), 1)
            nc.scalar.activation(lg, lg, ACT.Exp).then_inc(S("lg_exp"), 1)
            act.sem_inc(S("xsT_ready"), 2)
            act.sem_inc(S("sil_ready"), 2)
            act.sem_inc(S("y_ready"), 2)
            for s in range(2):
                act.sem_inc(S(f"ys_st{s}"), 16)

            def keep_xsT(j, s):
                act.wait_ge(S("xsT_ps"), j + 3)
                nc.scalar.activation(xT[:, s, :, :], psum[:, 6, 0:D].rearrange("p (k n) -> p k n", k=KC), ACT.Copy).then_inc(S("xsT_ready"), 1)

            def silu(n, s):
                act.wait_ge(S("gu_ps"), n + 1)
                act.wait_ge(S("hid_ready"), n + 1)
                nc.scalar.activation(sil[:, s, :], psum[:, 2 * s, :], ACT.Silu).then_inc(S("sil_ready"), 1)

            def keep_y(j, s, i):
                act.wait_ge(S("dn_ps"), 2 * j + 4)
                act.wait_ge(S(f"ys_st{s}"), 16 * (i + 1))
                nc.scalar.activation(yst[:, s, :], psum[:, 7, 0:D], ACT.Copy).then_inc(S("y_ready"), 1)
                act.wait_ge(S("y_ready"), j + 3)
                act.dma_start(ys_d[ds(j * P, P), :], yst[:, s, :]).then_inc(S(f"ys_st{s}"), 16)

            keep_xsT(0, 0)
            keep_xsT(1, 1)
            silu(0, 0)
            silu(1, 1)
            with act.Fori(0, SLOT_TILES // 2 - 1) as i:
                silu(4 * i + 2, 0)
                keep_xsT(2 * i + 2, 0)
                silu(4 * i + 3, 1)
                keep_y(2 * i, 0, i)
                silu(4 * i + 4, 0)
                keep_xsT(2 * i + 3, 1)
                silu(4 * i + 5, 1)
                keep_y(2 * i + 1, 1, i)
            silu(2 * SLOT_TILES - 2, 0)
            silu(2 * SLOT_TILES - 1, 1)
            keep_y(SLOT_TILES - 2, 0, SLOT_TILES // 2 - 1)
            keep_y(SLOT_TILES - 1, 1, SLOT_TILES // 2 - 1)
            act.wait_ge(S("ln_stats"), 3)
            nc.scalar.activation(rstd[:, :], mv[:, :, 1], ACT.Sqrt).then_inc(S("ln_root"), 1)
            act.sem_inc(S("x1T_ready"), 2)
            act.sem_inc(S("qkT1_ready"), 2)
            act.sem_inc(S("v1_ready"), 2)
            for s in range(2):
                act.sem_inc(S(f"v1_st{s}"), 16)

            def keep_qkT1(t):
                act.wait_ge(S("qkT1_ps"), t + 3)
                nc.scalar.activation(qkT1[:, :, ds(t * P, P)], psum[:, 6, :].rearrange("p (k n) -> p k n", k=4), ACT.Copy).then_inc(S("qkT1_ready"), 1)

            def qkv1_step(t, s, i, first=False):
                act.wait_ge(S("x1T_ps"), t + 3)
                nc.scalar.activation(xT[:, s, :, :], psum[:, 5, 0:D].rearrange("p (k n) -> p k n", k=KC), ACT.Copy).then_inc(S("x1T_ready"), 1)
                act.wait_ge(S("qkv1_ps"), t + 1)
                act.wait_ge(S(f"v1_st{s}"), 16 * (i + 1))
                act.wait_ge(S("v1_ones"), 1)
                nc.scalar.activation(vst1[:, s, :, 0:DH1], psum[:, 2 * s + 1, 0:D].rearrange("p (h v) -> p h v", h=H1), ACT.Copy).then_inc(S("v1_ready"), 1)
                act.wait_ge(S("v1_ready"), t + 3)
                act.dma_start(v1_d[ds(t * P, P), :], vst1[:, s, :, :].rearrange("p h v -> p (h v)")).then_inc(S(f"v1_st{s}"), 16)
                if not first:
                    keep_qkT1(t - 1)

            qkv1_step(0, 0, 0, True)
            with act.Fori(0, TILES // 2 - 1) as i:
                qkv1_step(2 * i + 1, 1, i)
                qkv1_step(2 * i + 2, 0, i + 1)
            qkv1_step(TILES - 1, 1, TILES // 2 - 1)
            keep_qkT1(TILES - 1)
            for s in range(2):
                act.sem_inc(S(f"a1_st{s}"), 32)
            act.sem_inc(S("wT_ready"), 1)
            act.dma_start(ao1_d[IMAGES * SEQ:ROWS, :], zeros[0:ROWS - IMAGES * SEQ, :]).then_inc(S("a1_pad"), 16)

            def exp1(k, u):
                rows = P if u < 2 else REST
                act.wait_ge(S("s1_read"), k + 3)
                w = wts[0:rows, u % 2, :, :].rearrange("p h j -> p (h j)")
                nc.scalar.activation(w, w, ACT.Exp, scale=DH1 ** -0.5).then_inc(S("p1_ready"), 1)

            def keep_wT(b, u):
                g = u % 2
                if u < 2:
                    for n in range(4):
                        rows, lo = (P if n < 2 else REST), HG * g + 4 * (n % 2)
                        act.wait_ge(S("wT_ps"), 10 * b + 4 * u + n + 3)
                        nc.scalar.activation(wT[0:rows, n // 2, lo:lo + 4, 0:P], psum[0:rows, 6, :].rearrange("p (h i) -> p h i", h=4), ACT.Copy).then_inc(S("wT_ready"), 1)
                else:
                    for n, rows in enumerate((P, REST)):
                        act.wait_ge(S("wT_ps"), 10 * b + 8 + (u - 2) + 3)
                        m = nc.scalar.activation(wT[0:rows, n, HG * g:HG * g + HG, P:SEQ],
                                                 psum[0:rows, 6, n * P:n * P + HG * REST].rearrange("p (h i) -> p h i", h=HG), ACT.Copy)
                    m.then_inc(S("wT_ready"), 1)

            def store_a1(b, s):
                act.wait_ge(S("a1_ready"), 2 * b + 4)
                act.dma_start(ao1_d[ds(b * SEQ, P), :], a1m[:, s, :, :].rearrange("p h v -> p (h v)")).then_inc(S(f"a1_st{s}"), 16)
                act.dma_start(ao1_d[ds(b * SEQ + P, REST), :], a1r[0:REST, s, :, :].rearrange("p h v -> p (h v)")).then_inc(S(f"a1_st{s}"), 16)

            def image1_act(b, s, last=False):
                exp1(4 * b + 1, 1)
                keep_wT(b, 0)
                exp1(4 * b + 2, 2)
                keep_wT(b, 1)
                exp1(4 * b + 3, 3)
                keep_wT(b, 2)
                if not last:
                    exp1(4 * b + 4, 0)
                keep_wT(b, 3)
                store_a1(b, s)

            exp1(0, 0)
            with act.Fori(0, IMAGES // 2 - 1) as i:
                image1_act(2 * i, 0)
                image1_act(2 * i + 1, 1)
            image1_act(IMAGES - 2, 0)
            image1_act(IMAGES - 1, 1, True)
            act.sem_inc(S("a1T_ready"), 2)
            with act.Fori(0, TILES // 2) as i:
                for s in range(2):
                    t = 2 * i + s
                    act.wait_ge(S("a1T_ps"), t + 3)
                    act.wait_ge(S("o1_ps"), t + 1)
                    nc.scalar.activation(xT[:, s, :, :], psum[:, s, 0:D].rearrange("p (k n) -> p k n", k=KC), ACT.Copy).then_inc(S("a1T_ready"), 1)
            act.wait_ge(S("ln_stats"), 4)
            nc.scalar.activation(rstd[:, :], mv[:, :, 1], ACT.Sqrt).then_inc(S("ln_root"), 1)
            act.sem_inc(S("x3T_ready"), 2)
            with act.Fori(0, TILES // 2) as i:
                for s in range(2):
                    t = 2 * i + s
                    act.wait_ge(S("x3T_ps"), t + 3)
                    act.wait_ge(S("rt_ps"), t + 1)
                    nc.scalar.activation(x3T[:, s, :, :], psum[:, s, 0:D].rearrange("p (k n) -> p k n", k=KC), ACT.Copy).then_inc(S("x3T_ready"), 1)
            act.wait_ge(S("lg3_ready"), 1)
            nc.scalar.activation(lg3, lg3, ACT.Exp).then_inc(S("lg3_exp"), 1)
            act.sem_inc(S("hgT_ready"), 4)
            with act.Fori(0, TILES // 2) as i:
                for s in range(2):
                    t = 2 * i + s
                    act.wait_ge(S("hg_ps"), t + 3)
                    for k in range(KC):
                        nc.scalar.activation(hgT[:, k, :, ds(t * GB, GB)].rearrange("p h b -> p b h"),
                                             psum[:, s, k * P:(k + 1) * P].rearrange("p (b h) -> p b h", b=GB), ACT.Copy).then_inc(S("hgT_ready"), 1)
            for s in range(2):
                act.sem_inc(S(f"aof_st{s}"), 32)
            with act.Fori(0, PAIRS // 2) as i:
                for s in range(2):
                    p_ = 2 * i + s
                    act.wait_ge(S("mf_ready"), p_ + 1)
                    act.wait_ge(S("af_ready"), p_ + 1)
                    nc.scalar.activation(ef, psum[:, 6, 0:SEQ], ACT.Exp, bias=mf[:, s:s + 1], scale=DHF ** -0.5, accum_out=rf[:, s:s + 1]).then_inc(S("ef_ready"), 1)
                    act.wait_ge(S("aof_ready"), 2 * p_ + 4)
                    aof_bh = aof_d.rearrange("(b h) d -> b h d", h=HF)
                    act.dma_start(aof_bh[0:P, ds(2 * p_, 2), :], aofm[:, s, :, :]).then_inc(S(f"aof_st{s}"), 16)
                    act.dma_start(aof_bh[P:SEQ, ds(2 * p_, 2), :], aofr[0:REST, s, :, :]).then_inc(S(f"aof_st{s}"), 16)
            act.wait_ge(S("ln_stats"), 5)
            nc.scalar.activation(rstd[:, :], mv[:, :, 1], ACT.Sqrt).then_inc(S("ln_root"), 1)
            out_bs = out.rearrange("s b d -> b s d")
            for s in range(2):
                act.sem_inc(S(f"out_st{s}"), 16)
            with act.Fori(0, TILES // 2 - 1) as i:
                for s in range(2):
                    t = 2 * i + s
                    act.wait_ge(S("o1_ready"), t + 3)
                    act.dma_start(out_bs[ds(t * GB, GB), :, :], o1[:, s, :]).then_inc(S(f"out_st{s}"), 16)
            for s, t, n in ((0, TILES - 2, GB), (1, TILES - 1, LASTB)):
                act.wait_ge(S("o1_ready"), t + 3)
                act.dma_start(out_bs[t * GB:t * GB + n, :, :], o1[0:n * IMAGES, s, :]).then_inc(S(f"out_st{s}"), 16)
            for s in range(2):
                act.wait_ge(S(f"out_st{s}"), 16 * (TILES // 2 + 1))

        @block.vector
        def _(dve):
            c = Count()

            def step(ins):
                ins.then_inc(S("dve_step"), 1)
                dve.wait_ge(S("dve_step"), c.next())

            def inverse_root(n):
                for t in range(TILES):
                    last = nc.vector.bn_aggr(mv[:, t, :], st6[:, t, :])
                step(last)
                step(nc.vector.tensor_scalar(mv[:, :, 1], mv[:, :, 1], 1e-5, None, ALU.add))
                dve.sem_inc(S("ln_stats"), 1)
                dve.wait_ge(S("ln_root"), n)
                step(nc.vector.reciprocal(rstd[:, :], rstd[:, :]))

            def normed(out_, t):
                return nc.vector.tensor_scalar(out_, h[:, t, :], mv[:, t, 0:1], rstd[:, ds(t, 1)], ALU.subtract, ALU.mult)

            dve.wait_ge(S("tables_ld"), 32)
            step(nc.vector.tensor_tensor(posb, posb, rowv[:, 0, :], ALU.add))
            dve.sem_inc(S("tok_ready"), 2)
            with dve.Fori(0, IMAGES // 4) as i:
                for s in range(2):
                    t = 2 * i + s
                    dve.wait_ge(S("tok_ps"), t + 3)
                    dve.wait_ge(S(f"tok_st{s}"), 32 * (i + 1))
                    nc.vector.tensor_tensor(h0s[:, s, :], psum[:, s, 0:D], posb, ALU.add).then_inc(S("tok_ready"), 1)
            for s in range(2):
                dve.wait_ge(S(f"tok_st{s}"), 32 * (IMAGES // 4 + 1))
                m = nc.vector.memset(vst[:, s, :, DH0:V0], 1.0)
            m.then_inc(S("v0_ones"), 1)
            dve.wait_ge(S("h_ld"), 16)
            with dve.Fori(0, TILES) as t:
                c.enter(t, 1)
                step(nc.vector.bn_stats(st6[:, t, :], h[:, t, :]))
                c.leave(TILES)
            inverse_root(1)
            normed(xn[:, 0, :], 0).then_inc(S("xn_ready"), 1)
            dve.sem_inc(S("qkn_ready"), 2)

            def qk_step(t, s, last=False):
                if not last:
                    dve.wait_ge(S("xT_ps"), t)
                    normed(xn[:, 1 - s, :], t + 1).then_inc(S("xn_ready"), 1)
                dve.wait_ge(S("sq_ready"), t + 1)
                nc.vector.tensor_reduce(ssum[:, s, :], sq.rearrange("p (g d) -> p g d", d=DH0), X, ALU.add).then_inc(S("ssum_ready"), 1)
                dve.wait_ge(S("snorm_ready"), t + 1)
                step(nc.vector.tensor_scalar(snorm[:, s, :], snorm[:, s, :], 1e-12, None, ALU.max))
                step(nc.vector.reciprocal(snorm[:, s, :], snorm[:, s, :]))
                dve.wait_ge(S("qkT_ps"), 2 * t + 2)
                nc.vector.tensor_tensor(qkn[:, s, :].rearrange("p (g d) -> p g d", d=DH0),
                                        psum[:, 2 * s:2 * s + 2, :].rearrange("p a (g d) -> p (a g) d", d=DH0),
                                        snorm[:, s, :].unsqueeze(2).to_broadcast([P, 16, DH0]), ALU.mult).then_inc(S("qkn_ready"), 1)

            with dve.Fori(0, TILES // 2 - 1) as i:
                c.enter(i, 4)
                qk_step(2 * i, 0)
                qk_step(2 * i + 1, 1)
                c.leave(TILES // 2 - 1)
            qk_step(TILES - 2, 0)
            qk_step(TILES - 1, 1, True)
            dve.sem_inc(S("ao0_ready"), 2)
            with dve.Fori(0, IMAGES // 2) as i:
                c.enter(i, 8)
                for s in range(2):
                    b = 2 * i + s
                    dve.wait_ge(S(f"ao0_st{s}"), 32 * (i + 1))
                    for part, (o_, rows) in enumerate(((aom, P), (aor, REST))):
                        dve.wait_ge(S("pv0_ps"), 2 * b + part + 5)
                        pv = psum[0:rows, 6:8, 0:4 * V0].rearrange("p a (h v) -> p a h v", v=V0)
                        rs = rsum[0:rows, s, part, :]
                        step(nc.vector.tensor_scalar(rs.rearrange("p (a h) -> p a h", a=2), pv[:, :, :, DH0], 1e-6, None, ALU.max))
                        step(nc.vector.reciprocal(rs, rs))
                        nc.vector.tensor_tensor(o_[0:rows, s, :, :].rearrange("p (a h) v -> p a h v", a=2), pv[:, :, :, 0:DH0],
                                                rs.rearrange("p (a h) -> p a h", a=2).unsqueeze(3).to_broadcast([rows, 2, 4, DH0]),
                                                ALU.mult).then_inc(S("ao0_ready"), 1)
                c.leave(IMAGES // 2)
            dve.sem_inc(S("h1_ready"), 2)
            with dve.Fori(0, TILES // 2) as i:
                c.enter(i, 4)
                for s in range(2):
                    t = 2 * i + s
                    dve.wait_ge(S("o0_ps"), t + 3)
                    step(nc.vector.tensor_tensor(h[:, t, :], psum[:, 2 + s, 0:D], h[:, t, :], ALU.add))
                    dve.sem_inc(S("h1_ready"), 1)
                    step(nc.vector.bn_stats(st6[:, t, :], h[:, t, :]))
                c.leave(TILES // 2)
            inverse_root(2)
            with dve.Fori(0, TILES // 2) as i:
                for s in range(2):
                    t = 2 * i + s
                    dve.wait_ge(S("xT2_ps"), t + 1)
                    dve.wait_ge(S("xn2_kept"), t + 1)
                    normed(xn[:, s, :], t).then_inc(S("xn2_ready"), 1)
            dve.wait_ge(S("gate_ps"), TILES + 2)

            def over8(x, n=TILES):
                return x.unsqueeze(2).to_broadcast([P, n, EXPERTS])

            step(nc.vector.tensor_copy(lg, psum[:, 6, 0:E8].rearrange("p (t e) -> p t e", e=EXPERTS)))
            step(nc.vector.tensor_reduce(r18, lg, X, ALU.max))
            step(nc.vector.tensor_tensor(lg, lg, over8(r18), ALU.subtract))
            dve.sem_inc(S("lg_ready"), 1)
            dve.wait_ge(S("lg_exp"), 1)
            step(nc.vector.tensor_reduce(r18, lg, X, ALU.add))
            step(nc.vector.reciprocal(r18, r18))
            step(nc.vector.tensor_tensor(lg, lg, over8(r18), ALU.mult))
            experts = iota[:, 0:EXPERTS].unsqueeze(1).to_broadcast([P, TILES, EXPERTS])
            for k in range(2):
                step(nc.vector.tensor_reduce(val[:, k, :], lg, X, ALU.max))
                step(nc.vector.tensor_tensor(t8, lg, over8(val[:, k, :]), ALU.is_equal))
                step(nc.vector.tensor_scalar(u8, experts, -16.0, None, ALU.add))
                step(nc.vector.tensor_tensor(u8, u8, t8, ALU.mult))
                step(nc.vector.tensor_reduce(s18, u8, X, ALU.min))
                step(nc.vector.tensor_scalar(s18, s18, 16.0, None, ALU.add))
                step(nc.vector.tensor_tensor(oh[:, k, :, :], experts, over8(s18), ALU.is_equal))
                if k == 0:
                    step(nc.vector.scalar_tensor_tensor(out=lg, in0=oh[:, 0, :, :], scalar=-4.0, in1=lg, op0=ALU.mult, op1=ALU.add))
            step(nc.vector.tensor_tensor(s18, val[:, 0, :], val[:, 1, :], ALU.add))
            step(nc.vector.tensor_scalar(s18, s18, 1e-9, None, ALU.max))
            step(nc.vector.reciprocal(s18, s18))
            step(nc.vector.tensor_tensor(gates[:, :, :], val, s18.unsqueeze(1).to_broadcast([P, 2, TILES]), ALU.mult))
            step(nc.vector.tensor_tensor(mask, oh[:, 0, :, :], oh[:, 1, :, :], ALU.add))
            dve.sem_inc(S("mask_ready"), 1)
            dve.wait_ge(S("rank_ps"), 1)
            counts = psum[:, 5, 0:E8].rearrange("p (t e) -> p t e", e=EXPERTS)
            step(nc.vector.tensor_copy(ca, counts))
            x, y = ca, cb
            shift = 1
            while shift < TILES:
                step(nc.vector.tensor_tensor(y[:, shift:, :], x[:, shift:, :], x[:, 0:TILES - shift, :], ALU.add))
                step(nc.vector.tensor_copy(y[:, 0:shift, :], x[:, 0:shift, :]))
                x, y, shift = y, x, 2 * shift
            total = x[:, TILES - 1, :]
            step(nc.vector.tensor_tensor(cmp, total.unsqueeze(2).to_broadcast([P, EXPERTS, TILES]),
                                         q128.unsqueeze(1).to_broadcast([P, EXPERTS, TILES]), ALU.is_gt))
            step(nc.vector.tensor_reduce(nt, cmp, X, ALU.add))
            step(nc.vector.tensor_scalar(nt, nt, 1.0, None, ALU.max))
            step(nc.vector.memset(endf[:, 0:1], 0.0))
            for e in range(EXPERTS):
                step(nc.vector.tensor_tensor(endf[:, e + 1:e + 2], endf[:, e:e + 1], nt[:, e:e + 1], ALU.add))
            step(nc.vector.tensor_tensor(y, x, counts, ALU.subtract))
            step(nc.vector.tensor_tensor(y, psum[:, 7, 0:E8].rearrange("p (t e) -> p t e", e=EXPERTS), y, ALU.add))
            step(nc.vector.scalar_tensor_tensor(out=y, in0=endf[:, 0:EXPERTS].unsqueeze(1).to_broadcast([P, TILES, EXPERTS]),
                                                scalar=float(P), in1=y, op0=ALU.mult, op1=ALU.add))
            for k in range(2):
                step(nc.vector.tensor_tensor(t8, oh[:, k, :, :], y, ALU.mult))
                step(nc.vector.tensor_reduce(posf[:, k, :], t8, X, ALU.add))
            step(nc.vector.tensor_copy(slot[:, :, :], posf))
            dve.sem_inc(S("slots_ready"), 1)
            step(nc.vector.tensor_tensor(cmpj, tile_no.unsqueeze(2).to_broadcast([P, SLOT_TILES, EXPERTS]),
                                         endf[:, 1:].unsqueeze(1).to_broadcast([P, SLOT_TILES, EXPERTS]), ALU.is_ge))
            step(nc.vector.tensor_reduce(ej, cmpj, X, ALU.add))
            step(nc.vector.tensor_scalar(ej, ej, float(EXPERTS - 1), None, ALU.min))
            step(nc.vector.tensor_scalar(moe_tab[:, 0, :], ej[0:1, :], 1.0, None, ALU.add))
            step(nc.vector.tensor_scalar(ej2, ej, 1.0, None, ALU.is_ge))
            for e in range(2, EXPERTS):
                step(nc.vector.scalar_tensor_tensor(out=ej2, in0=ej, scalar=float(e), in1=ej2, op0=ALU.is_ge,
                                                    op1=ALU.add if e % 2 else ALU.subtract, **({} if e % 2 else {"reverse1": True})))
            step(nc.vector.tensor_scalar(moe_tab[:, 1, :], ej2[0:1, :], float(EXPW), None, ALU.mult))
            step(nc.vector.tensor_scalar(end_tab[:, :], endf[0:1, 1:], 2.0, 2.0, ALU.mult, ALU.add))
            dve.sem_inc(S("tables_ready"), 1)
            dve.sem_inc(S("hid_ready"), 2)
            dve.sem_inc(S("hidT_ready"), 2)

            def hidden(n, s):
                dve.wait_ge(S("sil_ready"), n + 3)
                dve.wait_ge(S("hidT_ps"), n + 1)
                nc.vector.tensor_tensor(hid[:, s, :], sil[:, s, :], psum[:, 2 * s + 1, :], ALU.mult).then_inc(S("hid_ready"), 1)

            def keep_hidT(n, s):
                dve.wait_ge(S("hidT_ps"), n + 3)
                dve.wait_ge(S("dn_ps"), n + 1)
                nc.vector.tensor_copy(hidT[:, s, :, :], psum[:, 4 + s, :].rearrange("p (k n) -> p k n", k=4)).then_inc(S("hidT_ready"), 1)

            hidden(0, 0)
            with dve.Fori(0, SLOT_TILES - 1) as j:
                hidden(2 * j + 1, 1)
                keep_hidT(2 * j, 0)
                hidden(2 * j + 2, 0)
                keep_hidT(2 * j + 1, 1)
            hidden(2 * SLOT_TILES - 1, 1)
            keep_hidT(2 * SLOT_TILES - 2, 0)
            keep_hidT(2 * SLOT_TILES - 1, 1)
            dve.wait_ge(S("yg_ld"), 32 * TILES)
            with dve.Fori(0, TILES) as t:
                c.enter(t, 3)
                for k in range(2):
                    step(nc.vector.scalar_tensor_tensor(out=h[:, t, :], in0=yg[:, k, t, :], scalar=gates[:, k, ds(t, 1)], in1=h[:, t, :],
                                                        op0=ALU.mult, op1=ALU.add))
                step(nc.vector.bn_stats(st6[:, t, :], h[:, t, :]))
                c.leave(TILES)
            inverse_root(3)
            for s in range(2):
                m = nc.vector.memset(vst1[:, s, :, DH1:V1], 1.0)
            m.then_inc(S("v1_ones"), 1)
            dve.sem_inc(S("qkr_ready"), 2)
            normed(xn[:, 0, :], 0).then_inc(S("xn1_ready"), 1)

            def rope_step(t, s, i, last=False):
                if not last:
                    dve.wait_ge(S("x1T_ps"), t + 2)
                    normed(xn[:, 1 - s, :], t + 1).then_inc(S("xn1_ready"), 1)
                dve.wait_ge(S("qkv1_ps"), t + 1)
                dve.wait_ge(S(f"rp_ld{s}"), 16 * (i + 1))
                dve.wait_ge(S("qkr_ready"), t + 2)
                qk = psum[:, 2 * s, :].rearrange("p (a e n) -> p a e n", a=2, e=2)
                nc.vector.tensor_tensor(ra, qk, rp[:, s, 0:2, :].unsqueeze(1).to_broadcast([P, 2, 2, P]), ALU.mult)
                step(nc.vector.tensor_tensor(rb, qk, rp[:, s, 1:3, :].unsqueeze(1).to_broadcast([P, 2, 2, P]), ALU.mult))
                dve.wait_ge(S("qkT1_ps"), t + 1)
                o_ = qkr[:, s, :, :].rearrange("p (a e) n -> p a e n", a=2)
                step(nc.vector.tensor_tensor(o_[:, :, 0, :], ra[:, :, 0, :], ra[:, :, 1, :], ALU.subtract))
                nc.vector.tensor_tensor(o_[:, :, 1, :], rb[:, :, 0, :], rb[:, :, 1, :], ALU.add).then_inc(S("qkr_ready"), 1)

            with dve.Fori(0, TILES // 2 - 1) as i:
                c.enter(i, 4)
                rope_step(2 * i, 0, i)
                rope_step(2 * i + 1, 1, i)
                c.leave(TILES // 2 - 1)
            rope_step(TILES - 2, 0, TILES // 2 - 1)
            rope_step(TILES - 1, 1, TILES // 2 - 1, True)
            dve.sem_inc(S("s1_read"), 2)
            dve.sem_inc(S("a1_ready"), 2)

            def less_max(b, u):
                k, rows, base = 4 * b + u, (P if u < 2 else REST), 3 * (u % 2)
                dve.wait_ge(S("s1_ps"), k + 1)
                dve.wait_ge(S("wT_ps"), 10 * b + (1, 2, 6, 10)[u])
                sc = psum[0:rows, base:base + 2, 0:3 * SEQ].rearrange("p a (h j) -> p a h j", j=SEQ)
                sc2 = psum[0:rows, base + 2, 0:2 * SEQ].rearrange("p (h j) -> p h j", j=SEQ)
                nc.vector.tensor_reduce(max1[0:rows, u % 2, 0:6].rearrange("p (a h) -> p a h", a=2), sc, X, ALU.max)
                step(nc.vector.tensor_reduce(max1[0:rows, u % 2, 6:8], sc2, X, ALU.max))
                nc.vector.tensor_tensor(wts[0:rows, u % 2, 0:6, :].rearrange("p (a h) j -> p a h j", a=2), sc,
                                        max1[0:rows, u % 2, 0:6].rearrange("p (a h) -> p a h", a=2).unsqueeze(3).to_broadcast([rows, 2, 3, SEQ]), ALU.subtract)
                nc.vector.tensor_tensor(wts[0:rows, u % 2, 6:8, :], sc2, max1[0:rows, u % 2, 6:8].unsqueeze(2).to_broadcast([rows, 2, SEQ]),
                                        ALU.subtract).then_inc(S("s1_read"), 1)

            def divide1(b, s, i, part):
                o_, rows = ((a1m, P), (a1r, REST))[part]
                dve.wait_ge(S("pv1_ps"), 2 * b + part + 5)
                dve.wait_ge(S(f"a1_st{s}"), 32 * (i + 1))
                pv = psum[0:rows, 7, 0:H1 * V1].rearrange("p (h v) -> p h v", v=V1)
                step(nc.vector.reciprocal(rs1[0:rows, :], pv[:, :, DH1]))
                nc.vector.tensor_tensor(o_[0:rows, s, :, :], pv[:, :, 0:DH1], rs1[0:rows, :].unsqueeze(2).to_broadcast([rows, H1, DH1]),
                                        ALU.mult).then_inc(S("a1_ready"), 1)

            def image1_dve(b, s, i, last=False):
                less_max(b, 2)
                less_max(b, 3)
                divide1(b, s, i, 0)
                if not last:
                    less_max(b + 1, 0)
                    less_max(b + 1, 1)
                divide1(b, s, i, 1)

            less_max(0, 0)
            less_max(0, 1)
            with dve.Fori(0, IMAGES // 2 - 1) as i:
                c.enter(i, 12)
                image1_dve(2 * i, 0, i)
                image1_dve(2 * i + 1, 1, i)
                c.leave(IMAGES // 2 - 1)
            image1_dve(IMAGES - 2, 0, IMAGES // 2 - 1)
            image1_dve(IMAGES - 1, 1, IMAGES // 2 - 1, True)
            dve.sem_inc(S("h3_tile"), 2)
            dve.wait_ge(S("h_bias"), 1)
            with dve.Fori(0, TILES // 2) as i:
                c.enter(i, 4)
                for s in range(2):
                    t = 2 * i + s
                    dve.wait_ge(S("o1_ps"), t + 3)
                    step(nc.vector.tensor_tensor(h[:, t, :], psum[:, 2 + s, 0:D], h[:, t, :], ALU.add))
                    dve.sem_inc(S("h3_tile"), 1)
                    step(nc.vector.bn_stats(st6[:, t, :], h[:, t, :]))
                c.leave(TILES // 2)
            dve.sem_inc(S("h3_ready"), 1)
            inverse_root(4)
            with dve.Fori(0, TILES) as t:
                c.enter(t, 1)
                step(normed(x3[:, t, :], t))
                c.leave(TILES)
            dve.sem_inc(S("x3_ready"), 1)
            dve.wait_ge(S("rt_ps"), TILES + 2)

            def over16(x):
                return x.unsqueeze(2).to_broadcast([P, TILES, HF])

            step(nc.vector.tensor_copy(lg3, psum[:, 4, 0:TILES * HF].rearrange("p (t e) -> p t e", e=HF)))
            step(nc.vector.tensor_reduce(rstd[:, :], lg3, X, ALU.max))
            step(nc.vector.tensor_tensor(lg3, lg3, over16(rstd[:, :]), ALU.subtract))
            dve.sem_inc(S("lg3_ready"), 1)
            dve.wait_ge(S("lg3_exp"), 1)
            step(nc.vector.tensor_reduce(rstd[:, :], lg3, X, ALU.add))
            step(nc.vector.reciprocal(rstd[:, :], rstd[:, :]))
            step(nc.vector.tensor_tensor(lg3, lg3, over16(rstd[:, :]), ALU.mult))
            dve.sem_inc(S("pr3_ready"), 1)
            dve.wait_ge(S("pr3T_ps"), 1)
            for rows, lo, n in ((P, 0, 2), (32, 2, 1)):
                def part(x):
                    return x[0:rows, lo * P:(lo + n) * P].rearrange("p (b s) -> p b s", s=IMAGES)

                nb = n * GB
                best = m3[0:rows, lo * GB:lo * GB + nb]
                over = best.unsqueeze(2).to_broadcast([rows, nb, IMAGES])
                images = iota[0:rows, :].unsqueeze(1).to_broadcast([rows, nb, IMAGES])
                step(nc.vector.tensor_copy(part(pT), psum[0:rows, 5, lo * P:(lo + n) * P].rearrange("p (b s) -> p b s", s=IMAGES)))
                step(nc.vector.tensor_reduce(best, part(pT), X, ALU.max))
                step(nc.vector.tensor_tensor(part(pT), part(pT), over, ALU.is_equal))
                step(nc.vector.tensor_scalar(part(uT), images, -float(IMAGES), None, ALU.add))
                step(nc.vector.tensor_tensor(part(uT), part(uT), part(pT), ALU.mult))
                step(nc.vector.tensor_reduce(best, part(uT), X, ALU.min))
                step(nc.vector.tensor_scalar(best, best, float(IMAGES), None, ALU.add))
                step(nc.vector.tensor_tensor(part(oT), images, over, ALU.is_equal))
            dve.sem_inc(S("oT_ready"), 1)
            dve.wait_ge(S("sel_ps"), 1)
            step(nc.vector.tensor_copy(sel, psum[:, 6, 0:TILES * HF].rearrange("p (t h) -> p t h", h=HF)))
            dve.sem_inc(S("sel_all_ready"), 2)
            with dve.Fori(0, TILES // 2) as i:
                for s in range(2):
                    t = 2 * i + s
                    dve.wait_ge(S("hg_ps"), t + 1)
                    nc.vector.tensor_tensor(selb[:, s, :, :], sel[:, t, :].unsqueeze(1).to_broadcast([P, GB, HF]),
                                            headmask.unsqueeze(2).to_broadcast([P, GB, HF]), ALU.mult).then_inc(S("selb_ready"), 1)
                    dve.wait_ge(S("hg_ps"), t + 3)
                    nc.vector.tensor_copy(sel_all[:, t, :], psum[:, 2 + s, 0:P]).then_inc(S("sel_all_ready"), 1)
            dve.wait_ge(S("bf_ld"), 16)
            dve.sem_inc(S("vf_ready"), 2)
            dve.sem_inc(S("af_ready"), 1)
            dve.sem_inc(S("aof_ready"), 2)
            with dve.Fori(0, PAIRS // 2) as i:
                c.enter(i, 8)
                for s in range(2):
                    p_ = 2 * i + s
                    dve.wait_ge(S("qkvf_ps"), p_ + 3)
                    step(nc.vector.tensor_scalar(qf, psum[:, 0, 0:SEQ], bf[:, ds(p_, 1), 0:1].rearrange("p a b -> p (a b)"), None, ALU.add))
                    nc.vector.scalar_tensor_tensor(out=kf, in0=psum[:, 1, 0:SEQ], scalar=bf[:, ds(p_, 1), 1:2].rearrange("p a b -> p (a b)"),
                                                   in1=qf, op0=ALU.add, op1=ALU.mult).then_inc(S("kf_ready"), 1)
                    step(nc.vector.tensor_scalar(vf, psum[:, 2, 0:SEQ], bf[:, ds(p_, 1), 2:3].rearrange("p a b -> p (a b)"), None, ALU.add))
                    dve.sem_inc(S("vf_ready"), 1)
                    dve.wait_ge(S("attf_ps"), p_ + 1)
                    step(nc.vector.tensor_reduce(mf[:, s:s + 1], psum[:, 6, 0:SEQ], X, ALU.max))
                    nc.vector.tensor_scalar(mf[:, s:s + 1], mf[:, s:s + 1], -(DHF ** -0.5), None, ALU.mult).then_inc(S("mf_ready"), 1)
                    dve.wait_ge(S("ef_ready"), p_ + 1)
                    step(nc.vector.reciprocal(rf[:, s:s + 1], rf[:, s:s + 1]))
                    dve.wait_ge(S("aof_ps"), 2 * p_ + 2)
                    nc.vector.scalar_tensor_tensor(out=af[:, s, :], in0=ef, scalar=rf[:, s:s + 1], in1=vf, op0=ALU.mult, op1=ALU.mult).then_inc(S("af_ready"), 1)
                    dve.wait_ge(S(f"aof_st{s}"), 32 * (i + 1))
                    for n, (o_, rows, bank) in enumerate(((aofm, P, 4), (aofr, REST, 6))):
                        dve.wait_ge(S("aof_ps"), 2 * p_ + n + 5)
                        nc.vector.tensor_tensor(o_[0:rows, s, :, :], psum[0:rows, bank:bank + 2, 0:D],
                                                rowv[0:rows, 2, :].unsqueeze(1).to_broadcast([rows, 2, D]), ALU.add).then_inc(S("aof_ready"), 1)
                c.leave(PAIRS // 2)
            dve.sem_inc(S("y_sum"), 2)
            dve.sem_inc(S("o1_ready"), 2)
            with dve.Fori(0, TILES // 2) as i:
                c.enter(i, 2)
                for s in range(2):
                    t = 2 * i + s
                    dve.wait_ge(S("yf_ps"), t + 3)
                    dve.wait_ge(S(f"x3b_ld{s}"), 16 * (i + 1))
                    nc.vector.tensor_tensor(ysum[:, t, :], psum[:, s, 0:D], xh[:, s, 0, :], ALU.add).then_inc(S("y_sum"), 1)
                    dve.wait_ge(S("y_sum"), t + 3)
                    step(nc.vector.bn_stats(st6[:, t, :], ysum[:, t, :]))
                c.leave(TILES // 2)
            inverse_root(5)
            with dve.Fori(0, TILES // 2) as i:
                c.enter(i, 4)
                for s in range(2):
                    t = 2 * i + s
                    dve.wait_ge(S(f"out_st{s}"), 16 * (i + 1))
                    step(nc.vector.tensor_scalar(o1[:, s, :], ysum[:, t, :], mv[:, t, 0:1], rstd[:, ds(t, 1)], ALU.subtract, ALU.mult))
                    step(nc.vector.tensor_tensor(o1[:, s, :], o1[:, s, :], rowv[:, 3, :], ALU.mult))
                    dve.wait_ge(S("hb_ready"), t + 1)
                    nc.vector.tensor_tensor(o1[:, s, :], o1[:, s, :], hb[:, s, :], ALU.add).then_inc(S("o1_ready"), 1)
                c.leave(TILES // 2)

        @block.tensor
        def _(pe):
            pe.sem_inc(S("tok_ps"), 2)
            pe.wait_ge(S("wtok_ld"), 16)
            with pe.Fori(0, IMAGES // 4) as i:
                for s in range(2):
                    t = 2 * i + s
                    pe.wait_ge(S(f"pt_ld{s}"), 16 * (i + 1))
                    pe.wait_ge(S("tok_ready"), t + 1)
                    for k in range(PK):
                        m = nc.tensor.matmul(psum[:, s, 0:D], pt[:, s, k, :], wtok_sb[:, k, :], start=(k == 0), stop=(k == PK - 1))
                    m.then_inc(S("tok_ps"), 1)
            pe.wait_ge(S("weights_ld"), 16 * 5)
            pe.wait_ge(S("tok_ready"), IMAGES // 2 + 2)
            pe.sem_inc(S("qkT_ps"), 4)

            def qkT_tile(t, s):
                pe.wait_ge(S("qkn_ready"), t + 3)
                for a in range(2):
                    pe.wait_ge(S("qkT_ready"), 2 * t + a + 1)
                    for k in range(4):
                        m = nc.tensor.transpose(psum[:, 6 + a, k * P:(k + 1) * P], qkn[:, s, (4 * a + k) * P:(4 * a + k + 1) * P], ident)
                    m.then_inc(S("qkT_ps"), 1)

            def qkv_tile(t, s, first=False):
                pe.wait_ge(S("xn_ready"), t + 1)
                pe.wait_ge(S("xT_ready"), t + 2)
                for k in range(KC):
                    m = nc.tensor.transpose(psum[:, 5, k * P:(k + 1) * P], xn[:, s, k * P:(k + 1) * P], ident)
                m.then_inc(S("xT_ps"), 1)
                pe.wait_ge(S("xT_ready"), t + 3)
                pe.wait_ge(S("qkn_ready"), t + 1)
                pe.wait_ge(S("v0_ready"), t + 1)
                for a, bank in ((0, 2 * s), (1, 2 * s + 1), (2, 4)):
                    for k in range(KC):
                        m = nc.tensor.matmul(psum[:, bank, :], xT[:, s, k, :], wqkv_sb[:, k, a * 512:(a + 1) * 512], start=(k == 0), stop=(k == KC - 1))
                m.then_inc(S("qkv_ps"), 1)
                if not first:
                    qkT_tile(t - 1, 1 - s)

            qkv_tile(0, 0, True)
            with pe.Fori(0, TILES // 2 - 1) as i:
                qkv_tile(2 * i + 1, 1)
                qkv_tile(2 * i + 2, 0)
            qkv_tile(TILES - 1, 1)
            qkT_tile(TILES - 1, 1)
            pe.sem_inc(S("pv0_ps"), 4)

            def scores0(b, s):
                pe.wait_ge(S("qks_ready"), b + 1)
                for lo, n, base in ((0, P, 0), (P, REST, 3)):
                    for hd in range(H0):
                        m = nc.tensor.matmul(psum[0:n, base + hd // 3, (hd % 3) * SEQ:(hd % 3 + 1) * SEQ],
                                             kz[:, s, hd // 2, lo:lo + n], qz[:, s, hd // 2, hd % 2, :], start=True, stop=True)
                    m.then_inc(S("s0_ps"), 1)

            def values0(s, lo, n):
                for hd in range(H0):
                    o_ = psum[0:n, 6 + hd // 4, (hd % 4) * V0:(hd % 4 + 1) * V0]
                    nc.tensor.matmul(o_, pm[:, s, hd, lo:lo + n], vm[:, s, hd, :], start=(hd % 4 == 0), stop=False, skip_group_check=True)
                    m = nc.tensor.matmul(o_, pr[0:REST, s, hd, lo:lo + n], vr[0:REST, s, hd, :], start=False, stop=(hd % 4 == 3), skip_group_check=True)
                m.then_inc(S("pv0_ps"), 1)

            def attend0_main(b, s, i):
                pe.wait_ge(S("p0_ready"), 4 * b + 4)
                pe.wait_ge(S(f"v0_ld{s}"), 32 * (i + 1))
                pe.wait_ge(S("ao0_ready"), 2 * b + 2)
                values0(s, 0, P)

            def attend0_rest(b, s):
                pe.wait_ge(S("ao0_ready"), 2 * b + 3)
                values0(s, P, REST)

            def image0(b, s, i):
                attend0_main(b, s, i)
                scores0(b + 1, 1 - s)
                attend0_rest(b, s)

            scores0(0, 0)
            with pe.Fori(0, IMAGES // 2 - 1) as i:
                image0(2 * i, 0, i)
                image0(2 * i + 1, 1, i)
            image0(IMAGES - 2, 0, IMAGES // 2 - 1)
            attend0_main(IMAGES - 1, 1, IMAGES // 2 - 1)
            attend0_rest(IMAGES - 1, 1)
            pe.wait_ge(S("weights_ld"), 16 * 5)
            pe.sem_inc(S("aT_ps"), 2)
            pe.sem_inc(S("o0_ps"), 2)

            def aT_tile(t, s, i):
                pe.wait_ge(S(f"aT_ld{s}"), 16 * (i + 1))
                pe.wait_ge(S("aT_ready"), t + 1)
                for k in range(4):
                    m = nc.tensor.transpose(psum[:, s, k * P:(k + 1) * P], aT_in[:, s, k * P:(k + 1) * P], ident)
                m.then_inc(S("aT_ps"), 1)

            def o0_tile(t, s):
                pe.wait_ge(S("aT_ready"), t + 3)
                pe.wait_ge(S("h1_ready"), t + 1)
                for k in range(4):
                    m = nc.tensor.matmul(psum[:, 2 + s, 0:D], aT[:, s, k, :], wo_sb[:, k, :], start=(k == 0), stop=(k == 3))
                m.then_inc(S("o0_ps"), 1)

            aT_tile(0, 0, 0)
            with pe.Fori(0, TILES // 2 - 1) as i:
                aT_tile(2 * i + 1, 1, i)
                o0_tile(2 * i, 0)
                aT_tile(2 * i + 2, 0, i + 1)
                o0_tile(2 * i + 1, 1)
            aT_tile(TILES - 1, 1, TILES // 2 - 1)
            o0_tile(TILES - 2, 0)
            o0_tile(TILES - 1, 1)
            pe.wait_ge(S("weights_ld"), 16 * 5)
            pe.sem_inc(S("xT2_ps"), 2)
            pe.sem_inc(S("gate_ps"), 2)

            def xT2_tile(t, s):
                pe.wait_ge(S("xn2_ready"), t + 1)
                pe.wait_ge(S("xT2_ready"), t + 1)
                for k in range(KC):
                    m = nc.tensor.transpose(psum[:, 4 + s, k * P:(k + 1) * P], xn[:, s, k * P:(k + 1) * P], ident)
                m.then_inc(S("xT2_ps"), 1)

            def gate_tile(t, s):
                pe.wait_ge(S("xT2_ready"), t + 3)
                for k in range(KC):
                    m = nc.tensor.matmul(psum[:, 6, ds(t * EXPERTS, EXPERTS)], xT[:, s, k, :], wgate_sb[:, k, :], start=(k == 0), stop=(k == KC - 1))
                m.then_inc(S("gate_ps"), 1)

            xT2_tile(0, 0)
            with pe.Fori(0, TILES // 2 - 1) as i:
                xT2_tile(2 * i + 1, 1)
                gate_tile(2 * i, 0)
                xT2_tile(2 * i + 2, 0)
                gate_tile(2 * i + 1, 1)
            xT2_tile(TILES - 1, 1)
            gate_tile(TILES - 2, 0)
            gate_tile(TILES - 1, 1)
            pe.wait_ge(S("mask_ready"), 1)
            nc.tensor.matmul(psum[:, 7, 0:E8], tri, mask.rearrange("p t e -> p (t e)"), start=True, stop=True)
            nc.tensor.matmul(psum[:, 5, 0:E8], ones[:, :], mask.rearrange("p t e -> p (t e)"), start=True, stop=True).then_inc(S("rank_ps"), 1)
            pe.sem_inc(S("xsT_ps"), 2)
            pe.sem_inc(S("hidT_ps"), 2)
            pe.sem_inc(S("dn_ps"), 2)

            def xsT_tile(j, s, i):
                pe.wait_ge(S(f"xsl_ld{s}"), 16 * (i + 1))
                pe.wait_ge(S("xsT_ready"), j + 2)
                for k in range(KC):
                    m = nc.tensor.transpose(psum[:, 6, k * P:(k + 1) * P], xsl[:, s, k * P:(k + 1) * P], ident)
                m.then_inc(S("xsT_ps"), 1)

            def gu_half(n, s, half, at):
                pe.wait_ge(S("hid_ready"), n + 1)
                for a in range(2):
                    for k in range(KC):
                        m = nc.tensor.matmul(psum[:, 2 * half + a, :], xT[:, s, k, :], wexp[:, ds(at + k * 2 * F + a * F + half * 512, 512)],
                                             start=(k == 0), stop=(k == KC - 1))
                m.then_inc(S("gu_ps"), 1)

            def hidT_half(n, half):
                pe.wait_ge(S("hid_ready"), n + 3)
                pe.wait_ge(S("hidT_ready"), n + 1)
                for k in range(4):
                    m = nc.tensor.transpose(psum[:, 4 + half, k * P:(k + 1) * P], hid[:, half, k * P:(k + 1) * P], ident)
                m.then_inc(S("hidT_ps"), 1)

            def down_half(n, half, at):
                pe.wait_ge(S("hidT_ready"), n + 3)
                for k in range(4):
                    m = nc.tensor.matmul(psum[:, 7, 0:D], hidT[:, half, k, :], wexp[:, ds(at + KC * 2 * F + (4 * half + k) * D, D)],
                                         start=(half == 0 and k == 0), stop=(half == 1 and k == 3))
                m.then_inc(S("dn_ps"), 1)

            def expert_of(j):
                return (pe.value_load(moe_tab[0:1, 0, ds(j, 1)], min_val=1, max_val=EXPERTS),
                        pe.value_load(moe_tab[0:1, 1, ds(j, 1)], min_val=0, max_val=EXPW))

            def expert_tile(j, s, i, nxt=True):
                _, before = expert_of(j - 1)
                ready, at = expert_of(j)
                pe.wait_ge(S("wexp_ready"), ready)
                pe.sem_inc(S("pe_passed"), 1)
                pe.wait_ge(S("xsT_ready"), j + 3)
                gu_half(2 * j, s, 0, at)
                hidT_half(2 * j - 1, 1)
                pe.wait_ge(S("y_ready"), j + 1)
                down_half(2 * j - 2, 0, before)
                if nxt:
                    xsT_tile(j + 1, 1 - s, i)
                gu_half(2 * j + 1, s, 1, at)
                hidT_half(2 * j, 0)
                down_half(2 * j - 1, 1, before)

            pe.wait_ge(S("tables_ready"), 1)
            xsT_tile(0, 0, 0)
            xsT_tile(1, 1, 0)
            ready, first = expert_of(0)
            pe.wait_ge(S("xsT_ready"), 3)
            pe.wait_ge(S("wexp_ready"), ready)
            gu_half(0, 0, 0, first)
            gu_half(1, 0, 1, first)
            hidT_half(0, 0)
            LASTJ = SLOT_TILES - 1
            with pe.Fori(0, SLOT_TILES // 2 - 1) as i:
                for s, j in ((1, 2 * i + 1), (0, 2 * i + 2)):
                    expert_tile(j, s, i + 1, nxt=True)
            expert_tile(LASTJ, 1, 0, nxt=False)
            _, last_at = expert_of(LASTJ)
            hidT_half(2 * LASTJ + 1, 1)
            pe.wait_ge(S("y_ready"), LASTJ + 2)
            down_half(2 * LASTJ, 0, last_at)
            down_half(2 * LASTJ + 1, 1, last_at)
            pe.wait_ge(S("weights1_ld"), 32)
            pe.sem_inc(S("x1T_ps"), 2)
            pe.sem_inc(S("qkT1_ps"), 2)

            def qkT1_tile(t, s):
                pe.wait_ge(S("qkr_ready"), t + 3)
                pe.wait_ge(S("qkT1_ready"), t + 2)
                for k in range(4):
                    m = nc.tensor.transpose(psum[:, 6, k * P:(k + 1) * P], qkr[:, s, k, :], ident)
                m.then_inc(S("qkT1_ps"), 1)

            def qkv1_tile(t, s, first=False):
                pe.wait_ge(S("xn1_ready"), t + 1)
                pe.wait_ge(S("x1T_ready"), t + 2)
                for k in range(KC):
                    m = nc.tensor.transpose(psum[:, 5, k * P:(k + 1) * P], xn[:, s, k * P:(k + 1) * P], ident)
                m.then_inc(S("x1T_ps"), 1)
                pe.wait_ge(S("x1T_ready"), t + 3)
                pe.wait_ge(S("qkr_ready"), t + 1)
                pe.wait_ge(S("v1_ready"), t + 1)
                for a, n in ((0, 512), (1, D)):
                    for k in range(KC):
                        m = nc.tensor.matmul(psum[:, 2 * s + a, 0:n], xT[:, s, k, :], wqkv1_sb[:, k, a * 512:a * 512 + n], start=(k == 0), stop=(k == KC - 1))
                m.then_inc(S("qkv1_ps"), 1)
                if not first:
                    qkT1_tile(t - 1, 1 - s)

            qkv1_tile(0, 0, True)
            with pe.Fori(0, TILES // 2 - 1) as i:
                qkv1_tile(2 * i + 1, 1)
                qkv1_tile(2 * i + 2, 0)
            qkv1_tile(TILES - 1, 1)
            qkT1_tile(TILES - 1, 1)
            pe.sem_inc(S("pv1_ps"), 4)
            pe.sem_inc(S("wT_ps"), 2)

            def scores1(b, u, s):
                g, lo, n = u % 2, (0 if u < 2 else P), (P if u < 2 else REST)
                if u == 0:
                    pe.wait_ge(S("q1_ready"), b + 1)
                pe.wait_ge(S("s1_read"), 4 * b + u + 1)
                for bank, h_, m_ in ((0, 0, 3), (1, 3, 3), (2, 6, 2)):
                    m = nc.tensor.matmul(psum[0:n, 3 * (u % 2) + bank, 0:m_ * SEQ], q1[:, s, g, lo:lo + n],
                                         kblk[:, s, g, h_:h_ + m_, :].rearrange("p h j -> p (h j)"), start=True, stop=True)
                m.then_inc(S("s1_ps"), 1)

            def transpose1(b, u):
                g = u % 2
                pe.wait_ge(S("p1_ready"), 4 * b + u + 1)
                if u < 2:
                    for n in range(4):
                        rows, lo = (P, 0) if n < 2 else (REST, P)
                        pe.wait_ge(S("wT_ready"), 10 * b + 4 * u + n + 1)
                        for hd in range(4):
                            m = nc.tensor.transpose(psum[0:rows, 6, hd * P:(hd + 1) * P], wts[:, g, 4 * (n % 2) + hd, lo:lo + rows], ident)
                        m.then_inc(S("wT_ps"), 1)
                else:
                    pe.wait_ge(S("wT_ready"), 10 * b + 8 + u - 2 + 1)
                    pe.sem_inc(S("pe_passed"), 1)
                    for n, (rows, lo) in enumerate(((P, 0), (REST, P))):
                        for hd in range(HG):
                            m = nc.tensor.transpose(psum[0:rows, 6, n * P + hd * REST:n * P + (hd + 1) * REST], wts[0:REST, g, hd, lo:lo + rows], ident[0:REST, 0:REST])
                    m.then_inc(S("wT_ps"), 1)

            def values1(b, s, i, part):
                lo, n = ((0, P), (P, REST))[part]
                pe.wait_ge(S("wT_ready"), 10 * b + (8, 10)[part] + 1)
                if part == 0:
                    pe.wait_ge(S(f"v1_ld{s}"), 32 * (i + 1))
                pe.wait_ge(S("a1_ready"), 2 * b + part + 2)
                for hd in range(H1):
                    o_ = psum[0:n, 7, hd * V1:(hd + 1) * V1]
                    nc.tensor.matmul(o_, wT[:, 0, hd, lo:lo + n], v1m[:, s, hd, :], start=(hd == 0), stop=False, skip_group_check=True)
                    m = nc.tensor.matmul(o_, wT[0:REST, 1, hd, lo:lo + n], v1r[0:REST, s, hd, :], start=False, stop=(hd == H1 - 1), skip_group_check=True)
                m.then_inc(S("pv1_ps"), 1)

            def image1(b, s, i, last=False):
                transpose1(b, 0)
                scores1(b, 2, s)
                transpose1(b, 1)
                scores1(b, 3, s)
                values1(b, s, i, 0)
                transpose1(b, 2)
                if not last:
                    scores1(b + 1, 0, 1 - s)
                transpose1(b, 3)
                if not last:
                    scores1(b + 1, 1, 1 - s)
                values1(b, s, i, 1)

            scores1(0, 0, 0)
            scores1(0, 1, 0)
            with pe.Fori(0, IMAGES // 2 - 1) as i:
                image1(2 * i, 0, i)
                image1(2 * i + 1, 1, i)
            image1(IMAGES - 2, 0, IMAGES // 2 - 1)
            image1(IMAGES - 1, 1, IMAGES // 2 - 1, True)
            pe.sem_inc(S("a1T_ps"), 2)
            pe.sem_inc(S("o1_ps"), 2)

            def a1T_tile(t, s, i):
                pe.wait_ge(S(f"a1T_ld{s}"), 16 * (i + 1))
                pe.wait_ge(S("a1T_ready"), t + 1)
                for k in range(KC):
                    m = nc.tensor.transpose(psum[:, s, k * P:(k + 1) * P], a1T_in[:, s, k * P:(k + 1) * P], ident)
                m.then_inc(S("a1T_ps"), 1)

            def o1_tile(t, s):
                pe.wait_ge(S("a1T_ready"), t + 3)
                pe.wait_ge(S("h3_tile"), t + 1)
                for k in range(KC):
                    m = nc.tensor.matmul(psum[:, 2 + s, 0:D], xT[:, s, k, :], wo1_sb[:, k, :], start=(k == 0), stop=(k == KC - 1))
                m.then_inc(S("o1_ps"), 1)

            a1T_tile(0, 0, 0)
            with pe.Fori(0, TILES // 2 - 1) as i:
                a1T_tile(2 * i + 1, 1, i)
                o1_tile(2 * i, 0)
                a1T_tile(2 * i + 2, 0, i + 1)
                o1_tile(2 * i + 1, 1)
            a1T_tile(TILES - 1, 1, TILES // 2 - 1)
            o1_tile(TILES - 2, 0)
            o1_tile(TILES - 1, 1)
            pe.wait_ge(S("weights_ld"), 16 * 5)
            pe.sem_inc(S("x3T_ps"), 2)
            pe.sem_inc(S("rt_ps"), 2)
            with pe.Fori(0, TILES // 2) as i:
                for s in range(2):
                    t = 2 * i + s
                    pe.wait_ge(S(f"xg_ld{s}"), 16 * (i + 1))
                    pe.wait_ge(S("x3T_ready"), t + 1)
                    for k in range(KC):
                        m = nc.tensor.transpose(psum[:, s, k * P:(k + 1) * P], xg[:, s, k * P:(k + 1) * P], ident)
                    m.then_inc(S("x3T_ps"), 1)
                    pe.wait_ge(S("x3T_ready"), t + 3)
                    for k in range(KC):
                        m = nc.tensor.matmul(psum[:, 4, ds(t * HF, HF)], x3T[:, s, k, :], wrout_sb[:, k, :], start=(k == 0), stop=(k == KC - 1))
                    m.then_inc(S("rt_ps"), 1)
            pe.wait_ge(S("pr3_ready"), 1)
            pr3 = lg3.rearrange("p t e -> p (t e)")
            for n, cols in enumerate((P, P, 32)):
                m = nc.tensor.transpose(psum[0:cols, 5, n * P:(n + 1) * P], pr3[:, n * P:n * P + cols], ident)
            m.then_inc(S("pr3T_ps"), 1)
            pe.wait_ge(S("oT_ready"), 1)
            for n, rows in enumerate((P, P, 32)):
                m = nc.tensor.transpose(psum[:, 6, n * P:n * P + rows], oT[0:rows, n * P:(n + 1) * P], ident[0:rows, 0:rows])
            m.then_inc(S("sel_ps"), 1)
            pe.sem_inc(S("hg_ps"), 2)
            with pe.Fori(0, TILES // 2) as i:
                for s in range(2):
                    t = 2 * i + s
                    pe.wait_ge(S(f"xg_ld{s}"), 16 * (i + 1 + TILES // 2))
                    pe.wait_ge(S("selb_ready"), t + 1)
                    pe.wait_ge(S("sel_all_ready"), t + 1)
                    pe.wait_ge(S("hgT_ready"), 2 * t + 2)
                    selm = selb[:, s, :, :].rearrange("p b h -> p (b h)")
                    for k in range(KC):
                        nc.tensor.matmul(psum[:, s, k * P:(k + 1) * P], xg[:, s, k * P:(k + 1) * P], selm, start=True, stop=True)
                    nc.tensor.transpose(psum[:, 2 + s, 0:P], selm, ident).then_inc(S("hg_ps"), 1)
            pe.sem_inc(S("qkvf_ps"), 2)
            pe.sem_inc(S("aof_ps"), 4)

            def qkvf_pair(p_, s, i):
                pe.wait_ge(S(f"wf_ld{s}"), 32 * (i + 1))
                pe.wait_ge(S("hgp_ready"), p_ + 1)
                pe.wait_ge(S("vf_ready"), p_ + 2)
                for x in range(3):
                    for r in range(2):
                        for k in range(KC):
                            m = nc.tensor.matmul(psum[64 * r:64 * r + 64, x, 0:SEQ], wf[:, s, k, x, 64 * r:64 * r + 64], hgp[:, s, k, r, :],
                                                 start=(k == 0), stop=(k == KC - 1))
                m.then_inc(S("qkvf_ps"), 1)

            with pe.Fori(0, PAIRS // 2) as i:
                for s in range(2):
                    p_ = 2 * i + s
                    qkvf_pair(p_, s, i)
                    pe.wait_ge(S("kf_ready"), p_ + 1)
                    pe.wait_ge(S("aof_ready"), 2 * p_ + 2)
                    nc.tensor.matmul(psum[:, 6, 0:SEQ], blockones, kf, start=True, stop=True).then_inc(S("attf_ps"), 1)
                    pe.wait_ge(S(f"wf_ld{s}"), 32 * (i + 1))
                    pe.wait_ge(S("af_ready"), p_ + 2)
                    for lo, n, bank in ((0, P, 4), (P, REST, 6)):
                        for r in range(2):
                            m = nc.tensor.matmul(psum[0:n, bank + r, 0:D], af[64 * r:64 * r + 64, s, lo:lo + n], wof[64 * r:64 * r + 64, s, :], start=True, stop=True)
                        m.then_inc(S("aof_ps"), 1)
            pe.sem_inc(S("yf_ps"), 2)
            with pe.Fori(0, TILES // 2) as i:
                for s in range(2):
                    t = 2 * i + s
                    pe.wait_ge(S(f"aofl_ld{s}"), 16 * (i + 1))
                    pe.wait_ge(S("sel_ready"), t + 1)
                    pe.wait_ge(S("y_sum"), t + 1)
                    nc.tensor.matmul(psum[:, s, 0:D], sel_s[:, s, :], aofl[:, s, :], start=True, stop=True).then_inc(S("yf_ps"), 1)


_OUTS = [((IMAGES, SEQ, D), "float32")]


def shape_constants():
    import numpy as np
    c = np.zeros((P, C_WIDTH), np.float32)
    r = np.arange(P)
    c[:, C_IDENT:C_IDENT + P] = np.eye(P)
    c[:, C_TRI:C_TRI + P] = r[:, None] < r[None, :]
    c[:, C_BLOCK:C_BLOCK + P] = r[:, None] // DHF == r[None, :] // DHF
    c[:, C_HEAD:C_HEAD + 8] = r[:, None] // 16 == np.arange(8)
    c[:, C_IOTA:C_IOTA + 16] = np.arange(16)
    c[:, C_TILE:C_TILE + SLOT_TILES] = np.arange(SLOT_TILES)
    c[:, C_Q128:C_Q128 + TILES] = P * np.arange(TILES)
    grid = np.arange(8)
    hp, wp = (g.reshape(-1).astype(np.float32) for g in np.meshgrid(grid, grid, indexing="ij"))
    quarter = D // 4
    factor = np.float32(10000.0) ** (np.arange(quarter, dtype=np.float32) / quarter)
    a, b = hp[:, None] / factor, wp[:, None] / factor
    pos = np.concatenate([np.sin(a), np.cos(a), np.sin(b), np.cos(b)], -1).astype(np.float32)
    pos = np.concatenate([pos, pos])
    freqs = np.exp(np.arange(0, D, 2, dtype=np.float32) * np.float32(-np.log(10000.0) / D))
    ang = (np.arange(ROWS) % SEQ).astype(np.float32)[:, None] * freqs
    cs = np.stack([np.cos(ang), np.sin(ang), np.cos(ang)], 1).astype(np.float32)
    rope = np.ascontiguousarray(cs.reshape(TILES, P, 3, P).transpose(1, 0, 2, 3))
    return c, pos, rope


def layouts(i):
    import numpy as np

    def chunks(w):
        return np.ascontiguousarray(w.reshape(-1, P, w.shape[-1]).transpose(1, 0, 2))

    i = {k: np.asarray(v) for k, v in i.items()}
    c, pos, rope = shape_constants()
    x = i["x"].reshape(IMAGES, 3, 8, 16, 8, 16).transpose(1, 3, 5, 0, 2, 4).reshape(PK, P, 8, P)
    wp = i["L0_tok_Wp"].reshape(D, 16, 16, 3).transpose(3, 1, 2, 0).reshape(768, D)
    even_odd = np.concatenate([np.arange(0, D, 2), np.arange(1, D, 2)])
    qkv1 = np.concatenate([i["L1_attn_wq"][even_odd].T, i["L1_attn_wk"][even_odd].T, i["L1_attn_wv"].T], 1)
    wq = i["L1_ffn_Wq"]
    wkv = i["L1_ffn_Wkv"]
    qkvf = np.stack([wq, wkv[..., :DHF], wkv[..., DHF:]], 2)
    qkvf = qkvf.reshape(PAIRS, 2, KC, P, 3, DHF).transpose(0, 3, 2, 4, 1, 5).reshape(PAIRS, P, KC * 3 * 2 * DHF)
    bf = np.stack([i["L1_ffn_bq"], i["L1_ffn_bkv"][:, :DHF], i["L1_ffn_bkv"][:, DHF:]], 1)
    bf = bf.reshape(PAIRS, 2, 3, DHF).transpose(1, 3, 0, 2).reshape(P, PAIRS * 3)
    rowv = np.stack([i["L0_tok_b"], i["L1_attn_wo_b"], i["L1_ffn_bo"], i["L1_ffn_ln_g"], i["L1_ffn_ln_b"]])
    gu = i["L0_ffn_w_gate_up"].reshape(EXPERTS, KC, P, 2 * F).transpose(0, 2, 1, 3)
    dn = i["L0_ffn_w_down"].reshape(EXPERTS, FK, P, D).transpose(0, 2, 1, 3)
    a = {
        "patches": x.transpose(2, 1, 0, 3), "txt": i["txt"], "pos_table": pos,
        "row_vectors": np.broadcast_to(rowv, (P, 5, D)), "w_tok": chunks(wp),
        "w_qkv0": chunks(np.concatenate([i["L0_attn_Wq"], i["L0_attn_Wkv"]], 1)), "w_o0": chunks(i["L0_attn_Wo"]),
        "w_gate": chunks(i["L0_ffn_w_gate"]), "w_gu": gu.reshape(EXPERTS, P, KC * 2 * F), "w_down": dn.reshape(EXPERTS, P, FK * D),
        "w_qkv1": chunks(qkv1), "w_o1": chunks(i["L1_attn_wo_w"].T), "rope": rope, "w_router": chunks(i["L1_ffn_Wg"]),
        "w_qkvf": qkvf, "b_qkvf": bf, "w_of": i["L1_ffn_Wo"].reshape(PAIRS, P, D), "constants": c,
    }
    return {k: np.ascontiguousarray(v) for k, v in a.items()}


def kernel(**inputs):
    import numpy as _np
    import concourse.bacc as _bacc
    from concourse import mybir as _mybir
    from concourse.bass_utils import run_bass_kernel_spmd as _run

    nc = _bacc.Bacc("TRN2", target_bir_lowering=False, num_devices=1)
    arrays, args = {}, []
    for name, a in layouts(inputs).items():
        arrays[f"in_{name}"] = a
        args.append(nc.dram_tensor(f"in_{name}", a.shape, _mybir.dt.from_np(a.dtype), kind="ExternalInput").ap())
    shape, dtype = _OUTS[0]
    args.append(nc.dram_tensor("out_0", shape, _mybir.dt.from_np(_np.dtype(dtype)), kind="ExternalOutput").ap())
    fusion_kernel(nc, *args)
    r = _run(nc, [arrays], core_ids=[0])
    return r.results[0]["out_0"]
```

```python
import concourse.bass as bass
from concourse import mybir
from contextlib import ExitStack

IMAGES = 16
PATCHES = 64
TEXT = 77
SEQ = PATCHES + TEXT
D = 256
P = 128
KC = D // P
TILES = -(-IMAGES * SEQ // P)
ROWS = TILES * P
REST = SEQ - P
PK = 768 // P
H0, DH0 = 8, 64
INNER = H0 * DH0
V0 = DH0 + 1
H1, DH1 = 16, 16
V1 = DH1 + 1
HG = P // DH1
RQ = HG * REST
EXPERTS = 8
F = 1024
FK = F // P
SLOT_TILES = 44
SLOTS = SLOT_TILES * P
HF, DHF = 16, 64
POS = ROWS // IMAGES
GB = P // IMAGES
PAIRS = HF // 2
GROUPS = 3
GT = TILES // GROUPS
HT = GT // 2
EXPW = KC * 2 * F + FK * D
assert SLOT_TILES >= (2 * ROWS + EXPERTS * (P - 1)) // P and POS >= SEQ and TILES % (2 * GROUPS) == 0
C_IDENT, C_TRI, C_BLOCK, C_HEAD, C_IOTA, C_TILE, C_Q128 = 0, 128, 256, 384, 392, 408, 452
C_REST = 470
C_CHUNK = 478
C_WIDTH = 510


class Count:

    def __init__(self):
        self.n, self.off = 0, 0

    def next(self, k=1):
        self.n += k
        return self.off + self.n

    def enter(self, i, per):
        self.mark, self.per, self.off = self.n, per, i * per

    def leave(self, turns):
        assert self.n - self.mark == self.per, (self.n - self.mark, self.per)
        self.n, self.off = self.mark + self.per * turns, 0


def ds(start, size):
    return bass.ds(start, size)


def load_expert(nc, S, place, w_gu, w_down, e):
    nc.gpsimd.dma_start(place[:, 0:KC * 2 * F], w_gu[e, :, :]).then_inc(S("wexp_ld"), 16)
    nc.gpsimd.dma_start(place[:, KC * 2 * F:EXPW], w_down[e, :, :]).then_inc(S("wexp_ld"), 16)


def fusion_kernel(nc, patches, txt, pos_table, row_vectors, w_tok, w_qkv0, w_o0, w_gate, w_gu, w_down,
                  w_qkv1, w_o1, rope, w_router, w_qkvf, b_qkvf, w_of, constants, out):
    f32, i32 = mybir.dt.float32, mybir.dt.int32
    ALU, ACT, X = mybir.AluOpType, mybir.ActivationFunctionType, mybir.AxisListType.X
    ctx = ExitStack()
    with ctx:
        starts = {}

        def sb(name, shape, dt=f32):
            base = -(-nc.sbuf_base // 32) * 32
            starts[name] = base
            return ctx.enter_context(nc.sbuf_tensor(name, shape, dt))

        def over(name, buffer, at, width):
            return nc.alloc_sbuf_tensor_at(name, [P, width], f32, offset=starts[buffer] + 4 * at)[:, :]

        def dram(name, shape):
            return nc.dram_tensor(name, shape, f32).ap()

        h0_d = dram("h0_scratch", [ROWS, D])
        v0_d = dram("v0_scratch", [ROWS, H0 * V0])
        ao0_d = dram("attn0_scratch", [ROWS, INNER])
        xs_d = dram("slot_in_scratch", [SLOTS, D])
        ys_d = dram("slot_out_scratch", [SLOTS, D])
        v1_d = dram("v1_scratch", [ROWS, H1 * V1])
        ao1_d = dram("attn1_scratch", [ROWS, D])
        x3_d = dram("x3_scratch", [ROWS, D])
        h3_d = dram("h3_scratch", [ROWS, D])
        aof_d = dram("aof_scratch", [POS * HF, D])

        psum = ctx.enter_context(nc.psum_tensor("psum", [P, 8, 512], f32))

        const = sb("const", [P, C_WIDTH])
        ident = const[:, C_IDENT:C_IDENT + P]
        tri = const[:, C_TRI:C_TRI + P]
        blockones = const[:, C_BLOCK:C_BLOCK + P]
        headmask = const[:, C_HEAD:C_HEAD + 8]
        chunkmask = const[:, C_CHUNK:C_CHUNK + 32]
        restmask = const[:, C_REST:C_REST + 8]
        iota = const[:, C_IOTA:C_IOTA + 16]
        tile_no = const[:, C_TILE:C_TILE + SLOT_TILES]
        q128 = const[:, C_Q128:C_Q128 + TILES]
        rowv = sb("rowv", [P, 5, D])
        ones = sb("ones", [P, P])
        zeros = sb("zeros", [P, D])
        minus16 = sb("minus16", [P, 1])
        h = sb("h", [P, TILES, D])
        wqkv = sb("wqkv", [P, KC * 3 * INNER])
        wo_sb = sb("wo_sb", [P, 4, D])
        wgate_sb = sb("wgate_sb", [P, KC, EXPERTS])
        wrout_sb = sb("wrout_sb", [P, KC, HF])
        big = sb("big", [P, 8 * ROWS])
        wexp = sb("wexp", [P, 2 * EXPW])
        xbuf = sb("xbuf", [P, 2 * D + 2 * D])
        mv = sb("mv", [P, TILES, 2])
        st6 = sb("st6", [P, TILES, 6])
        rstd = sb("rstd", [P, TILES])
        moe_tab = sb("moe_tab", [1, 2, SLOT_TILES], i32)
        end_tab = sb("end_tab", [1, EXPERTS], i32)
        slot = sb("slot", [P, 2, TILES], i32)
        gates = sb("gates", [P, 2, TILES])
        work = sb("work", [P, 10112])

        def f32r(x):
            return x.bitcast(mybir.dt.float32r)

        sems = {}

        def S(name):
            if name not in sems:
                sems[name] = ctx.enter_context(nc.semaphore(name))
            return sems[name]

        def view(base, at, *shape):
            n = 1
            for x in shape:
                n *= x
            v = base[:, at:at + n]
            if len(shape) == 1:
                return v
            names = "abcd"[:len(shape)]
            return v.rearrange(f"p ({' '.join(names)}) -> p {' '.join(names)}", **dict(zip(names, shape)))

        xn = view(xbuf, 0, 2, D)
        xT = view(xbuf, 2 * D, 2, KC, P)
        wqkv_sb = view(wqkv, 0, KC, 3 * INNER)
        wqkv1_sb = view(wqkv, 0, KC, 3 * D)
        wo1_sb = view(wqkv, KC * 3 * D, KC, D)
        wtok_sb = view(big, 0, PK, D)
        pt = view(work, 0, 2, PK, P)
        posb = view(work, 1536, D)
        h0s = view(work, 1792, 2, D)
        qkT = view(big, 0, 8, ROWS)
        vst = view(work, 0, 2, H0, V0)
        sq = view(work, 1040, 1024)
        qkn = view(work, 2064, 2, 1024)
        ssum = view(work, 4112, 2, 16)
        snorm = view(work, 4144, 2, 16)
        qz = view(work, 0, 2, 4, 2, SEQ)
        kz = view(work, 2256, 2, 4, P)
        kblk0 = view(work, 3280, 2, 4, RQ)
        vm = view(work, 4112, 2, H0, V0)
        vraw0 = view(work, 5152, 2, H0, V0)
        vdiag0 = view(work, 6192, 2, H0, V0)
        pm = view(work, 7232, 2, H0, SEQ)
        pr = view(work, 9488, 2, SEQ)
        aom = view(xbuf, 0, 2, H0, DH0)
        aor = view(wqkv, 2048, 2, H0, DH0)
        rsum = view(work, 9770, 2, 2, H0)

        aT_in = view(work, 0, 2, INNER)
        aT = view(work, 1024, 2, 4, P)
        xn2 = view(big, 0, TILES, D)
        E8 = TILES * EXPERTS
        lg = view(work, 2048, TILES, EXPERTS)
        oh = view(work, 2048 + E8, 2, TILES, EXPERTS)
        t8 = view(work, 2048 + 3 * E8, TILES, EXPERTS)
        u8 = view(work, 2048 + 4 * E8, TILES, EXPERTS)
        mask = view(work, 2048 + 5 * E8, TILES, EXPERTS)
        ca = view(work, 2048 + 6 * E8, TILES, EXPERTS)
        cb = view(work, 2048 + 7 * E8, TILES, EXPERTS)
        rank = view(work, 2048 + 8 * E8, TILES, EXPERTS)
        RB = 2048 + 9 * E8
        r18 = view(work, RB, TILES)
        s18 = view(work, RB + 18, TILES)
        val = view(work, RB + 36, 2, TILES)
        cmp = view(work, RB + 72, EXPERTS, TILES)
        nt = view(work, RB + 216, EXPERTS)
        endf = view(work, RB + 224, EXPERTS + 1)
        ej = view(work, RB + 240, SLOT_TILES)
        ej2 = view(work, RB + 284, SLOT_TILES)
        cmpj = view(work, RB + 328, SLOT_TILES, EXPERTS)
        posf = view(work, RB + 680, 2, TILES)

        xsl = view(work, 5120, 2, D)
        xTh = view(over("xT_high", "xbuf", 2 * D, 2 * D), 0, 2, KC, P)
        xTl = view(over("xT_low", "xbuf", 0, 2 * D), 0, 2, KC, P)
        hidTh = view(over("hidT_high", "work", 7680, 1024), 0, 2, 4, P)
        hidTl = view(over("hidT_low", "work", 0, 1024), 0, 2, 4, P)
        wraw = view(big, 0, EXPW)
        wraw01 = view(big, EXPW, 2 * EXPW)
        whigh = over("w_high", "wexp", 0, 2 * EXPW)
        wlow = over("w_low", "big", EXPW, 2 * EXPW)
        sil = view(work, 5632, 2, 512)
        hid = view(work, 6656, 2, 512)
        yst = view(work, 8704, 2, D)
        yg = view(big, 0, 2, TILES, D)
        h0_img = h0_d[0:IMAGES * SEQ, :].rearrange("(b n) d -> b n d", n=SEQ)
        qkT1 = view(big, 2 * TILES * D, 4, ROWS)
        vst1 = view(work, 0, 2, H1, V1)
        rp = view(work, 544, 2, 3, P)
        ra = view(work, 1312, 2, 2, P)
        rb = view(work, 1824, 2, 2, P)
        qkr = view(work, 2336, 2, 4, P)
        kblk = view(wexp, 0, 2, 2, HG, SEQ)
        vraw = view(wexp, 4512, 2, 2 * HG * V1)
        vdiag = view(wexp, 5056, 2, 2, HG, V1)
        qblk = view(wexp, 5600, 2, 2, RQ)
        wr = view(wexp, 6016, 2, SEQ)
        wrT = view(wexp, 6298, 2, 2, RQ)
        avr = view(wexp, 6714, 2, HG, DH1)
        mr = view(wexp, 6970, 2)
        rr = view(wexp, 6972, 2)
        a1r = view(wexp, 6974, 2, 2, DH1)
        wts = view(big, 0, 2, 2, HG * SEQ)
        UNIT = 4 * SEQ
        FIRST_AT, LAST_AT = (0, UNIT + 4 * REST), (4 * P, UNIT)
        wT = view(big, 4512, 2, H1, P)
        wTr = view(big, 8608, 2, 2, P)
        q1 = view(work, 3360, 2, 2, P)
        v1m = view(work, 3924, 2, H1, V1)
        a1m = view(work, 5012, 2, H1, DH1)
        max1 = view(work, 6036, 2, 4)
        rs1 = view(work, 6052, H1)
        a1T_in = view(work, 6100, 2, D)
        x3 = view(big, 0, TILES, D)
        xg = view(wexp, 8960, 2, HT, D)
        stg = view(work, 0, GT, 6)
        mvg = view(work, 40, GT, 2)
        rg = view(work, 56, GT)
        lg3 = view(work, 512, TILES, HF)
        pT = view(work, 800, 3 * P)
        uT = view(work, 1184, 3 * P)
        oT = view(work, 1568, 3 * P)
        m3 = view(work, 1952, 3 * GB)
        sel = view(work, 1980, TILES, HF)
        selb = view(work, 2268, 2, GB, HF)
        sel_all = view(work, 2524, TILES, P)
        hgT = view(big, 2 * TILES * D, KC, HF, POS)
        x3T = view(work, 4828, 2, KC, P)
        wf = view(wexp, 0, 2, KC, 3, 2 * DHF)
        wof = view(wexp, 1536, 2, D)
        bf = view(wexp, 2048, PAIRS, 3)
        hgp = view(wexp, 2072, 2, KC, 2, SEQ)
        qf = view(wexp, 3200, SEQ)
        kf = view(wexp, 3341, SEQ)
        vf = view(wexp, 3482, SEQ)
        ef = view(wexp, 3623, SEQ)
        af = view(wexp, 3764, 2, SEQ)
        mf = view(wexp, 4046, 2)
        rf = view(wexp, 4048, 2)
        aofm = view(wexp, 4052, 2, 2, D)
        aofr = view(wexp, 5076, 2, 2, D)
        ysum = view(big, 0, GT, D)
        aofl = view(big, 9216, 2, HT, D)
        x3b = view(big, 13824, 2, HT, D)
        h3b = view(big, 15360, 2, HT, D)
        o1 = view(big, 4608, GT, D)
        sel_s = view(wexp, 7636, 2, P)

        LASTB = SEQ - (TILES - 1) * GB

        def by_position(rows_d):
            return bass.AP(rows_d.tensor, 0, [[D, POS], [SEQ * D, IMAGES], [1, D]])

        ROWS_X2, ROWS_X1, ROWS_A1, ROWS_X3 = (TILES * n for n in range(1, 5))
        PRODUCT_GATE, PRODUCT_O1, PRODUCT_ROUTER = (TILES * n for n in range(1, 4))
        RESIDUAL_3 = TILES
        RANKS, PROBS_T, CHOICES = 1, 2, 3
        EXP_EXPERTS, EXP_HEADS = 1, 2
        DID = {name: n + 1 for n, name in enumerate((
            "v0_ones",
            "lg_ready",
            "mask_ready",
            "slots_ready",
            "tables_ready",
            "v1_ones",
            "lg3_ready",
            "pr3_ready",
            "oT_ready"))}

        block = ctx.enter_context(nc.Block())

        @block.sync
        def _(sp):
            sp.dma_start(wtok_sb, w_tok).then_inc(S("wtok_ld"), 16)
            sp.dma_start(posb, pos_table).then_inc(S("tables_ld"), 16)
            sp.dma_start(rowv[:, :, :], row_vectors).then_inc(S("tables_ld"), 16)
            with sp.Fori(0, IMAGES // 4) as i:
                for s in range(2):
                    t = 2 * i + s
                    sp.wait_ge(S("tok_ps"), t + 1)
                    sp.dma_start(pt[:, s, :, :], patches[ds(t, 1), :, :, :].rearrange("o p k n -> p (o k) n")).then_inc(S(f"pt_ld{s}"), 16)
            sp.dma_start(h0_img[:, PATCHES:SEQ, :], txt).then_inc(S("h0_st"), 16)
            sp.wait_ge(S("fills"), 3)
            sp.dma_start(h0_d[IMAGES * SEQ:ROWS, :], zeros[0:ROWS - IMAGES * SEQ, :]).then_inc(S("h0_st"), 16)
            sp.dma_start(const[:, :], constants).then_inc(S("weights_ld"), 16)
            sp.dma_start(wqkv_sb, w_qkv0).then_inc(S("weights_ld"), 16)
            sp.dma_start(wo_sb[:, :, :], w_o0).then_inc(S("weights_ld"), 16)
            sp.dma_start(wgate_sb[:, :, :], w_gate).then_inc(S("weights_ld"), 16)
            sp.dma_start(wrout_sb[:, :, :], w_router).then_inc(S("weights_ld"), 16)
            sp.wait_ge(S("h0_st"), 32)
            for s in range(2):
                sp.wait_ge(S(f"tok_st{s}"), 32 * (IMAGES // 4 + 1))
            sp.dma_start(h[:, :, :], h0_d.rearrange("(t p) d -> p t d", p=P)).then_inc(S("h_ld"), 16)
            sp.dma_start(xs_d.rearrange("(t p) d -> p t d", p=P), zeros[:, :].unsqueeze(1).to_broadcast([P, SLOT_TILES, D])).then_inc(S("zero_st"), 16)
            sp.dma_start(aof_d[SEQ * HF:POS * HF, :], zeros[0:(POS - SEQ) * HF, :]).then_inc(S("zero_st"), 16)
            with sp.Fori(0, TILES // 2) as i:
                for s in range(2):
                    t = 2 * i + s
                    sp.wait_ge(S("v0_ready"), t + 2)
                    sp.dma_start(v0_d[ds(t * P, P), :], vst[:, s, :, :].rearrange("p h v -> p (h v)")).then_inc(S(f"v0_st{s}"), 16)
            for s in range(2):
                sp.wait_ge(S(f"v0_st{s}"), 16 * (TILES // 2 + 1))
            sp.wait_ge(S("qkv_ps"), TILES)
            sp.dma_start(wqkv1_sb, w_qkv1).then_inc(S("weights1_ld"), 16)
            sp.dma_start(wo1_sb, w_o1).then_inc(S("weights1_ld"), 16)
            sp.wait_ge(S("qkT_ready"), 2 * TILES + 2)
            sp.wait_ge(S("vraw0_zero"), 1)
            with sp.Fori(0, IMAGES // 2) as i:
                for s in range(2):
                    b = 2 * i + s
                    sp.wait_ge(S("pv0_ps"), 2 * b + 2)
                    sp.dma_start(vm[:, s, :, :], v0_d[ds(b * SEQ, P), :].rearrange("p (h v) -> p h v", h=H0)).then_inc(S(f"v0_ld{s}"), 16)
                    sp.dma_start(vraw0[0:RQ, s, :, :].rearrange("p h v -> p (h v)"), v0_d[ds(b * SEQ + P, REST), :].unsqueeze(0).to_broadcast([H0, REST, H0 * V0])).then_inc(S(f"v0_ld{s}"), 16)
            for s in range(2):
                sp.wait_ge(S(f"ao0_st{s}"), 32 * (IMAGES // 2 + 1))
            sp.wait_ge(S("ao0_pad"), 32)
            with sp.Fori(0, TILES // 2) as i:
                for s in range(2):
                    t = 2 * i + s
                    sp.wait_ge(S("rowsT_ps"), t + 1)
                    sp.dma_start(aT_in[:, s, :], ao0_d[ds(t * P, P), :]).then_inc(S(f"aT_ld{s}"), 16)
            sp.wait_ge(S("xs_st"), 16 * 2 * TILES)
            with sp.Fori(0, SLOT_TILES // 2) as i:
                for s in range(2):
                    j = 2 * i + s
                    sp.wait_ge(S("xsT_ps"), j + 1)
                    sp.dma_start(xsl[:, s, :], xs_d[ds(j * P, P), :]).then_inc(S(f"xsl_ld{s}"), 16)
            with sp.Fori(0, TILES // 2) as i:
                for s in range(2):
                    t = 2 * i + s
                    sp.wait_ge(S("qkr_ready"), t + 1)
                    sp.dma_start(rp[:, s, :, :], rope[:, ds(t, 1), :, :].rearrange("p o k n -> p (o k) n")).then_inc(S(f"rp_ld{s}"), 16)
            for s in range(2):
                sp.wait_ge(S(f"v1_st{s}"), 16 * (TILES // 2 + 1))
            sp.wait_ge(S("vraw_zero"), 1)
            with sp.Fori(0, IMAGES // 2) as i:
                for s in range(2):
                    b = 2 * i + s
                    sp.wait_ge(S("pv1_ps"), b + 1)
                    sp.dma_start(v1m[:, s, :, :], v1_d[ds(b * SEQ, P), :].rearrange("p (h v) -> p h v", h=H1)).then_inc(S(f"v1_ld{s}"), 16)
                    sp.dma_start(vraw[0:RQ, s, :], v1_d[ds(b * SEQ + P, REST), :].unsqueeze(0).to_broadcast([HG, REST, H1 * V1])).then_inc(S(f"v1_ld{s}"), 16)
            for s in range(2):
                sp.wait_ge(S(f"a1_st{s}"), 16 * (IMAGES // 2 + 1))
                sp.wait_ge(S(f"a1r_st{s}"), 32 * (IMAGES // 2 + 1))
            sp.wait_ge(S("a1_pad"), 16)
            with sp.Fori(0, TILES // 2) as i:
                for s in range(2):
                    t = 2 * i + s
                    sp.wait_ge(S("rowsT_ps"), ROWS_A1 + t + 1)
                    sp.dma_start(a1T_in[:, s, :], ao1_d[ds(t * P, P), :]).then_inc(S(f"a1T_ld{s}"), 16)
            with sp.Fori(0, GROUPS) as g:
                for n, (ready, rows_d, rows) in enumerate((("x3_ready", x3_d, x3), ("h3_ready", h3_d, h))):
                    sp.wait_ge(S(ready), g + 1)
                    sp.sem_inc(S("sp_passed"), 1)
                    sp.dma_start(rows_d[ds(g * GT * P, GT * P), :].rearrange("(t p) d -> p t d", p=P), rows[:, ds(g * GT, GT), :]).then_inc(S("rows3_st"), 16)
            sp.wait_ge(S("rows3_st"), 32 * GROUPS)
            x3_bs = by_position(x3_d)
            h3_bs = by_position(h3_d)
            for free, before in (("rowsT_ps", ROWS_X3 - 2), ("hg_ps", 0)):
                if free == "hg_ps":
                    sp.wait_ge(S("rowsT_ps"), ROWS_X3 + TILES + 2)
                with sp.Fori(0, GROUPS) as g:
                    for r in range(2):
                        sp.wait_ge(S(free), before + g * GT + r * HT + 1)
                        sp.sem_inc(S("sp_passed"), 1)
                        for n in range(HT):
                            sp.dma_start(xg[:, r, n, :], x3_bs[ds((g * GT + r * HT + n) * GB, GB), :, :]).then_inc(S(f"xg_ld{r}"), 16)
            sp.dma_start(bf, b_qkvf.rearrange("p (a b) -> p a b", a=PAIRS)).then_inc(S("bf_ld"), 16)
            with sp.Fori(0, PAIRS // 2) as i:
                for s in range(2):
                    p_ = 2 * i + s
                    sp.wait_ge(S("qkvf_ps"), p_ + 1)
                    sp.dma_start(wf[:, s, :, :, :].rearrange("p k x n -> p (k x n)"), w_qkvf[ds(p_, 1), :, :].rearrange("o p n -> p (o n)")).then_inc(S(f"wf_ld{s}"), 16)
                    sp.wait_ge(S("aof_ps"), 2 * p_ + 2)
                    sp.dma_start(wof[:, s, :], w_of[ds(p_, 1), :, :].rearrange("o p n -> p (o n)")).then_inc(S(f"wof_ld{s}"), 16)
            for s in range(2):
                sp.wait_ge(S(f"aof_st{s}"), 32 * (PAIRS // 2 + 1))
            sp.wait_ge(S("zero_st"), 32)
            with sp.Fori(0, GROUPS) as g:
                for r in range(2):
                    at = (g * GT + r * HT) * GB
                    sp.wait_ge(S("y_sum"), g * GT + r * HT + 1)
                    sp.sem_inc(S("sp_passed"), 1)
                    for n in range(HT):
                        sp.dma_start(aofl[:, r, n, :], aof_d[ds((g * GT + r * HT + n) * P, P), :]).then_inc(S(f"aofl_ld{r}"), 16)
                        sp.dma_start(x3b[:, r, n, :], x3_bs[ds(at + n * GB, GB), :, :]).then_inc(S(f"x3b_ld{r}"), 16)
                    sp.wait_ge(S("o1_ready"), g * GT + r * HT + 1)
                    sp.sem_inc(S("sp_passed"), 1)
                    for n in range(HT):
                        sp.dma_start(h3b[:, r, n, :], h3_bs[ds(at + n * GB, GB), :, :]).then_inc(S(f"h3b_ld{r}"), 16)

        @block.gpsimd
        def _(pool):
            nc.gpsimd.memset(zeros[:, :], 0.0).then_inc(S("fills"), 1)
            nc.gpsimd.memset(ones[:, :], 1.0).then_inc(S("fills"), 1)
            nc.gpsimd.memset(minus16[:, :], -16.0).then_inc(S("fills"), 1)
            for s in range(2):
                pool.wait_ge(S(f"v0_st{s}"), 16 * (TILES // 2 + 1))
            pool.wait_ge(S("qkT_ready"), 2 * TILES + 2)
            nc.gpsimd.memset(vraw0.rearrange("p s h v -> p (s h v)"), 0.0).then_inc(S("vraw0_zero"), 1)
            with pool.Fori(0, IMAGES // 2) as i:
                for s in range(2):
                    b = 2 * i + s
                    pool.wait_ge(S("s0_ps"), 2 * b + 2)
                    nc.gpsimd.tensor_copy(kz[:, s, :, :], qkT[:, 4:8, ds(b * SEQ, P)])
                    for r in range(2):
                        m = nc.gpsimd.tensor_tensor(qz[:, s, :, r, :], qkT[:, 0:4, ds(b * SEQ, SEQ)],
                                                    blockones[:, 64 * r:64 * r + 1].unsqueeze(2).to_broadcast([P, 4, SEQ]), ALU.mult)
                    m.then_inc(S("qks_ready"), 1)
                    nc.gpsimd.tensor_tensor(kblk0[:, s, :, :].rearrange("p c (h k) -> p c h k", h=H0),
                                            qkT[:, 4:8, ds(b * SEQ + P, REST)].unsqueeze(2).to_broadcast([P, 4, H0, REST]),
                                            chunkmask.rearrange("p (c h) -> p c h", c=4).unsqueeze(3).to_broadcast([P, 4, H0, REST]), ALU.mult).then_inc(S("qks_ready"), 1)
                    pool.wait_ge(S(f"v0_ld{s}"), 32 * (i + 1))
                    pool.wait_ge(S("pv0_ps"), 2 * b + 2)
                    nc.gpsimd.tensor_tensor(vdiag0[:, s, :, :], vraw0[:, s, :, :], restmask.unsqueeze(2).to_broadcast([P, H0, V0]), ALU.mult).then_inc(S("vdiag0_ready"), 1)
            pool.wait_ge(S("rowsT_ps"), TILES // 2 + 2)
            for e in range(2):
                load_expert(nc, S, wraw01[:, e * EXPW:(e + 1) * EXPW], w_gu, w_down, e)
            pool.sem_inc(S("xn2_kept"), 2)
            pool.wait_ge(S("vdiag0_ready"), IMAGES)
            with pool.Fori(0, TILES // 2) as i:
                for s in range(2):
                    t = 2 * i + s
                    pool.wait_ge(S("xn2_ready"), t + 1)
                    nc.gpsimd.tensor_copy(xn2[:, t, :], xn[:, s, :]).then_inc(S("xn2_kept"), 1)
            pool.wait_ge(S("dve_did"), DID["slots_ready"])
            pool.wait_ge(S("xn2_kept"), TILES + 2)
            pool.wait_ge(S("zero_st"), 32)
            for k in range(2):
                for t in range(TILES):
                    nc.gpsimd.indirect_dma_start(xs_d, bass.IndirectOffsetOnAxis(slot[:, k, t:t + 1], 0), xn2[:, t, :], None).then_inc(S("xs_st"), 16)
            pool.wait_ge(S("split_ready"), 2)
            pool.sem_inc(S("wexp_ready"), 2)
            pool.wait_ge(S("xs_st"), 16 * 2 * TILES)
            load_expert(nc, S, wraw, w_gu, w_down, 2)
            for e in range(2, EXPERTS):
                at = (e % 2) * EXPW
                pool.wait_ge(S("wexp_ld"), 32 * (e + 1))
                done = pool.value_load(end_tab[0:1, e - 2:e - 1], min_val=2, max_val=2 * SLOT_TILES + 2)
                pool.wait_ge(S("dn_ps"), done)
                pool.sem_inc(S("wexp_free"), 1)
                nc.gpsimd.tensor_tensor(f32r(whigh[:, at:at + EXPW]), wraw, ones[:, 0:1].to_broadcast([P, EXPW]), ALU.mult).then_inc(S("split_hi"), 1)
                pool.wait_ge(S("split_hi"), e - 1)
                nc.gpsimd.tensor_tensor(f32r(wlow[:, at:at + EXPW]), wraw, whigh[:, at:at + EXPW], ALU.subtract).then_inc(S("wexp_ready"), 1)
                if e + 1 < EXPERTS:
                    pool.wait_ge(S("wexp_ready"), e + 1)
                    load_expert(nc, S, wraw, w_gu, w_down, e + 1)
            pool.wait_ge(S("xs_st"), 16 * 2 * TILES)
            for s in range(2):
                pool.wait_ge(S(f"ys_st{s}"), 16 * (SLOT_TILES // 2 + 1))
            for t in range(TILES):
                for k in range(2):
                    nc.gpsimd.indirect_dma_start(yg[:, k, t, :], None, ys_d, bass.IndirectOffsetOnAxis(slot[:, k, t:t + 1], 0)).then_inc(S(f"yg_ld{t // GT}"), 16)
            pool.wait_ge(S("qkT1_ready"), TILES + 2)
            pool.wait_ge(S("xn1_ready"), TILES)
            nc.gpsimd.memset(vraw, 0.0).then_inc(S("vraw_zero"), 1)
            with pool.Fori(0, IMAGES // 2) as i:
                for s in range(2):
                    b = 2 * i + s
                    pool.wait_ge(S("sr_ps"), b + 1)
                    nc.gpsimd.tensor_copy(q1[:, s, :, :], qkT1[:, 0:2, ds(b * SEQ, P)])
                    for g in range(2):
                        nc.gpsimd.tensor_tensor(kblk[:, s, g, :, :], qkT1[:, 2 + g, ds(b * SEQ, SEQ)].unsqueeze(1).to_broadcast([P, HG, SEQ]),
                                                headmask.unsqueeze(2).to_broadcast([P, HG, SEQ]), ALU.mult)
                    for g in range(2):
                        m = nc.gpsimd.tensor_tensor(qblk[:, s, g, :].rearrange("p (h i) -> p h i", h=HG),
                                                    qkT1[:, g, ds(b * SEQ + P, REST)].unsqueeze(1).to_broadcast([P, HG, REST]),
                                                    headmask.unsqueeze(2).to_broadcast([P, HG, REST]), ALU.mult)
                    m.then_inc(S("q1_ready"), 1)
                    pool.wait_ge(S(f"v1_ld{s}"), 32 * (i + 1))
                    pool.wait_ge(S("pv1_ps"), b + 1)
                    nc.gpsimd.tensor_tensor(vdiag[:, s, :, :, :], vraw[:, s, :].rearrange("p (g h v) -> p g h v", g=2, h=HG),
                                            restmask.unsqueeze(1).unsqueeze(3).to_broadcast([P, 2, HG, V1]), ALU.mult).then_inc(S("vdiag_ready"), 1)
            nc.gpsimd.tensor_tensor(h[:, :, :], h[:, :, :], rowv[:, 1, :].unsqueeze(1).to_broadcast([P, TILES, D]), ALU.add).then_inc(S("h_bias"), 1)
            with pool.Fori(0, GROUPS) as g:
                pool.wait_ge(S("x3_ready"), g + 1)
                nc.gpsimd.tensor_tensor(h[:, ds(g * GT, GT), :], h[:, ds(g * GT, GT), :], rowv[:, 4, :].unsqueeze(1).to_broadcast([P, GT, D]), ALU.add).then_inc(S("h3_ready"), 1)
            pool.wait_ge(S("hgT_ready"), 2 * TILES + 4)
            with pool.Fori(0, PAIRS // 2) as i:
                for s in range(2):
                    p_ = 2 * i + s
                    pool.wait_ge(S("qkvf_ps"), p_ + 1)
                    nc.gpsimd.tensor_copy(hgp[:, s, :, :, :], hgT[:, :, ds(2 * p_, 2), 0:SEQ]).then_inc(S("hgp_ready"), 1)
            with pool.Fori(0, TILES // 2) as i:
                for s in range(2):
                    t = 2 * i + s
                    pool.wait_ge(S("yf_ps"), t + 1)
                    nc.gpsimd.tensor_copy(sel_s[:, s, :], sel_all[:, t, :]).then_inc(S("sel_ready"), 1)
        @block.scalar
        def _(act):
            for s in range(2):
                act.sem_inc(S(f"tok_st{s}"), 32)
            with act.Fori(0, IMAGES // 4) as i:
                for s in range(2):
                    t = 2 * i + s
                    act.wait_ge(S("tok_ready"), t + 3)
                    for r in range(2):
                        act.dma_start(h0_img[ds(2 * t + r, 1), 0:PATCHES, :].rearrange("o n d -> (o n) d"),
                                      h0s[64 * r:64 * r + 64, s, :]).then_inc(S(f"tok_st{s}"), 16)
            act.sem_inc(S("xT_ready"), 2)
            act.sem_inc(S("qkT_ready"), 2)
            act.sem_inc(S("v0_ready"), 1)
            for s in range(2):
                act.sem_inc(S(f"v0_st{s}"), 16)
            act.wait_ge(S("ln_stats"), 1)
            nc.scalar.activation(rstd[:, :], mv[:, :, 1], ACT.Sqrt).then_inc(S("ln_root"), 1)

            def keep_qkT(t):
                for a in range(2):
                    act.wait_ge(S("qkT_ps"), 2 * t + a + 5)
                    nc.scalar.activation(qkT[:, 4 * a:4 * a + 4, ds(t * P, P)],
                                         psum[:, 6 + a, :].rearrange("p (k n) -> p k n", k=4), ACT.Copy).then_inc(S("qkT_ready"), 1)

            def keep_xT(t, s):
                act.wait_ge(S("xT_ps"), t + 1)
                nc.scalar.activation(xT[:, s, :, :], psum[:, 5, 0:D].rearrange("p (k n) -> p k n", k=KC), ACT.Copy).then_inc(S("xT_ready"), 1)

            def qkv_step(t, s, i, first=False, last=False):
                act.wait_ge(S("qkv_ps"), t + 1)
                if not last:
                    keep_xT(t + 1, 1 - s)
                act.wait_ge(S(f"v0_st{s}"), 16 * (i + 1))
                act.wait_ge(S("dve_did"), DID["v0_ones"])
                nc.scalar.activation(vst[:, s, :, 0:DH0], psum[:, 4, :].rearrange("p (h v) -> p h v", h=H0), ACT.Copy).then_inc(S("v0_ready"), 1)
                if not first:
                    act.wait_ge(S("ssum_ready"), t)
                nc.scalar.activation(sq.rearrange("p (a n) -> p a n", a=2), psum[:, 2 * s:2 * s + 2, :], ACT.Square).then_inc(S("sq_ready"), 1)
                if not first:
                    keep_qkT(t - 1)
                act.wait_ge(S("ssum_ready"), t + 1)
                nc.scalar.activation(snorm[:, s, :], ssum[:, s, :], ACT.Sqrt).then_inc(S("snorm_ready"), 1)

            keep_xT(0, 0)
            qkv_step(0, 0, 0, first=True)
            with act.Fori(0, TILES // 2 - 1) as i:
                qkv_step(2 * i + 1, 1, i)
                qkv_step(2 * i + 2, 0, i + 1)
            qkv_step(TILES - 1, 1, TILES // 2 - 1, last=True)
            keep_qkT(TILES - 1)
            for s in range(2):
                act.sem_inc(S(f"ao0_st{s}"), 32)

            act.sem_inc(S("p0_ready"), 2)

            def exp0(b, s):
                act.wait_ge(S("pv0_ps"), 2 * b + 2)
                for u in range(2):
                    act.wait_ge(S("s0_ps"), 2 * b + u + 5)
                    m = nc.scalar.activation(pm[:, s, 4 * u:4 * u + 4, :].rearrange("p (a c) i -> p a (c i)", c=2),
                                             psum[:, 2 * u:2 * u + 2, 0:2 * SEQ], ACT.Exp, bias=minus16[:, :], scale=16.0)
                    if u:
                        m = nc.scalar.activation(pr[0:RQ, s, :], psum[0:RQ, 3, 2 * SEQ:3 * SEQ], ACT.Exp, bias=minus16[0:RQ, :], scale=16.0)
                    m.then_inc(S("p0_ready"), 1)

            def store_ao0(b, s):
                act.wait_ge(S("ao0_ready"), 2 * b + 4)
                act.dma_start(ao0_d[ds(b * SEQ, P), :], aom[:, s, :, :].rearrange("p h v -> p (h v)")).then_inc(S(f"ao0_st{s}"), 16)
                act.dma_start(ao0_d[ds(b * SEQ + P, REST), :], aor[0:REST, s, :, :].rearrange("p h v -> p (h v)")).then_inc(S(f"ao0_st{s}"), 16)

            act.dma_start(ao0_d[IMAGES * SEQ:ROWS, 0:D], zeros[0:ROWS - IMAGES * SEQ, :]).then_inc(S("ao0_pad"), 16)
            act.dma_start(ao0_d[IMAGES * SEQ:ROWS, D:INNER], zeros[0:ROWS - IMAGES * SEQ, :]).then_inc(S("ao0_pad"), 16)
            act.wait_ge(S("fills"), 3)
            exp0(0, 0)
            with act.Fori(0, IMAGES // 2 - 1) as i:
                for s in range(2):
                    exp0(2 * i + s + 1, 1 - s)
                    store_ao0(2 * i + s, s)
            exp0(IMAGES - 1, 1)
            store_ao0(IMAGES - 2, 0)
            store_ao0(IMAGES - 1, 1)
            act.sem_inc(S("rowsT_ready"), 2)

            def keep_aT(t, s):
                act.wait_ge(S("rowsT_ps"), t + 3)
                act.wait_ge(S("product_ps"), t + 1)
                nc.scalar.activation(aT[:, s, :, :], psum[:, s, :].rearrange("p (k n) -> p k n", k=4), ACT.Copy).then_inc(S("rowsT_ready"), 1)

            with act.Fori(0, TILES // 2) as i:
                for s in range(2):
                    keep_aT(2 * i + s, s)
            act.wait_ge(S("ln_stats"), 2)
            nc.scalar.activation(rstd[:, :], mv[:, :, 1], ACT.Sqrt).then_inc(S("ln_root"), 1)
            with act.Fori(0, TILES // 2) as i:
                for s in range(2):
                    t = 2 * i + s
                    act.wait_ge(S("rowsT_ps"), ROWS_X2 + t + 3)
                    act.wait_ge(S("product_ps"), PRODUCT_GATE + t + 1)
                    nc.scalar.activation(xT[:, s, :, :], psum[:, 4 + s, 0:D].rearrange("p (k n) -> p k n", k=KC), ACT.Copy).then_inc(S("rowsT_ready"), 1)
            act.wait_ge(S("dve_did"), DID["lg_ready"])
            nc.scalar.activation(lg, lg, ACT.Exp).then_inc(S("act_did"), 1)
            act.wait_ge(S("wexp_ld"), 64)
            for e in range(2):
                nc.scalar.activation(f32r(whigh[:, e * EXPW:(e + 1) * EXPW]), wraw01[:, e * EXPW:(e + 1) * EXPW], ACT.Copy).then_inc(S("split01_hi"), 1)
            act.sem_inc(S("xsT_ready"), 2)
            act.sem_inc(S("sil_ready"), 2)
            act.sem_inc(S("y_ready"), 2)
            for s in range(2):
                act.sem_inc(S(f"ys_st{s}"), 16)

            def keep_xsT(j, s):
                act.wait_ge(S("xsT_ps"), j + 3)
                nc.scalar.activation(f32r(xTh[:, s, :, :]), psum[:, 6, 0:D].rearrange("p (k n) -> p k n", k=KC), ACT.Copy).then_inc(S("xsT_ready"), 1)

            def silu(n, s):
                act.wait_ge(S("gu_ps"), n + 1)
                act.wait_ge(S("hid_ready"), n + 1)
                nc.scalar.activation(sil[:, s, :], psum[:, 2 * s, :], ACT.Silu).then_inc(S("sil_ready"), 1)

            def keep_y(j, s, i):
                act.wait_ge(S("dn_ps"), 2 * j + 4)
                act.wait_ge(S(f"ys_st{s}"), 16 * (i + 1))
                nc.scalar.activation(yst[:, s, :], psum[:, 7, 0:D], ACT.Copy).then_inc(S("y_ready"), 1)
                act.wait_ge(S("y_ready"), j + 3)
                act.dma_start(ys_d[ds(j * P, P), :], yst[:, s, :]).then_inc(S(f"ys_st{s}"), 16)

            keep_xsT(0, 0)
            keep_xsT(1, 1)
            silu(0, 0)
            silu(1, 1)
            with act.Fori(0, SLOT_TILES // 2 - 1) as i:
                silu(4 * i + 2, 0)
                keep_xsT(2 * i + 2, 0)
                silu(4 * i + 3, 1)
                keep_y(2 * i, 0, i)
                silu(4 * i + 4, 0)
                keep_xsT(2 * i + 3, 1)
                silu(4 * i + 5, 1)
                keep_y(2 * i + 1, 1, i)
            silu(2 * SLOT_TILES - 2, 0)
            silu(2 * SLOT_TILES - 1, 1)
            keep_y(SLOT_TILES - 2, 0, SLOT_TILES // 2 - 1)
            keep_y(SLOT_TILES - 1, 1, SLOT_TILES // 2 - 1)
            for s in range(2):
                act.sem_inc(S(f"v1_st{s}"), 16)
            act.sem_inc(S("qkT1_ready"), 2)
            act.sem_inc(S("v1_ready"), 2)

            def root1(g):
                act.wait_ge(S("ln_stats"), g + 3)
                nc.scalar.activation(rstd[:, ds(g * GT, GT)], mv[:, ds(g * GT, GT), 1], ACT.Sqrt).then_inc(S("ln_root"), 1)

            def keep_qkT1(t):
                act.wait_ge(S("qkT1_ps"), t + 3)
                nc.scalar.activation(qkT1[:, :, ds(t * P, P)], psum[:, 6, :].rearrange("p (k n) -> p k n", k=4), ACT.Copy).then_inc(S("qkT1_ready"), 1)

            def keep_x1T(t, s):
                act.wait_ge(S("rowsT_ps"), ROWS_X1 + t + 3)
                nc.scalar.activation(xT[:, s, :, :], psum[:, 5, 0:D].rearrange("p (k n) -> p k n", k=KC), ACT.Copy).then_inc(S("rowsT_ready"), 1)

            def qkv1_group_act(g, first=False):
                root1(g)
                for n in range(GT):
                    t, s = g * GT + n, n % 2
                    if n == 0:
                        keep_x1T(t, s)
                    act.wait_ge(S("qkv1_ps"), t + 1)
                    if n < GT - 1:
                        keep_x1T(t + 1, 1 - s)
                    act.wait_ge(S(f"v1_st{s}"), 16 * (g * HT + n // 2 + 1))
                    act.wait_ge(S("dve_did"), DID["v1_ones"])
                    nc.scalar.activation(vst1[:, s, :, 0:DH1], psum[:, 2 * s + 1, 0:D].rearrange("p (h v) -> p h v", h=H1), ACT.Copy).then_inc(S("v1_ready"), 1)
                    act.wait_ge(S("v1_ready"), t + 3)
                    act.dma_start(v1_d[ds(t * P, P), :], vst1[:, s, :, :].rearrange("p h v -> p (h v)")).then_inc(S(f"v1_st{s}"), 16)
                    if n or not first:
                        keep_qkT1(t - 1)

            qkv1_group_act(0, first=True)
            with act.Fori(1, GROUPS) as g:
                qkv1_group_act(g)
            keep_qkT1(TILES - 1)
            for s in range(2):
                act.sem_inc(S(f"a1_st{s}"), 16)
                act.sem_inc(S(f"a1r_st{s}"), 32)
            act.sem_inc(S("wT_ready"), 2)
            act.dma_start(ao1_d[IMAGES * SEQ:ROWS, :], zeros[0:ROWS - IMAGES * SEQ, :]).then_inc(S("a1_pad"), 16)

            def exp1(b, s, u):
                act.wait_ge(S("s1_read"), 4 * b + u + 3)
                w = wts[:, s, u // 2, (u % 2) * UNIT:(u % 2 + 1) * UNIT]
                nc.scalar.activation(w, w, ACT.Exp, scale=DH1 ** -0.5).then_inc(S("p1_ready"), 1)

            def keep_wT(b, s, n):
                act.wait_ge(S("wT_ps"), 5 * b + n + 1)
                if n < 4:
                    m = nc.scalar.activation(wT[:, s, 4 * n:4 * n + 4, :], psum[:, 4 + (5 * s + n) % 2, :].rearrange("p (h i) -> p h i", h=4), ACT.Copy)
                else:
                    m = nc.scalar.activation(wTr[0:RQ, s, :, :], psum[0:RQ, 4 + (5 * s + n) % 2, 0:2 * P].rearrange("p (g i) -> p g i", g=2), ACT.Copy)
                m.then_inc(S("wT_ready"), 1)

            def exp_rest(b):
                act.wait_ge(S("mr_ready"), b + 1)
                for g in range(2):
                    m = nc.scalar.activation(wr[0:RQ, g, :], psum[0:RQ, 7, g * SEQ:(g + 1) * SEQ], ACT.Exp, bias=mr[0:RQ, g:g + 1],
                                             scale=DH1 ** -0.5, accum_out=rr[0:RQ, g:g + 1])
                m.then_inc(S("wr_ready"), 1)

            def keep_wrT(b):
                act.wait_ge(S("wrT_ps"), b + 1)
                for n, rows in enumerate((P, REST)):
                    m = nc.scalar.activation(wrT[0:rows, n, :, :], psum[0:rows, 7, n * 2 * RQ:(n + 1) * 2 * RQ].rearrange("p (g i) -> p g i", g=2), ACT.Copy)
                m.then_inc(S("wrT_ready"), 1)

            def store_main(b, s):
                act.wait_ge(S("a1_ready"), b + 1)
                act.dma_start(ao1_d[ds(b * SEQ, P), :], a1m[:, s, :, :].rearrange("p h v -> p (h v)")).then_inc(S(f"a1_st{s}"), 16)

            def store_rest(b, s):
                act.wait_ge(S("a1r_ready"), b + 2)
                for g in range(2):
                    act.dma_start(ao1_d[ds(b * SEQ + P, REST), g * P:(g + 1) * P].rearrange("q (h d) -> h q d", h=HG), a1r[0:RQ, s, g, :]).then_inc(S(f"a1r_st{s}"), 16)

            def image1_act(b, s, first=False, last=False):
                exp1(b, s, 1)
                keep_wT(b, s, 0)
                if not first:
                    store_rest(b - 1, 1 - s)
                exp1(b, s, 2)
                keep_wT(b, s, 1)
                if not first:
                    store_main(b - 1, 1 - s)
                exp1(b, s, 3)
                exp_rest(b)
                keep_wT(b, s, 2)
                if not last:
                    exp1(b + 1, 1 - s, 0)
                keep_wrT(b)
                keep_wT(b, s, 3)
                keep_wT(b, s, 4)

            exp1(0, 0, 0)
            image1_act(0, 0, first=True)
            with act.Fori(0, IMAGES // 2 - 1) as i:
                image1_act(2 * i + 1, 1)
                image1_act(2 * i + 2, 0)
            image1_act(IMAGES - 1, 1, last=True)
            store_rest(IMAGES - 1, 1)
            store_main(IMAGES - 1, 1)
            with act.Fori(0, GROUPS) as g:
                for n in range(GT):
                    t = g * GT + n
                    act.wait_ge(S("rowsT_ps"), ROWS_A1 + t + 3)
                    act.wait_ge(S("product_ps"), PRODUCT_O1 + t + 1)
                    nc.scalar.activation(xT[:, n % 2, :, :], psum[:, n % 2, 0:D].rearrange("p (k n) -> p k n", k=KC), ACT.Copy).then_inc(S("rowsT_ready"), 1)
                act.wait_ge(S("ln_stats"), g + GROUPS + 3)
                nc.scalar.activation(rg, mvg[:, :, 1], ACT.Sqrt).then_inc(S("ln_root"), 1)
            with act.Fori(0, TILES // 2) as i:
                for s in range(2):
                    t = 2 * i + s
                    act.wait_ge(S("rowsT_ps"), ROWS_X3 + t + 3)
                    act.wait_ge(S("product_ps"), PRODUCT_ROUTER + t + 1)
                    nc.scalar.activation(x3T[:, s, :, :], psum[:, s, 0:D].rearrange("p (k n) -> p k n", k=KC), ACT.Copy).then_inc(S("rowsT_ready"), 1)
            act.wait_ge(S("dve_did"), DID["lg3_ready"])
            nc.scalar.activation(lg3, lg3, ACT.Exp).then_inc(S("act_did"), 1)
            act.sem_inc(S("hgT_ready"), 4)
            with act.Fori(0, TILES // 2) as i:
                for s in range(2):
                    t = 2 * i + s
                    act.wait_ge(S("hg_ps"), t + 5)
                    for k in range(KC):
                        nc.scalar.activation(hgT[:, k, :, ds(t * GB, GB)].rearrange("p h b -> p b h"),
                                             psum[:, s, k * P:(k + 1) * P].rearrange("p (b h) -> p b h", b=GB), ACT.Copy).then_inc(S("hgT_ready"), 1)
            for s in range(2):
                act.sem_inc(S(f"aof_st{s}"), 32)
            with act.Fori(0, PAIRS // 2) as i:
                for s in range(2):
                    p_ = 2 * i + s
                    act.wait_ge(S("mf_ready"), p_ + 1)
                    act.wait_ge(S("af_ready"), p_ + 1)
                    nc.scalar.activation(ef, psum[:, 2, 0:SEQ], ACT.Exp, bias=mf[:, s:s + 1], scale=DHF ** -0.5, accum_out=rf[:, s:s + 1]).then_inc(S("ef_ready"), 1)
                    act.wait_ge(S("aof_ready"), 2 * p_ + 4)
                    aof_bh = aof_d.rearrange("(b h) d -> b h d", h=HF)
                    act.dma_start(aof_bh[0:P, ds(2 * p_, 2), :], aofm[:, s, :, :]).then_inc(S(f"aof_st{s}"), 16)
                    act.dma_start(aof_bh[P:SEQ, ds(2 * p_, 2), :], aofr[0:REST, s, :, :]).then_inc(S(f"aof_st{s}"), 16)
            out_bs = out.rearrange("s b d -> b s d")
            for s in range(2):
                act.sem_inc(S(f"out_st{s}"), 16)

            def store_group(g, last=False):
                act.wait_ge(S("ln_stats"), g + 2 * GROUPS + 3)
                nc.scalar.activation(rg, mvg[:, :, 1], ACT.Sqrt).then_inc(S("ln_root"), 1)
                for n in range(GT):
                    t = g * GT + n
                    act.wait_ge(S("o1_ready"), t + 5)
                    if last and n == GT - 1:
                        act.dma_start(out_bs[SEQ - LASTB:SEQ, :, :], o1[0:LASTB * IMAGES, n, :]).then_inc(S(f"out_st{n % 2}"), 16)
                    else:
                        act.dma_start(out_bs[ds(t * GB, GB), :, :], o1[:, n, :]).then_inc(S(f"out_st{n % 2}"), 16)

            with act.Fori(0, GROUPS - 1) as g:
                store_group(g)
            store_group(GROUPS - 1, last=True)
            for s in range(2):
                act.wait_ge(S(f"out_st{s}"), 16 * (TILES // 2 + 1))

        @block.vector
        def _(dve):
            c = Count()

            def step(ins):
                ins.then_inc(S("dve_step"), 1)
                dve.wait_ge(S("dve_step"), c.next())

            def inverse_root(n):
                for t in range(TILES):
                    last = nc.vector.bn_aggr(mv[:, t, :], st6[:, t, :])
                step(last)
                step(nc.vector.tensor_scalar(mv[:, :, 1], mv[:, :, 1], 1e-5, None, ALU.add))
                dve.sem_inc(S("ln_stats"), 1)
                dve.wait_ge(S("ln_root"), n)
                step(nc.vector.reciprocal(rstd[:, :], rstd[:, :]))

            def normed(out_, t):
                return nc.vector.tensor_scalar(out_, h[:, t, :], mv[:, t, 0:1], rstd[:, ds(t, 1)], ALU.subtract, ALU.mult)

            dve.wait_ge(S("tables_ld"), 32)
            step(nc.vector.tensor_tensor(posb, posb, rowv[:, 0, :], ALU.add))
            dve.sem_inc(S("tok_ready"), 2)
            with dve.Fori(0, IMAGES // 4) as i:
                for s in range(2):
                    t = 2 * i + s
                    dve.wait_ge(S("tok_ps"), t + 3)
                    dve.wait_ge(S(f"tok_st{s}"), 32 * (i + 1))
                    nc.vector.tensor_tensor(h0s[:, s, :], psum[:, s, 0:D], posb, ALU.add).then_inc(S("tok_ready"), 1)
            for s in range(2):
                dve.wait_ge(S(f"tok_st{s}"), 32 * (IMAGES // 4 + 1))
                m = nc.vector.memset(vst[:, s, :, DH0:V0], 1.0)
            step(m)
            dve.sem_inc(S("dve_did"), 1)
            dve.wait_ge(S("h_ld"), 16)
            for t in range(TILES):
                m = nc.vector.bn_stats(st6[:, t, :], h[:, t, :])
            step(m)
            inverse_root(1)
            normed(xn[:, 0, :], 0).then_inc(S("xn_ready"), 1)
            dve.sem_inc(S("qkn_ready"), 2)

            def qk_step(t, s, last=False):
                if not last:
                    dve.wait_ge(S("xT_ps"), t)
                    normed(xn[:, 1 - s, :], t + 1).then_inc(S("xn_ready"), 1)
                dve.wait_ge(S("sq_ready"), t + 1)
                nc.vector.tensor_reduce(ssum[:, s, :], sq.rearrange("p (g d) -> p g d", d=DH0), X, ALU.add).then_inc(S("ssum_ready"), 1)
                dve.wait_ge(S("snorm_ready"), t + 1)
                step(nc.vector.tensor_scalar(snorm[:, s, :], snorm[:, s, :], 1e-12, None, ALU.max))
                step(nc.vector.reciprocal(snorm[:, s, :], snorm[:, s, :]))
                dve.wait_ge(S("qkT_ps"), 2 * t + 2)
                nc.vector.tensor_tensor(qkn[:, s, :].rearrange("p (g d) -> p g d", d=DH0),
                                        psum[:, 2 * s:2 * s + 2, :].rearrange("p a (g d) -> p (a g) d", d=DH0),
                                        snorm[:, s, :].unsqueeze(2).to_broadcast([P, 16, DH0]), ALU.mult).then_inc(S("qkn_ready"), 1)

            with dve.Fori(0, TILES // 2 - 1) as i:
                c.enter(i, 4)
                qk_step(2 * i, 0)
                qk_step(2 * i + 1, 1)
                c.leave(TILES // 2 - 1)
            qk_step(TILES - 2, 0)
            qk_step(TILES - 1, 1, True)
            dve.sem_inc(S("ao0_ready"), 2)
            with dve.Fori(0, IMAGES // 2) as i:
                c.enter(i, 8)
                for s in range(2):
                    b = 2 * i + s
                    dve.wait_ge(S(f"ao0_st{s}"), 32 * (i + 1))
                    for part, (o_, rows) in enumerate(((aom, P), (aor, REST))):
                        dve.wait_ge(S("pv0_ps"), 2 * b + part + 5)
                        pv = psum[0:rows, 4 + 2 * part:6 + 2 * part, 0:4 * V0].rearrange("p a (h v) -> p a h v", v=V0)
                        rs = rsum[0:rows, s, part, :]
                        step(nc.vector.tensor_scalar(rs.rearrange("p (a h) -> p a h", a=2), pv[:, :, :, DH0], 1e-6, None, ALU.max))
                        step(nc.vector.reciprocal(rs, rs))
                        nc.vector.tensor_tensor(o_[0:rows, s, :, :].rearrange("p (a h) v -> p a h v", a=2), pv[:, :, :, 0:DH0],
                                                rs.rearrange("p (a h) -> p a h", a=2).unsqueeze(3).to_broadcast([rows, 2, 4, DH0]),
                                                ALU.mult).then_inc(S("ao0_ready"), 1)
                c.leave(IMAGES // 2)
            dve.sem_inc(S("residual_ready"), 2)
            with dve.Fori(0, TILES // 2) as i:
                c.enter(i, 4)
                for s in range(2):
                    t = 2 * i + s
                    dve.wait_ge(S("product_ps"), t + 3)
                    step(nc.vector.tensor_tensor(h[:, t, :], psum[:, 2 + s, 0:D], h[:, t, :], ALU.add))
                    dve.sem_inc(S("residual_ready"), 1)
                    step(nc.vector.bn_stats(st6[:, t, :], h[:, t, :]))
                c.leave(TILES // 2)
            inverse_root(2)
            with dve.Fori(0, TILES // 2) as i:
                for s in range(2):
                    t = 2 * i + s
                    dve.wait_ge(S("rowsT_ps"), ROWS_X2 + t + 1)
                    dve.wait_ge(S("xn2_kept"), t + 1)
                    normed(xn[:, s, :], t).then_inc(S("xn2_ready"), 1)
            dve.wait_ge(S("product_ps"), PRODUCT_GATE + TILES + 2)

            def over8(x, n=TILES):
                return x.unsqueeze(2).to_broadcast([P, n, EXPERTS])

            step(nc.vector.tensor_copy(lg, psum[:, 6, 0:E8].rearrange("p (t e) -> p t e", e=EXPERTS)))
            step(nc.vector.tensor_reduce(r18, lg, X, ALU.max))
            step(nc.vector.tensor_tensor(lg, lg, over8(r18), ALU.subtract))
            dve.sem_inc(S("dve_did"), 1)
            dve.wait_ge(S("act_did"), EXP_EXPERTS)
            step(nc.vector.tensor_reduce(r18, lg, X, ALU.add))
            step(nc.vector.reciprocal(r18, r18))
            step(nc.vector.tensor_tensor(lg, lg, over8(r18), ALU.mult))
            experts = iota[:, 0:EXPERTS].unsqueeze(1).to_broadcast([P, TILES, EXPERTS])
            for k in range(2):
                step(nc.vector.tensor_reduce(val[:, k, :], lg, X, ALU.max))
                step(nc.vector.tensor_tensor(t8, lg, over8(val[:, k, :]), ALU.is_equal))
                step(nc.vector.tensor_scalar(u8, experts, -16.0, None, ALU.add))
                step(nc.vector.tensor_tensor(u8, u8, t8, ALU.mult))
                step(nc.vector.tensor_reduce(s18, u8, X, ALU.min))
                step(nc.vector.tensor_scalar(s18, s18, 16.0, None, ALU.add))
                step(nc.vector.tensor_tensor(oh[:, k, :, :], experts, over8(s18), ALU.is_equal))
                if k == 0:
                    step(nc.vector.scalar_tensor_tensor(out=lg, in0=oh[:, 0, :, :], scalar=-4.0, in1=lg, op0=ALU.mult, op1=ALU.add))
            step(nc.vector.tensor_tensor(s18, val[:, 0, :], val[:, 1, :], ALU.add))
            step(nc.vector.tensor_scalar(s18, s18, 1e-9, None, ALU.max))
            step(nc.vector.reciprocal(s18, s18))
            step(nc.vector.tensor_tensor(gates[:, :, :], val, s18.unsqueeze(1).to_broadcast([P, 2, TILES]), ALU.mult))
            step(nc.vector.tensor_tensor(mask, oh[:, 0, :, :], oh[:, 1, :, :], ALU.add))
            dve.sem_inc(S("dve_did"), 1)
            dve.wait_ge(S("pe_did"), RANKS)
            counts = psum[:, 5, 0:E8].rearrange("p (t e) -> p t e", e=EXPERTS)
            step(nc.vector.tensor_copy(ca, counts))
            x, y = ca, cb
            shift = 1
            while shift < TILES:
                step(nc.vector.tensor_tensor(y[:, shift:, :], x[:, shift:, :], x[:, 0:TILES - shift, :], ALU.add))
                step(nc.vector.tensor_copy(y[:, 0:shift, :], x[:, 0:shift, :]))
                x, y, shift = y, x, 2 * shift
            total = x[:, TILES - 1, :]
            step(nc.vector.tensor_tensor(cmp, total.unsqueeze(2).to_broadcast([P, EXPERTS, TILES]),
                                         q128.unsqueeze(1).to_broadcast([P, EXPERTS, TILES]), ALU.is_gt))
            step(nc.vector.tensor_reduce(nt, cmp, X, ALU.add))
            step(nc.vector.tensor_scalar(nt, nt, 1.0, None, ALU.max))
            step(nc.vector.memset(endf[:, 0:1], 0.0))
            for e in range(EXPERTS):
                step(nc.vector.tensor_tensor(endf[:, e + 1:e + 2], endf[:, e:e + 1], nt[:, e:e + 1], ALU.add))
            step(nc.vector.tensor_tensor(y, x, counts, ALU.subtract))
            step(nc.vector.tensor_tensor(y, psum[:, 7, 0:E8].rearrange("p (t e) -> p t e", e=EXPERTS), y, ALU.add))
            step(nc.vector.scalar_tensor_tensor(out=y, in0=endf[:, 0:EXPERTS].unsqueeze(1).to_broadcast([P, TILES, EXPERTS]),
                                                scalar=float(P), in1=y, op0=ALU.mult, op1=ALU.add))
            for k in range(2):
                step(nc.vector.tensor_tensor(t8, oh[:, k, :, :], y, ALU.mult))
                step(nc.vector.tensor_reduce(posf[:, k, :], t8, X, ALU.add))
            step(nc.vector.tensor_copy(slot[:, :, :], posf))
            dve.sem_inc(S("dve_did"), 1)
            step(nc.vector.tensor_tensor(cmpj, tile_no.unsqueeze(2).to_broadcast([P, SLOT_TILES, EXPERTS]),
                                         endf[:, 1:].unsqueeze(1).to_broadcast([P, SLOT_TILES, EXPERTS]), ALU.is_ge))
            step(nc.vector.tensor_reduce(ej, cmpj, X, ALU.add))
            step(nc.vector.tensor_scalar(ej, ej, float(EXPERTS - 1), None, ALU.min))
            step(nc.vector.tensor_scalar(moe_tab[:, 0, :], ej[0:1, :], 1.0, None, ALU.add))
            step(nc.vector.tensor_scalar(ej2, ej, 1.0, None, ALU.is_ge))
            for e in range(2, EXPERTS):
                step(nc.vector.scalar_tensor_tensor(out=ej2, in0=ej, scalar=float(e), in1=ej2, op0=ALU.is_ge,
                                                    op1=ALU.add if e % 2 else ALU.subtract, **({} if e % 2 else {"reverse1": True})))
            step(nc.vector.tensor_scalar(moe_tab[:, 1, :], ej2[0:1, :], float(EXPW), None, ALU.mult))
            step(nc.vector.tensor_scalar(end_tab[:, :], endf[0:1, 1:], 2.0, 2.0, ALU.mult, ALU.add))
            dve.sem_inc(S("dve_did"), 1)
            for e in range(2):
                dve.wait_ge(S("split01_hi"), e + 1)
                w = slice(e * EXPW, (e + 1) * EXPW)
                nc.vector.tensor_tensor(f32r(wlow[:, w]), wraw01[:, w], whigh[:, w], ALU.subtract).then_inc(S("split_ready"), 1)
            dve.sem_inc(S("hid_ready"), 2)
            dve.sem_inc(S("hidT_ready"), 2)
            dve.sem_inc(S("xTl_ready"), 2)

            def low_xT(j, s):
                dve.wait_ge(S("xsT_ready"), j + 3)
                nc.vector.tensor_tensor(f32r(xTl[:, s, :, :]), psum[:, 6, 0:D].rearrange("p (k n) -> p k n", k=KC), xTh[:, s, :, :],
                                        ALU.subtract).then_inc(S("xTl_ready"), 1)

            def hidden(n, s):
                dve.wait_ge(S("sil_ready"), n + 3)
                dve.wait_ge(S("hidT_ps"), n + 1)
                nc.vector.tensor_tensor(hid[:, s, :], sil[:, s, :], psum[:, 2 * s + 1, :], ALU.mult).then_inc(S("hid_ready"), 1)

            def keep_hidT(n, s):
                dve.wait_ge(S("hidT_ps"), n + 3)
                dve.wait_ge(S("dn_ps"), n + 1)
                t_ = psum[:, 4 + s, :].rearrange("p (k n) -> p k n", k=4)
                step(nc.vector.tensor_copy(f32r(hidTh[:, s, :, :]), t_))
                nc.vector.tensor_tensor(f32r(hidTl[:, s, :, :]), t_, hidTh[:, s, :, :], ALU.subtract).then_inc(S("hidT_ready"), 1)

            low_xT(0, 0)
            low_xT(1, 1)
            hidden(0, 0)
            hidden(1, 1)
            keep_hidT(0, 0)
            hidden(2, 0)
            keep_hidT(1, 1)
            with dve.Fori(0, SLOT_TILES // 2 - 1) as i:
                c.enter(i, 4)
                for j, s in ((2 * i + 1, 0), (2 * i + 2, 1)):
                    low_xT(j + 1, s)
                    hidden(2 * j + 1, 1)
                    keep_hidT(2 * j, 0)
                    hidden(2 * j + 2, 0)
                    keep_hidT(2 * j + 1, 1)
                c.leave(SLOT_TILES // 2 - 1)
            hidden(2 * SLOT_TILES - 1, 1)
            keep_hidT(2 * SLOT_TILES - 2, 0)
            keep_hidT(2 * SLOT_TILES - 1, 1)
            def combine(t, k):
                return nc.vector.scalar_tensor_tensor(out=h[:, t, :], in0=yg[:, k, t, :], scalar=gates[:, k, ds(t, 1)], in1=h[:, t, :],
                                                      op0=ALU.mult, op1=ALU.add)

            def combine_tile(t):
                for k in range(2):
                    step(combine(t, k))
                step(nc.vector.bn_stats(st6[:, t, :], h[:, t, :]))

            def root_group(g):
                tiles = slice(g * GT, (g + 1) * GT)
                for t in range(g * GT, (g + 1) * GT):
                    m = nc.vector.bn_aggr(mv[:, t, :], st6[:, t, :])
                step(m)
                step(nc.vector.tensor_scalar(mv[:, tiles, 1], mv[:, tiles, 1], 1e-5, None, ALU.add))
                dve.sem_inc(S("ln_stats"), 1)
                dve.wait_ge(S("ln_root"), g + 3)
                step(nc.vector.reciprocal(rstd[:, tiles], rstd[:, tiles]))
                dve.wait_ge(S("rowsT_ps"), ROWS_X1 + g * GT + 1)
                normed(xn[:, 0, :], g * GT).then_inc(S("xn1_ready"), 1)

            dve.wait_ge(S("yg_ld0"), 32 * GT)
            for k in range(2):
                for t in range(GT):
                    m = combine(t, k)
                step(m)
            for t in range(GT):
                m = nc.vector.bn_stats(st6[:, t, :], h[:, t, :])
            step(m)
            for s in range(2):
                m = nc.vector.memset(vst1[:, s, :, DH1:V1], 1.0)
            step(m)
            dve.sem_inc(S("dve_did"), 1)
            dve.sem_inc(S("qkr_ready"), 2)
            root_group(0)

            def rope_step(t, s, i, last=False):
                if not last:
                    dve.wait_ge(S("rowsT_ps"), ROWS_X1 + t + 2)
                    normed(xn[:, 1 - s, :], t + 1).then_inc(S("xn1_ready"), 1)
                dve.wait_ge(S("qkv1_ps"), t + 1)
                dve.wait_ge(S(f"rp_ld{s}"), 16 * (i + 1))
                dve.wait_ge(S("qkr_ready"), t + 2)
                qk = psum[:, 2 * s, :].rearrange("p (a e n) -> p a e n", a=2, e=2)
                nc.vector.tensor_tensor(ra, qk, rp[:, s, 0:2, :].unsqueeze(1).to_broadcast([P, 2, 2, P]), ALU.mult)
                step(nc.vector.tensor_tensor(rb, qk, rp[:, s, 1:3, :].unsqueeze(1).to_broadcast([P, 2, 2, P]), ALU.mult))
                dve.wait_ge(S("qkT1_ps"), t + 1)
                o_ = qkr[:, s, :, :].rearrange("p (a e) n -> p a e n", a=2)
                step(nc.vector.tensor_tensor(o_[:, :, 0, :], ra[:, :, 0, :], ra[:, :, 1, :], ALU.subtract))
                nc.vector.tensor_tensor(o_[:, :, 1, :], rb[:, :, 0, :], rb[:, :, 1, :], ALU.add).then_inc(S("qkr_ready"), 1)

            for g in range(GROUPS - 1):
                dve.wait_ge(S(f"yg_ld{g + 1}"), 32 * GT)
                with dve.Fori(0, GT // 2 - 1) as i:
                    c.enter(i, 10)
                    for s in range(2):
                        rope_step(g * GT + 2 * i + s, s, g * (GT // 2) + i)
                        combine_tile((g + 1) * GT + 2 * i + s)
                    c.leave(GT // 2 - 1)
                for s in range(2):
                    rope_step((g + 1) * GT - 2 + s, s, (g + 1) * (GT // 2) - 1, last=bool(s))
                    combine_tile((g + 2) * GT - 2 + s)
                root_group(g + 1)
            with dve.Fori(0, GT // 2 - 1) as i:
                c.enter(i, 4)
                for s in range(2):
                    rope_step(TILES - GT + 2 * i + s, s, (TILES - GT) // 2 + i)
                c.leave(GT // 2 - 1)
            for s in range(2):
                rope_step(TILES - 2 + s, s, TILES // 2 - 1, last=bool(s))
            dve.sem_inc(S("s1_read"), 2)
            dve.sem_inc(S("a1r_ready"), 1)

            def less_max(b, s, u):
                base = 2 * (u % 2)
                dve.wait_ge(S("s1_ps"), 4 * b + u + 1)
                sc = psum[:, base:base + 2, 0:2 * SEQ].rearrange("p a (h j) -> p a h j", j=SEQ)
                best = max1[:, u % 2, :]
                step(nc.vector.tensor_reduce(best.rearrange("p (a h) -> p a h", a=2), sc, X, ALU.max))
                for at, lo, n in ((FIRST_AT[u % 2], 0, P), (LAST_AT[u % 2], P, REST)):
                    m = nc.vector.tensor_tensor(wts[:, s, u // 2, at:at + 4 * n].rearrange("p (a h j) -> p a h j", a=2, h=2), sc[:, :, :, lo:lo + n],
                                                best.rearrange("p (a h) -> p a h", a=2).unsqueeze(3).to_broadcast([P, 2, 2, n]), ALU.subtract)
                m.then_inc(S("s1_read"), 1)

            def max_rest(b):
                dve.wait_ge(S("sr_ps"), b + 3)
                step(nc.vector.tensor_reduce(mr[0:RQ, :], psum[0:RQ, 7, 0:2 * SEQ].rearrange("p (g j) -> p g j", g=2), X, ALU.max))
                nc.vector.tensor_scalar(mr[0:RQ, :], mr[0:RQ, :], -(DH1 ** -0.5), None, ALU.mult).then_inc(S("mr_ready"), 1)

            def divide_main(b, s, turn):
                dve.wait_ge(S("pv1_ps"), b + 3)
                dve.wait_ge(S(f"a1_st{s}"), 16 * (turn + 1))
                pv = psum[:, 6, 0:H1 * V1].rearrange("p (h v) -> p h v", v=V1)
                step(nc.vector.reciprocal(rs1, pv[:, :, DH1]))
                nc.vector.tensor_tensor(a1m[:, s, :, :], pv[:, :, 0:DH1], rs1.unsqueeze(2).to_broadcast([P, H1, DH1]), ALU.mult).then_inc(S("a1_ready"), 1)

            def divide_rest(b, s, turn):
                dve.wait_ge(S("avr_ps"), b + 1)
                dve.wait_ge(S(f"a1r_st{s}"), 32 * (turn + 1))
                step(nc.vector.reciprocal(rr[0:RQ, :], rr[0:RQ, :]))
                step(nc.vector.tensor_tensor(avr[0:RQ, :, :, :], psum[0:RQ, 7, 0:2 * P].rearrange("p (g h v) -> p g h v", g=2, h=HG),
                                             restmask[0:RQ, :].unsqueeze(1).unsqueeze(3).to_broadcast([RQ, 2, HG, DH1]), ALU.mult))
                step(nc.vector.tensor_reduce(a1r[0:RQ, s, :, :], avr[0:RQ, :, :, :].rearrange("p g h v -> p g v h"), X, ALU.add))
                nc.vector.tensor_tensor(a1r[0:RQ, s, :, :], a1r[0:RQ, s, :, :], rr[0:RQ, :].unsqueeze(2).to_broadcast([RQ, 2, DH1]), ALU.mult).then_inc(S("a1r_ready"), 1)

            def image1_dve(b, s, turn, first=False, last=False):
                less_max(b, s, 2)
                if not first:
                    divide_main(b - 1, 1 - s, turn if s else turn - 1)
                less_max(b, s, 3)
                max_rest(b)
                if not last:
                    less_max(b + 1, 1 - s, 0)
                    less_max(b + 1, 1 - s, 1)
                divide_rest(b, s, turn)

            less_max(0, 0, 0)
            less_max(0, 0, 1)
            image1_dve(0, 0, 0, first=True)
            with dve.Fori(0, IMAGES // 2 - 1) as i:
                c.enter(i, 18)
                image1_dve(2 * i + 1, 1, i)
                image1_dve(2 * i + 2, 0, i + 1)
                c.leave(IMAGES // 2 - 1)
            image1_dve(IMAGES - 1, 1, IMAGES // 2 - 1, last=True)
            divide_main(IMAGES - 1, 1, IMAGES // 2 - 1)
            dve.wait_ge(S("h_bias"), 1)

            def group_root(stage, g):
                dve.sem_inc(S("dve_passed"), 1)
                for n in range(GT):
                    m = nc.vector.bn_aggr(mvg[:, n, :], stg[:, n, :])
                step(m)
                step(nc.vector.tensor_scalar(mvg[:, :, 1], mvg[:, :, 1], 1e-5, None, ALU.add))
                dve.sem_inc(S("ln_stats"), 1)
                dve.wait_ge(S("ln_root"), g + stage * GROUPS + 3)
                step(nc.vector.reciprocal(rg, rg))

            with dve.Fori(0, GROUPS) as g:
                c.enter(g, 5)
                for n in range(GT):
                    t = g * GT + n
                    dve.wait_ge(S("product_ps"), PRODUCT_O1 + t + 3)
                    nc.vector.tensor_tensor(h[:, t, :], psum[:, 2 + n % 2, 0:D], h[:, t, :], ALU.add).then_inc(S("residual_ready"), 1)
                dve.wait_ge(S("residual_ready"), RESIDUAL_3 + (g + 1) * GT + 2)
                dve.sem_inc(S("dve_passed"), 1)
                for n in range(GT):
                    m = nc.vector.bn_stats(stg[:, n, :], h[:, g * GT + n, :])
                step(m)
                group_root(1, g)
                for n in range(GT):
                    m = nc.vector.tensor_scalar(x3[:, g * GT + n, :], h[:, g * GT + n, :], mvg[:, n, 0:1], rg[:, n:n + 1], ALU.subtract, ALU.mult)
                step(m)
                dve.sem_inc(S("x3_ready"), 1)
                c.leave(GROUPS)
            dve.wait_ge(S("product_ps"), PRODUCT_ROUTER + TILES + 2)

            def over16(x):
                return x.unsqueeze(2).to_broadcast([P, TILES, HF])

            step(nc.vector.tensor_copy(lg3, psum[:, 4, 0:TILES * HF].rearrange("p (t e) -> p t e", e=HF)))
            step(nc.vector.tensor_reduce(rstd[:, :], lg3, X, ALU.max))
            step(nc.vector.tensor_tensor(lg3, lg3, over16(rstd[:, :]), ALU.subtract))
            dve.sem_inc(S("dve_did"), 1)
            dve.wait_ge(S("act_did"), EXP_HEADS)
            step(nc.vector.tensor_reduce(rstd[:, :], lg3, X, ALU.add))
            step(nc.vector.reciprocal(rstd[:, :], rstd[:, :]))
            step(nc.vector.tensor_tensor(lg3, lg3, over16(rstd[:, :]), ALU.mult))
            dve.sem_inc(S("dve_did"), 1)
            dve.wait_ge(S("pe_did"), PROBS_T)
            for rows, lo, n in ((P, 0, 2), (32, 2, 1)):
                def part(x):
                    return x[0:rows, lo * P:(lo + n) * P].rearrange("p (b s) -> p b s", s=IMAGES)

                nb = n * GB
                best = m3[0:rows, lo * GB:lo * GB + nb]
                over = best.unsqueeze(2).to_broadcast([rows, nb, IMAGES])
                images = iota[0:rows, :].unsqueeze(1).to_broadcast([rows, nb, IMAGES])
                step(nc.vector.tensor_copy(part(pT), psum[0:rows, 5, lo * P:(lo + n) * P].rearrange("p (b s) -> p b s", s=IMAGES)))
                step(nc.vector.tensor_reduce(best, part(pT), X, ALU.max))
                step(nc.vector.tensor_tensor(part(pT), part(pT), over, ALU.is_equal))
                step(nc.vector.tensor_scalar(part(uT), images, -float(IMAGES), None, ALU.add))
                step(nc.vector.tensor_tensor(part(uT), part(uT), part(pT), ALU.mult))
                step(nc.vector.tensor_reduce(best, part(uT), X, ALU.min))
                step(nc.vector.tensor_scalar(best, best, float(IMAGES), None, ALU.add))
                step(nc.vector.tensor_tensor(part(oT), images, over, ALU.is_equal))
            dve.sem_inc(S("dve_did"), 1)
            dve.wait_ge(S("pe_did"), CHOICES)
            step(nc.vector.tensor_copy(sel, psum[:, 6, 0:TILES * HF].rearrange("p (t h) -> p t h", h=HF)))
            dve.sem_inc(S("sel_all_ready"), 2)

            def select_tile(t, s):
                dve.wait_ge(S("hg_ps"), t + 3)
                nc.vector.tensor_tensor(selb[:, s, :, :], sel[:, t, :].unsqueeze(1).to_broadcast([P, GB, HF]),
                                        headmask.unsqueeze(2).to_broadcast([P, GB, HF]), ALU.mult).then_inc(S("selb_ready"), 1)

            def keep_selection(t, s):
                dve.wait_ge(S("hg_ps"), t + 5)
                nc.vector.tensor_copy(sel_all[:, t, :], psum[:, 2 + s, 0:P]).then_inc(S("sel_all_ready"), 1)

            select_tile(0, 0)
            with dve.Fori(0, TILES // 2 - 1) as i:
                for s in range(2):
                    select_tile(2 * i + s + 1, 1 - s)
                    keep_selection(2 * i + s, s)
            select_tile(TILES - 1, 1)
            keep_selection(TILES - 2, 0)
            keep_selection(TILES - 1, 1)
            dve.wait_ge(S("bf_ld"), 16)
            dve.sem_inc(S("vf_ready"), 2)
            dve.sem_inc(S("af_ready"), 1)
            dve.sem_inc(S("aof_ready"), 2)

            def bias(p_, x):
                return bf[:, ds(p_, 1), x:x + 1].rearrange("p a b -> p (a b)")

            def add_biases(p_, s):
                dve.wait_ge(S("qkvf_ps"), p_ + 3)
                qkv = psum[:, s, 0:3 * SEQ].rearrange("p (x n) -> p x n", x=3)
                step(nc.vector.tensor_scalar(qf, qkv[:, 0, :], bias(p_, 0), None, ALU.add))
                nc.vector.scalar_tensor_tensor(out=kf, in0=qkv[:, 1, :], scalar=bias(p_, 1), in1=qf, op0=ALU.add, op1=ALU.mult).then_inc(S("kf_ready"), 1)
                nc.vector.tensor_scalar(vf, qkv[:, 2, :], bias(p_, 2), None, ALU.add).then_inc(S("vf_ready"), 1)

            def weigh(p_, s):
                dve.wait_ge(S("attf_ps"), p_ + 1)
                step(nc.vector.tensor_reduce(mf[:, s:s + 1], psum[:, 2, 0:SEQ], X, ALU.max))
                nc.vector.tensor_scalar(mf[:, s:s + 1], mf[:, s:s + 1], -(DHF ** -0.5), None, ALU.mult).then_inc(S("mf_ready"), 1)
                dve.wait_ge(S("ef_ready"), p_ + 1)
                step(nc.vector.reciprocal(rf[:, s:s + 1], rf[:, s:s + 1]))
                dve.wait_ge(S("vf_ready"), p_ + 3)
                dve.wait_ge(S("aof_ps"), 2 * p_ + 2)
                nc.vector.scalar_tensor_tensor(out=af[:, s, :], in0=ef, scalar=rf[:, s:s + 1], in1=vf, op0=ALU.mult, op1=ALU.mult).then_inc(S("af_ready"), 1)

            def add_out_bias(p_, s, i):
                dve.wait_ge(S(f"aof_st{s}"), 32 * (i + 1))
                for n, (o_, rows, bank) in enumerate(((aofm, P, 4), (aofr, REST, 6))):
                    dve.wait_ge(S("aof_ps"), 2 * p_ + n + 5)
                    nc.vector.tensor_tensor(o_[0:rows, s, :, :], psum[0:rows, bank:bank + 2, 0:D],
                                            rowv[0:rows, 2, :].unsqueeze(1).to_broadcast([rows, 2, D]), ALU.add).then_inc(S("aof_ready"), 1)

            def pair_dve(p_, s, i, last=False):
                weigh(p_, s)
                if not last:
                    dve.wait_ge(S("af_ready"), p_ + 2)
                    add_biases(p_ + 1, 1 - s)
                add_out_bias(p_, s, i)

            add_biases(0, 0)
            with dve.Fori(0, PAIRS // 2 - 1) as i:
                c.enter(i, 6)
                pair_dve(2 * i, 0, i)
                pair_dve(2 * i + 1, 1, i)
                c.leave(PAIRS // 2 - 1)
            pair_dve(PAIRS - 2, 0, PAIRS // 2 - 1)
            pair_dve(PAIRS - 1, 1, PAIRS // 2 - 1, last=True)
            dve.sem_inc(S("y_sum"), 4)
            dve.sem_inc(S("o1_ready"), 4)
            with dve.Fori(0, GROUPS) as g:
                c.enter(g, 5)
                for n in range(GT):
                    t = g * GT + n
                    dve.wait_ge(S("yf_ps"), t + 3)
                    if n % HT == 0:
                        dve.wait_ge(S(f"x3b_ld{n // HT}"), 16 * HT * (g + 1))
                    nc.vector.tensor_tensor(ysum[:, n, :], psum[:, n, 0:D], x3b[:, n // HT, n % HT, :], ALU.add).then_inc(S("y_sum"), 1)
                dve.wait_ge(S("y_sum"), (g + 1) * GT + 4)
                dve.sem_inc(S("dve_passed"), 1)
                for n in range(GT):
                    m = nc.vector.bn_stats(stg[:, n, :], ysum[:, n, :])
                step(m)
                group_root(2, g)
                for s in range(2):
                    dve.wait_ge(S(f"out_st{s}"), 16 * HT * g + 16)
                for n in range(GT):
                    m = nc.vector.scalar_tensor_tensor(out=o1[:, n, :], in0=ysum[:, n, :], scalar=mvg[:, n, 0:1], in1=rowv[:, 3, :], op0=ALU.subtract, op1=ALU.mult)
                step(m)
                for n in range(GT):
                    if n % HT == 0:
                        dve.wait_ge(S(f"h3b_ld{n // HT}"), 16 * HT * (g + 1))
                    nc.vector.scalar_tensor_tensor(out=o1[:, n, :], in0=o1[:, n, :], scalar=rg[:, n:n + 1], in1=h3b[:, n // HT, n % HT, :],
                                                   op0=ALU.mult, op1=ALU.add).then_inc(S("o1_ready"), 1)
                c.leave(GROUPS)

        @block.tensor
        def _(pe):
            pe.sem_inc(S("tok_ps"), 2)
            pe.wait_ge(S("wtok_ld"), 16)
            with pe.Fori(0, IMAGES // 4) as i:
                for s in range(2):
                    t = 2 * i + s
                    pe.wait_ge(S(f"pt_ld{s}"), 16 * (i + 1))
                    pe.wait_ge(S("tok_ready"), t + 1)
                    for k in range(PK):
                        m = nc.tensor.matmul(psum[:, s, 0:D], pt[:, s, k, :], wtok_sb[:, k, :], start=(k == 0), stop=(k == PK - 1))
                    m.then_inc(S("tok_ps"), 1)
            pe.wait_ge(S("weights_ld"), 16 * 5)
            pe.wait_ge(S("tok_ready"), IMAGES // 2 + 2)
            pe.sem_inc(S("qkT_ps"), 4)

            def qkT_tile(t, s):
                pe.wait_ge(S("qkn_ready"), t + 3)
                for a in range(2):
                    pe.wait_ge(S("qkT_ready"), 2 * t + a + 1)
                    for k in range(4):
                        m = nc.tensor.transpose(psum[:, 6 + a, k * P:(k + 1) * P], qkn[:, s, (4 * a + k) * P:(4 * a + k + 1) * P], ident)
                    m.then_inc(S("qkT_ps"), 1)

            def xT_tile(t, s):
                pe.wait_ge(S("xn_ready"), t + 1)
                pe.wait_ge(S("xT_ready"), t + 2)
                for k in range(KC):
                    m = nc.tensor.transpose(psum[:, 5, k * P:(k + 1) * P], xn[:, s, k * P:(k + 1) * P], ident)
                m.then_inc(S("xT_ps"), 1)

            def qkv_tile(t, s, first=False, last=False):
                pe.wait_ge(S("xT_ready"), t + 3)
                pe.wait_ge(S("qkn_ready"), t + 1)
                for a, bank in ((0, 2 * s), (1, 2 * s + 1), (2, 4)):
                    if a == 2:
                        pe.wait_ge(S("v0_ready"), t + 1)
                    for k in range(KC):
                        m = nc.tensor.matmul(psum[:, bank, :], xT[:, s, k, :], wqkv_sb[:, k, a * 512:(a + 1) * 512], start=(k == 0), stop=(k == KC - 1))
                m.then_inc(S("qkv_ps"), 1)
                if not last:
                    xT_tile(t + 1, 1 - s)
                if not first:
                    qkT_tile(t - 1, 1 - s)

            xT_tile(0, 0)
            qkv_tile(0, 0, first=True)
            with pe.Fori(0, TILES // 2 - 1) as i:
                qkv_tile(2 * i + 1, 1)
                qkv_tile(2 * i + 2, 0)
            qkv_tile(TILES - 1, 1, last=True)
            qkT_tile(TILES - 1, 1)
            pe.sem_inc(S("pv0_ps"), 4)
            pe.sem_inc(S("s0_ps"), 4)

            def scores0(b, s, u):
                pe.wait_ge(S("qks_ready"), 2 * b + u + 1)
                pe.wait_ge(S("p0_ready"), 2 * b + u + 1)
                for r in range(2):
                    m = nc.tensor.matmul(psum[:, 2 * u + r, 0:2 * SEQ], kz[:, s, 2 * u + r, :], qz[:, s, 2 * u + r, :, :].rearrange("p h i -> p (h i)"),
                                         start=True, stop=True)
                if u:
                    for ch in range(4):
                        m = nc.tensor.matmul(psum[0:RQ, 3, 2 * SEQ:3 * SEQ], kblk0[:, s, ch, :], qkT[:, ch, ds(b * SEQ, SEQ)], start=(ch == 0), stop=(ch == 3))
                m.then_inc(S("s0_ps"), 1)

            def values0(s, part):
                lo, n = ((0, P), (P, REST))[part]
                for a in range(2):
                    bank = 4 + 2 * part + a
                    for hd in range(4):
                        nc.tensor.matmul(psum[0:n, bank, hd * V0:(hd + 1) * V0], pm[:, s, 4 * a + hd, lo:lo + n], vm[:, s, 4 * a + hd, :],
                                         start=(hd == 0), stop=False, skip_group_check=True)
                    m = nc.tensor.matmul(psum[0:n, bank, 0:4 * V0], pr[0:RQ, s, lo:lo + n],
                                         vdiag0[0:RQ, s, 4 * a:4 * a + 4, :].rearrange("p h v -> p (h v)"), start=False, stop=True, skip_group_check=True)
                m.then_inc(S("pv0_ps"), 1)

            def image0(b, s, i, last=False):
                if not last:
                    scores0(b + 1, 1 - s, 0)
                pe.wait_ge(S("p0_ready"), 2 * b + 4)
                pe.wait_ge(S("vdiag0_ready"), b + 1)
                pe.wait_ge(S(f"v0_ld{s}"), 32 * (i + 1))
                pe.wait_ge(S("ao0_ready"), 2 * b + 1)
                values0(s, 0)
                if not last:
                    scores0(b + 1, 1 - s, 1)
                pe.wait_ge(S("ao0_ready"), 2 * b + 2)
                values0(s, 1)

            scores0(0, 0, 0)
            scores0(0, 0, 1)
            with pe.Fori(0, IMAGES // 2 - 1) as i:
                image0(2 * i, 0, i)
                image0(2 * i + 1, 1, i)
            image0(IMAGES - 2, 0, IMAGES // 2 - 1)
            image0(IMAGES - 1, 1, IMAGES // 2 - 1, last=True)
            pe.wait_ge(S("weights_ld"), 16 * 5)
            pe.sem_inc(S("rowsT_ps"), 2)
            pe.sem_inc(S("product_ps"), 2)

            def aT_tile(t, s, i):
                pe.wait_ge(S(f"aT_ld{s}"), 16 * (i + 1))
                pe.wait_ge(S("rowsT_ready"), t + 1)
                for k in range(4):
                    m = nc.tensor.transpose(psum[:, s, k * P:(k + 1) * P], aT_in[:, s, k * P:(k + 1) * P], ident)
                m.then_inc(S("rowsT_ps"), 1)

            def o0_tile(t, s):
                pe.wait_ge(S("rowsT_ready"), t + 3)
                pe.wait_ge(S("residual_ready"), t + 1)
                for k in range(4):
                    m = nc.tensor.matmul(psum[:, 2 + s, 0:D], aT[:, s, k, :], wo_sb[:, k, :], start=(k == 0), stop=(k == 3))
                m.then_inc(S("product_ps"), 1)

            aT_tile(0, 0, 0)
            with pe.Fori(0, TILES // 2 - 1) as i:
                aT_tile(2 * i + 1, 1, i)
                o0_tile(2 * i, 0)
                aT_tile(2 * i + 2, 0, i + 1)
                o0_tile(2 * i + 1, 1)
            aT_tile(TILES - 1, 1, TILES // 2 - 1)
            o0_tile(TILES - 2, 0)
            o0_tile(TILES - 1, 1)
            pe.wait_ge(S("weights_ld"), 16 * 5)

            def xT2_tile(t, s):
                pe.wait_ge(S("xn2_ready"), t + 1)
                pe.wait_ge(S("rowsT_ready"), ROWS_X2 + t + 1)
                for k in range(KC):
                    m = nc.tensor.transpose(psum[:, 4 + s, k * P:(k + 1) * P], xn[:, s, k * P:(k + 1) * P], ident)
                m.then_inc(S("rowsT_ps"), 1)

            def gate_tile(t, s):
                pe.wait_ge(S("rowsT_ready"), ROWS_X2 + t + 3)
                for k in range(KC):
                    m = nc.tensor.matmul(psum[:, 6, ds(t * EXPERTS, EXPERTS)], xT[:, s, k, :], wgate_sb[:, k, :], start=(k == 0), stop=(k == KC - 1))
                m.then_inc(S("product_ps"), 1)

            xT2_tile(0, 0)
            with pe.Fori(0, TILES // 2 - 1) as i:
                xT2_tile(2 * i + 1, 1)
                gate_tile(2 * i, 0)
                xT2_tile(2 * i + 2, 0)
                gate_tile(2 * i + 1, 1)
            xT2_tile(TILES - 1, 1)
            gate_tile(TILES - 2, 0)
            gate_tile(TILES - 1, 1)
            pe.wait_ge(S("dve_did"), DID["mask_ready"])
            nc.tensor.matmul(psum[:, 7, 0:E8], tri, mask.rearrange("p t e -> p (t e)"), start=True, stop=True)
            nc.tensor.matmul(psum[:, 5, 0:E8], ones[:, :], mask.rearrange("p t e -> p (t e)"), start=True, stop=True).then_inc(S("pe_did"), 1)
            pe.sem_inc(S("xsT_ps"), 2)
            pe.sem_inc(S("hidT_ps"), 2)
            pe.sem_inc(S("dn_ps"), 2)

            def xsT_tile(j, s, i):
                pe.wait_ge(S(f"xsl_ld{s}"), 16 * (i + 1))
                pe.wait_ge(S("xTl_ready"), j + 2)
                for k in range(KC):
                    m = nc.tensor.transpose(psum[:, 6, k * P:(k + 1) * P], xsl[:, s, k * P:(k + 1) * P], ident)
                m.then_inc(S("xsT_ps"), 1)

            def gu_half(n, s, half, at):
                pe.wait_ge(S("hid_ready"), n + 1)
                for a in range(2):
                    for k in range(KC):
                        for n, (x_, w_) in enumerate(((xTh, whigh), (xTl, whigh), (xTh, wlow))):
                            m = nc.tensor.matmul(psum[:, 2 * half + a, :], f32r(x_[:, s, k, :]), f32r(w_[:, ds(at + k * 2 * F + a * F + half * 512, 512)]),
                                                 start=(k == 0 and n == 0), stop=(k == KC - 1 and n == 2))
                m.then_inc(S("gu_ps"), 1)

            def hidT_half(n, half):
                pe.wait_ge(S("hid_ready"), n + 3)
                pe.wait_ge(S("hidT_ready"), n + 1)
                for k in range(4):
                    m = nc.tensor.transpose(psum[:, 4 + half, k * P:(k + 1) * P], hid[:, half, k * P:(k + 1) * P], ident)
                m.then_inc(S("hidT_ps"), 1)

            def down_half(n, half, at):
                pe.wait_ge(S("hidT_ready"), n + 3)
                for k in range(4):
                    for n, (x_, w_) in enumerate(((hidTh, whigh), (hidTl, whigh), (hidTh, wlow))):
                        m = nc.tensor.matmul(psum[:, 7, 0:D], f32r(x_[:, half, k, :]), f32r(w_[:, ds(at + KC * 2 * F + (4 * half + k) * D, D)]),
                                             start=(half == 0 and k == 0 and n == 0), stop=(half == 1 and k == 3 and n == 2))
                m.then_inc(S("dn_ps"), 1)

            def expert_of(j):
                return pe.value_load(moe_tab[0:1, 0, ds(j, 1)], min_val=1, max_val=EXPERTS)

            def place_of(j):
                return pe.value_load(moe_tab[0:1, 1, ds(j, 1)], min_val=0, max_val=EXPW)

            def expert_tile(j, s, i, ready, before, at, nxt=True, carry=True):
                pe.wait_ge(S("wexp_ready"), ready)
                pe.sem_inc(S("pe_passed"), 1)
                pe.wait_ge(S("xTl_ready"), j + 3)
                gu_half(2 * j, s, 0, at)
                hidT_half(2 * j - 1, 1)
                pe.wait_ge(S("y_ready"), j + 1)
                down_half(2 * j - 2, 0, before)
                if nxt:
                    xsT_tile(j + 1, 1 - s, i)
                gu_half(2 * j + 1, s, 1, at)
                following = (expert_of(j + 1), place_of(j + 1)) if nxt and carry else None
                hidT_half(2 * j, 0)
                down_half(2 * j - 1, 1, before)
                return following

            pe.wait_ge(S("dve_did"), DID["tables_ready"])
            xsT_tile(0, 0, 0)
            xsT_tile(1, 1, 0)
            ready, first = expert_of(0), place_of(0)
            pe.wait_ge(S("xTl_ready"), 3)
            pe.wait_ge(S("wexp_ready"), ready)
            gu_half(0, 0, 0, first)
            gu_half(1, 0, 1, first)
            hidT_half(0, 0)
            LASTJ = SLOT_TILES - 1
            with pe.Fori(0, SLOT_TILES // 2 - 1) as i:
                before, ready, at = place_of(2 * i), expert_of(2 * i + 1), place_of(2 * i + 1)
                ready2, at2 = expert_tile(2 * i + 1, 1, i + 1, ready, before, at)
                expert_tile(2 * i + 2, 0, i + 1, ready2, at, at2, carry=False)
            before, ready, at = place_of(LASTJ - 1), expert_of(LASTJ), place_of(LASTJ)
            expert_tile(LASTJ, 1, 0, ready, before, at, nxt=False)
            hidT_half(2 * LASTJ + 1, 1)
            pe.wait_ge(S("y_ready"), LASTJ + 2)
            down_half(2 * LASTJ, 0, at)
            down_half(2 * LASTJ + 1, 1, at)
            pe.wait_ge(S("weights1_ld"), 32)
            pe.sem_inc(S("qkT1_ps"), 2)

            def qkT1_tile(t, s):
                pe.wait_ge(S("qkr_ready"), t + 3)
                pe.wait_ge(S("qkT1_ready"), t + 2)
                for k in range(4):
                    m = nc.tensor.transpose(psum[:, 6, k * P:(k + 1) * P], qkr[:, s, k, :], ident)
                m.then_inc(S("qkT1_ps"), 1)

            def x1T_tile(t, s):
                pe.wait_ge(S("xn1_ready"), t + 1)
                pe.wait_ge(S("rowsT_ready"), ROWS_X1 + t + 2)
                for k in range(KC):
                    m = nc.tensor.transpose(psum[:, 5, k * P:(k + 1) * P], xn[:, s, k * P:(k + 1) * P], ident)
                m.then_inc(S("rowsT_ps"), 1)

            def qkv1_tile(t, s):
                pe.wait_ge(S("rowsT_ready"), ROWS_X1 + t + 3)
                pe.wait_ge(S("qkr_ready"), t + 1)
                pe.wait_ge(S("v1_ready"), t + 1)
                for a, n in ((0, 512), (1, D)):
                    for k in range(KC):
                        m = nc.tensor.matmul(psum[:, 2 * s + a, 0:n], xT[:, s, k, :], wqkv1_sb[:, k, a * 512:a * 512 + n], start=(k == 0), stop=(k == KC - 1))
                m.then_inc(S("qkv1_ps"), 1)

            def qkv1_group(g, first=False):
                for n in range(GT):
                    t, s = g * GT + n, n % 2
                    if n == 0:
                        x1T_tile(t, s)
                    qkv1_tile(t, s)
                    if n < GT - 1:
                        x1T_tile(t + 1, 1 - s)
                    if n or not first:
                        qkT1_tile(t - 1, 1 - s)

            qkv1_group(0, first=True)
            with pe.Fori(1, GROUPS) as g:
                qkv1_group(g)
            qkT1_tile(TILES - 1, 1)
            pe.sem_inc(S("pv1_ps"), 2)
            pe.sem_inc(S("sr_ps"), 2)

            def scores1(b, s, u):
                if u == 0:
                    pe.wait_ge(S("q1_ready"), b + 1)
                pe.wait_ge(S("s1_read"), 4 * b + u + 1)
                for r in range(2):
                    lo = 4 * (u % 2) + 2 * r
                    m = nc.tensor.matmul(psum[:, 2 * (u % 2) + r, 0:2 * SEQ], q1[:, s, u // 2, :],
                                         kblk[:, s, u // 2, lo:lo + 2, :].rearrange("p h j -> p (h j)"), start=True, stop=True)
                m.then_inc(S("s1_ps"), 1)

            def transpose1(b, s, n):
                if n < 4:
                    pe.wait_ge(S("p1_ready"), 4 * b + n + 1)
                pe.wait_ge(S("wT_ready"), 5 * b + n + 1)
                bank = 4 + (5 * s + n) % 2
                if n < 4:
                    for hd in range(4):
                        at = FIRST_AT[n % 2] + hd * P
                        m = nc.tensor.transpose(psum[:, bank, hd * P:(hd + 1) * P], wts[:, s, n // 2, at:at + P], ident)
                else:
                    for g in range(2):
                        m = nc.tensor.transpose(psum[0:RQ, bank, g * P:(g + 1) * P], wts[:, s, g, LAST_AT[0]:LAST_AT[0] + RQ], ident)
                m.then_inc(S("wT_ps"), 1)

            def values1(b, s):
                pe.wait_ge(S("wT_ready"), 5 * b + 7)
                pe.wait_ge(S("vdiag_ready"), b + 1)
                for hd in range(H1):
                    nc.tensor.matmul(psum[:, 6, hd * V1:(hd + 1) * V1], wT[:, s, hd, :], v1m[:, s, hd, :], start=(hd == 0), stop=False, skip_group_check=True)
                for g in range(2):
                    m = nc.tensor.matmul(psum[:, 6, g * HG * V1:(g + 1) * HG * V1], wTr[0:RQ, s, g, :],
                                         vdiag[0:RQ, s, g, :, :].rearrange("p h v -> p (h v)"), start=False, stop=(g == 1), skip_group_check=True)
                m.then_inc(S("pv1_ps"), 1)

            def scores_rest(b, s):
                pe.wait_ge(S("a1r_ready"), b + 1)
                for g in range(2):
                    m = nc.tensor.matmul(psum[0:RQ, 7, g * SEQ:(g + 1) * SEQ], qblk[:, s, g, :], qkT1[:, 2 + g, ds(b * SEQ, SEQ)], start=True, stop=True)
                m.then_inc(S("sr_ps"), 1)

            def transpose_rest(b):
                pe.wait_ge(S("wr_ready"), b + 1)
                for n, (rows, lo) in enumerate(((P, 0), (REST, P))):
                    for g in range(2):
                        m = nc.tensor.transpose(psum[0:rows, 7, (2 * n + g) * RQ:(2 * n + g + 1) * RQ], wr[0:RQ, g, lo:lo + rows], ident[0:RQ, 0:RQ])
                m.then_inc(S("wrT_ps"), 1)

            def values_rest(b, s):
                pe.wait_ge(S("wrT_ready"), b + 1)
                for g in range(2):
                    o_ = psum[0:RQ, 7, g * P:(g + 1) * P].rearrange("p (h v) -> p h v", h=HG)
                    nc.tensor.matmul(o_, wrT[:, 0, g, :], v1m[:, s, HG * g:HG * (g + 1), 0:DH1], start=True, stop=False)
                    m = nc.tensor.matmul(o_, wrT[0:REST, 1, g, :],
                                         vraw[0:REST, s, :].rearrange("p (h v) -> p h v", h=H1)[:, HG * g:HG * (g + 1), 0:DH1], start=False, stop=True)
                m.then_inc(S("avr_ps"), 1)

            def image1(b, s, turn, first=False, last=False):
                scores1(b, s, 2)
                transpose1(b, s, 0)
                if not first:
                    values1(b - 1, 1 - s)
                scores1(b, s, 3)
                transpose1(b, s, 1)
                scores_rest(b, s)
                if not last:
                    scores1(b + 1, 1 - s, 0)
                transpose1(b, s, 2)
                transpose_rest(b)
                if not last:
                    scores1(b + 1, 1 - s, 1)
                transpose1(b, s, 3)
                transpose1(b, s, 4)
                pe.wait_ge(S(f"v1_ld{s}"), 32 * (turn + 1))
                values_rest(b, s)

            scores1(0, 0, 0)
            scores1(0, 0, 1)
            image1(0, 0, 0, first=True)
            with pe.Fori(0, IMAGES // 2 - 1) as i:
                image1(2 * i + 1, 1, i)
                image1(2 * i + 2, 0, i + 1)
            image1(IMAGES - 1, 1, IMAGES // 2 - 1, last=True)
            values1(IMAGES - 1, 1)

            def a1T_tile(t, s, i):
                pe.wait_ge(S(f"a1T_ld{s}"), 16 * (i + 1))
                pe.wait_ge(S("rowsT_ready"), ROWS_A1 + t + 1)
                for k in range(KC):
                    m = nc.tensor.transpose(psum[:, s, k * P:(k + 1) * P], a1T_in[:, s, k * P:(k + 1) * P], ident)
                m.then_inc(S("rowsT_ps"), 1)

            def o1_tile(t, s):
                pe.wait_ge(S("rowsT_ready"), ROWS_A1 + t + 3)
                pe.wait_ge(S("residual_ready"), RESIDUAL_3 + t + 1)
                for k in range(KC):
                    m = nc.tensor.matmul(psum[:, 2 + s, 0:D], xT[:, s, k, :], wo1_sb[:, k, :], start=(k == 0), stop=(k == KC - 1))
                m.then_inc(S("product_ps"), 1)

            a1T_tile(0, 0, 0)
            with pe.Fori(0, TILES // 2 - 1) as i:
                a1T_tile(2 * i + 1, 1, i)
                o1_tile(2 * i, 0)
                a1T_tile(2 * i + 2, 0, i + 1)
                o1_tile(2 * i + 1, 1)
            a1T_tile(TILES - 1, 1, TILES // 2 - 1)
            o1_tile(TILES - 2, 0)
            o1_tile(TILES - 1, 1)
            pe.wait_ge(S("weights_ld"), 16 * 5)

            def x3T_tile(g, n):
                if n % HT == 0:
                    pe.wait_ge(S(f"xg_ld{n // HT}"), 16 * HT * (g + 1))
                pe.wait_ge(S("rowsT_ready"), ROWS_X3 + g * GT + n + 1)
                for k in range(KC):
                    m = nc.tensor.transpose(psum[:, n % 2, k * P:(k + 1) * P], xg[:, n // HT, n % HT, k * P:(k + 1) * P], ident)
                m.then_inc(S("rowsT_ps"), 1)

            def router_tile(g, n):
                t = g * GT + n
                pe.wait_ge(S("rowsT_ready"), ROWS_X3 + t + 3)
                for k in range(KC):
                    m = nc.tensor.matmul(psum[:, 4, ds(t * HF, HF)], x3T[:, n % 2, k, :], wrout_sb[:, k, :], start=(k == 0), stop=(k == KC - 1))
                m.then_inc(S("product_ps"), 1)

            with pe.Fori(0, GROUPS) as g:
                x3T_tile(g, 0)
                for n in range(1, GT):
                    x3T_tile(g, n)
                    router_tile(g, n - 1)
                router_tile(g, GT - 1)
            pe.wait_ge(S("dve_did"), DID["pr3_ready"])
            pr3 = lg3.rearrange("p t e -> p (t e)")
            for n, cols in enumerate((P, P, 32)):
                m = nc.tensor.transpose(psum[0:cols, 5, n * P:(n + 1) * P], pr3[:, n * P:n * P + cols], ident)
            m.then_inc(S("pe_did"), 1)
            pe.wait_ge(S("dve_did"), DID["oT_ready"])
            for n, rows in enumerate((P, P, 32)):
                m = nc.tensor.transpose(psum[:, 6, n * P:n * P + rows], oT[0:rows, n * P:(n + 1) * P], ident[0:rows, 0:rows])
            m.then_inc(S("pe_did"), 1)
            pe.sem_inc(S("hg_ps"), 4)
            with pe.Fori(0, GROUPS) as g:
                for n in range(GT):
                    t, s = g * GT + n, n % 2
                    if n % HT == 0:
                        pe.wait_ge(S(f"xg_ld{n // HT}"), 16 * HT * (g + 1 + GROUPS))
                    pe.wait_ge(S("selb_ready"), t + 1)
                    pe.wait_ge(S("sel_all_ready"), t + 1)
                    pe.wait_ge(S("hgT_ready"), 2 * t + 2)
                    selm = selb[:, s, :, :].rearrange("p b h -> p (b h)")
                    for k in range(KC):
                        nc.tensor.matmul(psum[:, s, k * P:(k + 1) * P], xg[:, n // HT, n % HT, k * P:(k + 1) * P], selm, start=True, stop=True)
                    nc.tensor.transpose(psum[:, 2 + s, 0:P], selm, ident).then_inc(S("hg_ps"), 1)
            pe.sem_inc(S("qkvf_ps"), 2)
            pe.sem_inc(S("aof_ps"), 4)

            def qkvf_pair(p_, s, i):
                pe.wait_ge(S(f"wf_ld{s}"), 16 * (i + 1))
                pe.wait_ge(S("hgp_ready"), p_ + 1)
                pe.wait_ge(S("vf_ready"), p_ + 1)
                for x in range(3):
                    for r in range(2):
                        for k in range(KC):
                            m = nc.tensor.matmul(psum[64 * r:64 * r + 64, s, x * SEQ:(x + 1) * SEQ], wf[:, s, k, x, 64 * r:64 * r + 64], hgp[:, s, k, r, :],
                                                 start=(k == 0), stop=(k == KC - 1))
                m.then_inc(S("qkvf_ps"), 1)

            def pair_pe(p_, s, i, i_next, last=False):
                pe.wait_ge(S("kf_ready"), p_ + 1)
                nc.tensor.matmul(psum[:, 2, 0:SEQ], blockones, kf, start=True, stop=True).then_inc(S("attf_ps"), 1)
                if not last:
                    qkvf_pair(p_ + 1, 1 - s, i_next)
                pe.wait_ge(S(f"wof_ld{s}"), 16 * (i + 1))
                pe.wait_ge(S("af_ready"), p_ + 2)
                pe.wait_ge(S("aof_ready"), 2 * p_ + 2)
                for lo, n, bank in ((0, P, 4), (P, REST, 6)):
                    for r in range(2):
                        m = nc.tensor.matmul(psum[0:n, bank + r, 0:D], af[64 * r:64 * r + 64, s, lo:lo + n], wof[64 * r:64 * r + 64, s, :], start=True, stop=True)
                    m.then_inc(S("aof_ps"), 1)

            qkvf_pair(0, 0, 0)
            with pe.Fori(0, PAIRS // 2 - 1) as i:
                pair_pe(2 * i, 0, i, i)
                pair_pe(2 * i + 1, 1, i, i + 1)
            pair_pe(PAIRS - 2, 0, PAIRS // 2 - 1, PAIRS // 2 - 1)
            pair_pe(PAIRS - 1, 1, PAIRS // 2 - 1, 0, last=True)
            pe.sem_inc(S("yf_ps"), 2)
            with pe.Fori(0, GROUPS) as g:
                for n in range(GT):
                    t = g * GT + n
                    if n % HT == 0:
                        pe.wait_ge(S(f"aofl_ld{n // HT}"), 16 * HT * (g + 1))
                    pe.wait_ge(S("sel_ready"), t + 1)
                    if n == 0:
                        pe.wait_ge(S("y_sum"), g * GT + 4)
                    nc.tensor.matmul(psum[:, n, 0:D], sel_s[:, n % 2, :], aofl[:, n // HT, n % HT, :], start=True, stop=True).then_inc(S("yf_ps"), 1)


_OUTS = [((IMAGES, SEQ, D), "float32")]


def shape_constants():
    import numpy as np
    c = np.zeros((P, C_WIDTH), np.float32)
    r = np.arange(P)
    c[:, C_IDENT:C_IDENT + P] = np.eye(P)
    c[:, C_TRI:C_TRI + P] = r[:, None] < r[None, :]
    c[:, C_BLOCK:C_BLOCK + P] = r[:, None] // DHF == r[None, :] // DHF
    c[:, C_HEAD:C_HEAD + 8] = r[:, None] // 16 == np.arange(8)
    c[:, C_IOTA:C_IOTA + 16] = np.arange(16)
    c[:, C_TILE:C_TILE + SLOT_TILES] = np.arange(SLOT_TILES)
    c[:, C_Q128:C_Q128 + TILES] = P * np.arange(TILES)
    c[:, C_REST:C_REST + 8] = (r[:, None] // REST == np.arange(8))
    c[:, C_CHUNK:C_CHUNK + 32] = ((2 * np.arange(4)[:, None] + r[:, None, None] // DH0) == np.arange(8)).reshape(P, 32)
    grid = np.arange(8)
    hp, wp = (g.reshape(-1).astype(np.float32) for g in np.meshgrid(grid, grid, indexing="ij"))
    quarter = D // 4
    factor = np.float32(10000.0) ** (np.arange(quarter, dtype=np.float32) / quarter)
    a, b = hp[:, None] / factor, wp[:, None] / factor
    pos = np.concatenate([np.sin(a), np.cos(a), np.sin(b), np.cos(b)], -1).astype(np.float32)
    pos = np.concatenate([pos, pos])
    freqs = np.exp(np.arange(0, D, 2, dtype=np.float32) * np.float32(-np.log(10000.0) / D))
    ang = (np.arange(ROWS) % SEQ).astype(np.float32)[:, None] * freqs
    cs = np.stack([np.cos(ang), np.sin(ang), np.cos(ang)], 1).astype(np.float32)
    rope = np.ascontiguousarray(cs.reshape(TILES, P, 3, P).transpose(1, 0, 2, 3))
    return c, pos, rope


def layouts(i):
    import numpy as np

    def chunks(w):
        return np.ascontiguousarray(w.reshape(-1, P, w.shape[-1]).transpose(1, 0, 2))

    i = {k: np.asarray(v) for k, v in i.items()}
    c, pos, rope = shape_constants()
    x = i["x"].reshape(IMAGES, 3, 8, 16, 8, 16).transpose(1, 3, 5, 0, 2, 4).reshape(PK, P, 8, P)
    wp = i["L0_tok_Wp"].reshape(D, 16, 16, 3).transpose(3, 1, 2, 0).reshape(768, D)
    even_odd = np.concatenate([np.arange(0, D, 2), np.arange(1, D, 2)])
    qkv1 = np.concatenate([i["L1_attn_wq"][even_odd].T, i["L1_attn_wk"][even_odd].T, i["L1_attn_wv"].T], 1)
    wq = i["L1_ffn_Wq"]
    wkv = i["L1_ffn_Wkv"]
    qkvf = np.stack([wq, wkv[..., :DHF], wkv[..., DHF:]], 2)
    qkvf = qkvf.reshape(PAIRS, 2, KC, P, 3, DHF).transpose(0, 3, 2, 4, 1, 5).reshape(PAIRS, P, KC * 3 * 2 * DHF)
    bf = np.stack([i["L1_ffn_bq"], i["L1_ffn_bkv"][:, :DHF], i["L1_ffn_bkv"][:, DHF:]], 1)
    bf = bf.reshape(PAIRS, 2, 3, DHF).transpose(1, 3, 0, 2).reshape(P, PAIRS * 3)
    rowv = np.stack([i["L0_tok_b"], i["L1_attn_wo_b"], i["L1_ffn_bo"], i["L1_ffn_ln_g"], i["L1_ffn_ln_b"]])
    gu = i["L0_ffn_w_gate_up"].reshape(EXPERTS, KC, P, 2 * F).transpose(0, 2, 1, 3)
    dn = i["L0_ffn_w_down"].reshape(EXPERTS, FK, P, D).transpose(0, 2, 1, 3)
    a = {
        "patches": x.transpose(2, 1, 0, 3), "txt": i["txt"], "pos_table": pos,
        "row_vectors": np.broadcast_to(rowv, (P, 5, D)), "w_tok": chunks(wp),
        "w_qkv0": chunks(np.concatenate([i["L0_attn_Wq"], i["L0_attn_Wkv"]], 1)), "w_o0": chunks(i["L0_attn_Wo"]),
        "w_gate": chunks(i["L0_ffn_w_gate"]), "w_gu": gu.reshape(EXPERTS, P, KC * 2 * F), "w_down": dn.reshape(EXPERTS, P, FK * D),
        "w_qkv1": chunks(qkv1), "w_o1": chunks(i["L1_attn_wo_w"].T), "rope": rope, "w_router": chunks(i["L1_ffn_Wg"]),
        "w_qkvf": qkvf, "b_qkvf": bf, "w_of": i["L1_ffn_Wo"].reshape(PAIRS, P, D), "constants": c,
    }
    return {k: np.ascontiguousarray(v) for k, v in a.items()}


def kernel(**inputs):
    import numpy as _np
    import concourse.bacc as _bacc
    from concourse import mybir as _mybir
    from concourse.bass_utils import run_bass_kernel_spmd as _run

    nc = _bacc.Bacc("TRN2", target_bir_lowering=False, num_devices=1)
    arrays, args = {}, []
    for name, a in layouts(inputs).items():
        arrays[f"in_{name}"] = a
        args.append(nc.dram_tensor(f"in_{name}", a.shape, _mybir.dt.from_np(a.dtype), kind="ExternalInput").ap())
    shape, dtype = _OUTS[0]
    args.append(nc.dram_tensor("out_0", shape, _mybir.dt.from_np(_np.dtype(dtype)), kind="ExternalOutput").ap())
    fusion_kernel(nc, *args)
    r = _run(nc, [arrays], core_ids=[0])
    return r.results[0]["out_0"]
```

```python
import concourse.bass as bass
from concourse import mybir
from contextlib import ExitStack

IMAGES = 16
PATCHES = 64
TEXT = 77
SEQ = PATCHES + TEXT
D = 256
P = 128
KC = D // P
TILES = -(-IMAGES * SEQ // P)
ROWS = TILES * P
REST = SEQ - P
PK = 768 // P
H0, DH0 = 8, 64
INNER = H0 * DH0
V0 = DH0 + 1
H1, DH1 = 16, 16
V1 = DH1 + 1
HG = P // DH1
RQ = HG * REST
EXPERTS = 8
F = 1024
FK = F // P
SLOT_TILES = 44
SLOTS = SLOT_TILES * P
HF, DHF = 16, 64
POS = ROWS // IMAGES
GB = P // IMAGES
PAIRS = HF // 2
GROUPS = 3
GT = TILES // GROUPS
HT = GT // 2
EXPW = KC * 2 * F + FK * D
assert all(((b + 1) * SEQ - 1) // P <= min(b + 2, TILES - 1) for b in range(IMAGES))
assert SLOT_TILES >= (2 * ROWS + EXPERTS * (P - 1)) // P and POS >= SEQ and TILES % (2 * GROUPS) == 0
C_IDENT, C_TRI, C_BLOCK, C_HEAD, C_IOTA, C_TILE, C_Q128 = 0, 128, 256, 384, 392, 408, 452
C_REST = 470
C_CHUNK = 478
C_WIDTH = 510


class Count:

    def __init__(self):
        self.n, self.off = 0, 0

    def next(self, k=1):
        self.n += k
        return self.off + self.n

    def enter(self, i, per):
        self.mark, self.per, self.off = self.n, per, i * per

    def leave(self, turns):
        assert self.n - self.mark == self.per, (self.n - self.mark, self.per)
        self.n, self.off = self.mark + self.per * turns, 0


def ds(start, size):
    return bass.ds(start, size)


def load_expert(nc, S, place, w_gu, w_down, e):
    nc.gpsimd.dma_start(place[:, 0:KC * 2 * F], w_gu[e, :, :]).then_inc(S("wexp_ld"), 16)
    nc.gpsimd.dma_start(place[:, KC * 2 * F:EXPW], w_down[e, :, :]).then_inc(S("wexp_ld"), 16)


def fusion_kernel(nc, patches, txt, pos_table, row_vectors, w_tok, w_qkv0, w_o0, w_gate, w_gu, w_down,
                  w_qkv1, w_o1, rope, w_router, w_qkvf, b_qkvf, w_of, constants, out):
    f32, i32 = mybir.dt.float32, mybir.dt.int32
    ALU, ACT, X = mybir.AluOpType, mybir.ActivationFunctionType, mybir.AxisListType.X
    ctx = ExitStack()
    with ctx:
        starts = {}

        def sb(name, shape, dt=f32):
            base = -(-nc.sbuf_base // 32) * 32
            starts[name] = base
            return ctx.enter_context(nc.sbuf_tensor(name, shape, dt))

        def over(name, buffer, at, width):
            return nc.alloc_sbuf_tensor_at(name, [P, width], f32, offset=starts[buffer] + 4 * at)[:, :]

        def dram(name, shape):
            return nc.dram_tensor(name, shape, f32).ap()

        h0_d = dram("h0_scratch", [ROWS, D])
        v0_d = dram("v0_scratch", [ROWS, H0 * V0])
        ao0_d = dram("attn0_scratch", [ROWS, INNER])
        xs_d = dram("slot_in_scratch", [SLOTS, D])
        ys_d = dram("slot_out_scratch", [SLOTS, D])
        v1_d = dram("v1_scratch", [ROWS, H1 * V1])
        ao1_d = dram("attn1_scratch", [ROWS, D])
        x3_d = dram("x3_scratch", [ROWS, D])
        h3_d = dram("h3_scratch", [ROWS, D])
        aof_d = dram("aof_scratch", [POS * HF, D])

        psum = ctx.enter_context(nc.psum_tensor("psum", [P, 8, 512], f32))

        const = sb("const", [P, C_WIDTH])
        ident = const[:, C_IDENT:C_IDENT + P]
        tri = const[:, C_TRI:C_TRI + P]
        blockones = const[:, C_BLOCK:C_BLOCK + P]
        headmask = const[:, C_HEAD:C_HEAD + 8]
        chunkmask = const[:, C_CHUNK:C_CHUNK + 32]
        restmask = const[:, C_REST:C_REST + 8]
        iota = const[:, C_IOTA:C_IOTA + 16]
        tile_no = const[:, C_TILE:C_TILE + SLOT_TILES]
        q128 = const[:, C_Q128:C_Q128 + TILES]
        rowv = sb("rowv", [P, 5, D])
        ones = sb("ones", [P, P])
        zeros = sb("zeros", [P, D])
        minus16 = sb("minus16", [P, 1])
        h = sb("h", [P, TILES, D])
        wqkv = sb("wqkv", [P, KC * 3 * INNER])
        wo_sb = sb("wo_sb", [P, 4, D])
        wgate_sb = sb("wgate_sb", [P, KC, EXPERTS])
        wrout_sb = sb("wrout_sb", [P, KC, HF])
        big = sb("big", [P, 8 * ROWS])
        wexp = sb("wexp", [P, 2 * EXPW])
        xbuf = sb("xbuf", [P, 2 * D + 2 * D])
        mv = sb("mv", [P, TILES, 2])
        st6 = sb("st6", [P, TILES, 6])
        rstd = sb("rstd", [P, TILES])
        moe_tab = sb("moe_tab", [1, 2, SLOT_TILES], i32)
        end_tab = sb("end_tab", [1, EXPERTS], i32)
        slot = sb("slot", [P, 2, TILES], i32)
        gates = sb("gates", [P, 2, TILES])
        work = sb("work", [P, 10112])

        def f32r(x):
            return x.bitcast(mybir.dt.float32r)

        sems = {}

        def S(name):
            if name not in sems:
                sems[name] = ctx.enter_context(nc.semaphore(name))
            return sems[name]

        def view(base, at, *shape):
            n = 1
            for x in shape:
                n *= x
            v = base[:, at:at + n]
            if len(shape) == 1:
                return v
            names = "abcd"[:len(shape)]
            return v.rearrange(f"p ({' '.join(names)}) -> p {' '.join(names)}", **dict(zip(names, shape)))

        xn = view(xbuf, 0, 2, D)
        xT = view(xbuf, 2 * D, 2, KC, P)
        wqkv_sb = view(wqkv, 0, KC, 3 * INNER)
        wqkv1_sb = view(wqkv, 0, KC, 3 * D)
        wo1_sb = view(wqkv, KC * 3 * D, KC, D)
        wtok_sb = view(big, 0, PK, D)
        pt = view(work, 0, 2, PK, P)
        posb = view(work, 1536, D)
        h0s = view(work, 1792, 2, D)
        xTh = view(over("xT_high", "xbuf", 2 * D, 2 * D), 0, 2, KC, P)
        x0Tl = view(over("x0T_low", "work", 4400, 2 * D), 0, 2, KC, P)
        w0high = view(over("w0_high", "wexp", 0, KC * 3 * INNER), 0, KC, 3 * INNER)
        w0low = view(over("w0_low", "wexp", KC * 3 * INNER, KC * 3 * INNER), 0, KC, 3 * INNER)
        qkT = view(big, 0, 8, ROWS)
        vst = view(work, 0, 2, H0, V0)
        sq = view(work, 1040, 1024)
        qkn = view(work, 2064, 2, 1024)
        ssum = view(work, 4112, 2, 16)
        snorm = view(work, 4144, 2, 16)
        qz = view(work, 0, 2, 4, 2, SEQ)
        kz = view(work, 2256, 2, 4, P)
        kblk0 = view(work, 3280, 2, 4, RQ)
        vm = view(work, 4112, 2, H0, V0)
        vraw0 = view(work, 5152, 2, H0, V0)
        vdiag0 = view(work, 6192, 2, H0, V0)
        pm = view(work, 7232, 2, H0, SEQ)
        pr = view(work, 9488, 2, SEQ)
        aom = view(xbuf, 0, 2, H0, DH0)
        aor = view(wqkv, 2048, 2, H0, DH0)
        rsum = view(work, 9770, 2, 2, H0)

        aT_in = view(work, 0, 2, INNER)
        aT = view(work, 1024, 2, 4, P)
        xn2 = view(big, 0, TILES, D)
        E8 = TILES * EXPERTS
        lg = view(work, 2048, TILES, EXPERTS)
        oh = view(work, 2048 + E8, 2, TILES, EXPERTS)
        t8 = view(work, 2048 + 3 * E8, TILES, EXPERTS)
        u8 = view(work, 2048 + 4 * E8, TILES, EXPERTS)
        mask = view(work, 2048 + 5 * E8, TILES, EXPERTS)
        ca = view(work, 2048 + 6 * E8, TILES, EXPERTS)
        cb = view(work, 2048 + 7 * E8, TILES, EXPERTS)
        rank = view(work, 2048 + 8 * E8, TILES, EXPERTS)
        RB = 2048 + 9 * E8
        r18 = view(work, RB, TILES)
        s18 = view(work, RB + 18, TILES)
        val = view(work, RB + 36, 2, TILES)
        cmp = view(work, RB + 72, EXPERTS, TILES)
        nt = view(work, RB + 216, EXPERTS)
        endf = view(work, RB + 224, EXPERTS + 1)
        ej = view(work, RB + 240, SLOT_TILES)
        ej2 = view(work, RB + 284, SLOT_TILES)
        cmpj = view(work, RB + 328, SLOT_TILES, EXPERTS)
        posf = view(work, RB + 680, 2, TILES)

        xsl = view(work, 5120, 2, D)
        xTl = view(over("xT_low", "xbuf", 0, 2 * D), 0, 2, KC, P)
        hidTh = view(over("hidT_high", "work", 7680, 1024), 0, 2, 4, P)
        hidTl = view(over("hidT_low", "work", 0, 1024), 0, 2, 4, P)
        wraw = view(big, 0, EXPW)
        wraw01 = view(big, EXPW, 2 * EXPW)
        whigh = over("w_high", "wexp", 0, 2 * EXPW)
        wlow = over("w_low", "big", EXPW, 2 * EXPW)
        sil = view(work, 5632, 2, 512)
        hid = view(work, 6656, 2, 512)
        yst = view(work, 8704, 2, D)
        yg = view(big, 0, 2, TILES, D)
        h0_img = h0_d[0:IMAGES * SEQ, :].rearrange("(b n) d -> b n d", n=SEQ)
        qkT1 = view(big, 2 * TILES * D, 4, ROWS)
        vst1 = view(work, 0, 2, H1, V1)
        rp = view(work, 544, 2, 3, P)
        ra = view(work, 1312, 2, 2, P)
        rb = view(work, 1824, 2, 2, P)
        qkr = view(work, 2336, 2, 4, P)
        kblk = view(wexp, 0, 2, 2, HG, SEQ)
        vraw = view(wexp, 4512, 2, 2 * HG * V1)
        vdiag = view(wexp, 5056, 2, 2, HG, V1)
        qblk = view(wexp, 5600, 2, 2, RQ)
        wr = view(wexp, 6016, 2, SEQ)
        wrT = view(wexp, 6298, 2, 2, RQ)
        avr = view(wexp, 6714, 2, HG, DH1)
        mr = view(wexp, 6970, 2)
        rr = view(wexp, 6972, 2)
        a1r = view(wexp, 6974, 2, 2, DH1)
        wts = view(big, 0, 2, 2, HG * SEQ)
        UNIT = 4 * SEQ
        FIRST_AT, LAST_AT = (0, UNIT + 4 * REST), (4 * P, UNIT)
        wT = view(big, 4512, 2, H1, P)
        wTr = view(big, 8608, 2, 2, P)
        q1 = view(work, 3360, 2, 2, P)
        v1m = view(work, 3924, 2, H1, V1)
        a1m = view(work, 5012, 2, H1, DH1)
        max1 = view(work, 6036, 2, 4)
        rs1 = view(work, 6052, H1)
        a1T_in = view(work, 6100, 2, D)
        x3 = view(big, 0, TILES, D)
        xg = view(big, TILES * D, TILES, D)
        xgs = view(wexp, 8960, GT, D)
        stg = view(work, 0, GT, 6)
        mvg = view(work, 40, GT, 2)
        rg = view(work, 56, GT)
        lg3 = view(work, 512, TILES, HF)
        pT = view(work, 800, 3 * P)
        uT = view(work, 1184, 3 * P)
        oT = view(work, 1568, 3 * P)
        m3 = view(work, 1952, 3 * GB)
        sel = view(work, 1980, TILES, HF)
        selb = view(work, 2268, 2, GB, HF)
        sel_all = view(work, 2524, TILES, P)
        hgT = view(big, 2 * TILES * D, KC, HF, POS)
        x3T = view(work, 4828, 2, KC, P)
        wf = view(wexp, 0, 2, KC, 3, 2 * DHF)
        wof = view(wexp, 1536, 2, D)
        bf = view(wexp, 2048, PAIRS, 3)
        hgp = view(wexp, 2072, 2, KC, 2, SEQ)
        qf = view(wexp, 3200, SEQ)
        kf = view(wexp, 3341, SEQ)
        vf = view(wexp, 3482, SEQ)
        ef = view(wexp, 3623, SEQ)
        af = view(wexp, 3764, 2, SEQ)
        mf = view(wexp, 4046, 2)
        rf = view(wexp, 4048, 2)
        aofm = view(wexp, 4052, 2, 2, D)
        aofr = view(wexp, 5076, 2, 2, D)
        o1 = view(big, 0, GT, D)
        aofl = view(big, 2 * TILES * D, TILES, D)
        h3b = view(big, 3 * TILES * D, TILES, D)
        sel_s = view(wexp, 7636, 2, P)

        AHEAD = 2
        LASTB = SEQ - (TILES - 1) * GB

        def by_position(rows_d):
            return bass.AP(rows_d.tensor, 0, [[D, POS], [SEQ * D, IMAGES], [1, D]])

        ROWS_X2, ROWS_X1, ROWS_A1, ROWS_X3 = (TILES * n for n in range(1, 5))
        PRODUCT_GATE, PRODUCT_O1, PRODUCT_ROUTER = (TILES * n for n in range(1, 4))
        RESIDUAL_3 = TILES
        ROWS_LD_A1 = 16 * (TILES // 2)
        ROOT_2, ROOT_3, ROOT_4, ROOT_5 = GROUPS, GROUPS + 1, 2 * GROUPS + 1, 3 * GROUPS + 1
        RANKS, PROBS_T, CHOICES = 1, 2, 3
        W0_HIGH, EXP_EXPERTS, W01_HIGH, EXP_HEADS = 1, 2, 2, 5
        DID = {name: n + 1 for n, name in enumerate((
            "v0_ones",
            "w0low_ready",
            "lg_ready",
            "mask_ready",
            "slots_ready",
            "tables_ready",
            "v1_ones",
            "lg3_ready",
            "pr3_ready",
            "oT_ready"))}

        block = ctx.enter_context(nc.Block())

        @block.sync
        def _(sp):
            sp.dma_start(wtok_sb, w_tok).then_inc(S("wtok_ld"), 16)
            sp.dma_start(posb, pos_table).then_inc(S("tables_ld"), 16)
            sp.dma_start(rowv[:, :, :], row_vectors).then_inc(S("tables_ld"), 16)
            with sp.Fori(0, IMAGES // 4) as i:
                for s in range(2):
                    t = 2 * i + s
                    sp.wait_ge(S("tok_ps"), t + 1)
                    sp.dma_start(pt[:, s, :, :], patches[ds(t, 1), :, :, :].rearrange("o p k n -> p (o k) n")).then_inc(S(f"pt_ld{s}"), 16)
            sp.wait_ge(S("h0_st"), 32)
            for s in range(2):
                sp.wait_ge(S(f"tok_st{s}"), 32 * (IMAGES // 4 + 1))
            for g in range(GROUPS):
                sp.dma_start(h[:, g * GT:(g + 1) * GT, :], h0_d[g * GT * P:(g + 1) * GT * P, :].rearrange("(t p) d -> p t d", p=P)).then_inc(S(f"h_ld{g}"), 16)
            sp.dma_start(wo_sb[:, :, :], w_o0).then_inc(S("weights_ld"), 16)
            sp.dma_start(wgate_sb[:, :, :], w_gate).then_inc(S("weights_ld"), 16)
            sp.dma_start(wrout_sb[:, :, :], w_router).then_inc(S("weights_ld"), 16)
            sp.dma_start(xs_d.rearrange("(t p) d -> p t d", p=P), zeros[:, :].unsqueeze(1).to_broadcast([P, SLOT_TILES, D])).then_inc(S("zero_st"), 16)
            sp.dma_start(aof_d[SEQ * HF:POS * HF, :], zeros[0:(POS - SEQ) * HF, :]).then_inc(S("zero_st"), 16)
            with sp.Fori(0, TILES // 2) as i:
                for s in range(2):
                    t = 2 * i + s
                    sp.wait_ge(S("v0_ready"), t + 2)
                    sp.dma_start(v0_d[ds(t * P, P), :], vst[:, s, :, :].rearrange("p h v -> p (h v)")).then_inc(S(f"v0_st{s}"), 16)
            for s in range(2):
                sp.wait_ge(S(f"v0_st{s}"), 16 * (TILES // 2 + 1))
            sp.wait_ge(S("qkv_ps"), TILES)
            sp.dma_start(wqkv1_sb, w_qkv1).then_inc(S("weights1_ld"), 16)
            sp.dma_start(wo1_sb, w_o1).then_inc(S("weights1_ld"), 16)
            sp.wait_ge(S("qkT_ready"), 2 * TILES + 2)
            sp.wait_ge(S("vraw0_zero"), 1)
            with sp.Fori(0, IMAGES // 2) as i:
                for s in range(2):
                    b = 2 * i + s
                    sp.wait_ge(S("pv0_ps"), 2 * b + 2)
                    sp.dma_start(vm[:, s, :, :], v0_d[ds(b * SEQ, P), :].rearrange("p (h v) -> p h v", h=H0)).then_inc(S(f"v0_ld{s}"), 16)
                    sp.dma_start(vraw0[0:RQ, s, :, :].rearrange("p h v -> p (h v)"), v0_d[ds(b * SEQ + P, REST), :].unsqueeze(0).to_broadcast([H0, REST, H0 * V0])).then_inc(S(f"v0_ld{s}"), 16)
            for s in range(2):
                sp.wait_ge(S(f"ao0_st{s}"), 32 * (IMAGES // 2 + 1))
            sp.wait_ge(S("ao0_pad"), 32)
            with sp.Fori(0, TILES // 2) as i:
                for s in range(2):
                    t = 2 * i + s
                    sp.wait_ge(S("rowsT_ps"), t + 1)
                    sp.dma_start(aT_in[:, s, :], ao0_d[ds(t * P, P), :]).then_inc(S(f"aT_ld{s}"), 16)
            sp.wait_ge(S("xs_st"), 16 * 2 * TILES)
            with sp.Fori(0, SLOT_TILES // 2) as i:
                for s in range(2):
                    j = 2 * i + s
                    sp.wait_ge(S("xsT_ps"), j + 1)
                    sp.dma_start(xsl[:, s, :], xs_d[ds(j * P, P), :]).then_inc(S(f"xsl_ld{s}"), 16)
            with sp.Fori(0, TILES // 2) as i:
                for s in range(2):
                    t = 2 * i + s
                    sp.wait_ge(S("qkr_ready"), t + 1)
                    sp.dma_start(rp[:, s, :, :], rope[:, ds(t, 1), :, :].rearrange("p o k n -> p (o k) n")).then_inc(S(f"rp_ld{s}"), 16)
            for s in range(2):
                sp.wait_ge(S(f"v1_st{s}"), 16 * (TILES // 2 + 1))
            sp.wait_ge(S("vraw_zero"), 1)
            with sp.Fori(0, IMAGES // 2) as i:
                for s in range(2):
                    b = 2 * i + s
                    sp.wait_ge(S("pv1_ps"), b + 1)
                    sp.dma_start(v1m[:, s, :, :], v1_d[ds(b * SEQ, P), :].rearrange("p (h v) -> p h v", h=H1)).then_inc(S(f"v1_ld{s}"), 16)
                    sp.dma_start(vraw[0:RQ, s, :], v1_d[ds(b * SEQ + P, REST), :].unsqueeze(0).to_broadcast([HG, REST, H1 * V1])).then_inc(S(f"v1_ld{s}"), 16)
            for s in range(2):
                sp.wait_ge(S(f"a1_st{s}"), 16 * (IMAGES // 2 + 1))
                sp.wait_ge(S(f"a1r_st{s}"), 32 * (IMAGES // 2 + 1))
            sp.wait_ge(S("a1_pad"), 16)
            with sp.Fori(0, TILES // 2) as i:
                for s in range(2):
                    t = 2 * i + s
                    sp.wait_ge(S("rowsT_ps"), ROWS_A1 + t + 1)
                    sp.dma_start(a1T_in[:, s, :], ao1_d[ds(t * P, P), :]).then_inc(S(f"aT_ld{s}"), 16)
            with sp.Fori(0, GROUPS) as g:
                sp.wait_ge(S("x3_ready"), g + 1)
                sp.dma_start(x3_d[ds(g * GT * P, GT * P), :].rearrange("(t p) d -> p t d", p=P), x3[:, ds(g * GT, GT), :]).then_inc(S("x3_st"), 16)
            sp.wait_ge(S("x3_st"), 16 * GROUPS)
            for r in range(2):
                sp.sem_inc(S(f"xg_ld{r}"), 16 * HT)

            def load_rows(rows, rows_d, t, loaded):
                for n in range(HT):
                    sp.dma_start(rows[:, ds(t + n, 1), :].rearrange("p o d -> p (o d)"), by_position(rows_d)[ds((t + n) * GB, GB), :, :]).then_inc(loaded, 16)

            with sp.Fori(0, GROUPS) as g:
                for r in range(2):
                    sp.wait_ge(S(f"xg_ld{r}"), 16 * HT * (g + 1))
                    sp.sem_inc(S("passed"), 1)
                    load_rows(xg, x3_d, g * GT + r * HT, S(f"xg_ld{r}"))
            sp.wait_ge(S("h3_st"), 16)
            with sp.Fori(0, GROUPS) as g:
                for r in range(2):
                    load_rows(h3b, h3_d, g * GT + r * HT, S("h3b_ld"))
            sp.dma_start(bf, b_qkvf.rearrange("p (a b) -> p a b", a=PAIRS)).then_inc(S("bf_ld"), 16)
            def load_pair(i, s):
                p_ = 2 * i + s
                sp.wait_ge(S("qkvf_ps"), p_ + 1)
                sp.dma_start(wf[:, s, :, :, :].rearrange("p k x n -> p (k x n)"), w_qkvf[ds(p_, 1), :, :].rearrange("o p n -> p (o n)")).then_inc(S(f"wf_ld{s}"), 16)
                sp.wait_ge(S("aof_ps"), 2 * p_ + 2)
                sp.dma_start(wof[:, s, :], w_of[ds(p_, 1), :, :].rearrange("o p n -> p (o n)")).then_inc(S(f"wof_ld{s}"), 16)

            with sp.Fori(0, PAIRS // 2) as i:
                for s in range(2):
                    load_pair(i, s)
            for s in range(2):
                sp.wait_ge(S(f"aof_st{s}"), 32 * (PAIRS // 2 + 1))
            sp.wait_ge(S("zero_st"), 32)
            for r in range(2):
                sp.sem_inc(S(f"aofl_ld{r}"), 16)
            with sp.Fori(0, GROUPS) as g:
                for r in range(2):
                    sp.wait_ge(S(f"aofl_ld{r}"), 16 * (g + 1))
                    sp.dma_start(aofl[:, ds(g * GT + r * HT, HT), :],
                                 aof_d[ds((g * GT + r * HT) * P, HT * P), :].rearrange("(n p) d -> p n d", p=P)).then_inc(S(f"aofl_ld{r}"), 16)

        @block.gpsimd
        def _(pool):
            nc.gpsimd.memset(zeros[:, :], 0.0).then_inc(S("fills"), 1)
            nc.gpsimd.memset(ones[:, :], 1.0).then_inc(S("fills"), 1)
            nc.gpsimd.memset(minus16[:, :], -16.0).then_inc(S("fills"), 1)
            for s in range(2):
                pool.wait_ge(S(f"v0_st{s}"), 16 * (TILES // 2 + 1))
            pool.wait_ge(S("qkT_ready"), 2 * TILES + 2)
            nc.gpsimd.memset(vraw0.rearrange("p s h v -> p (s h v)"), 0.0).then_inc(S("vraw0_zero"), 1)
            with pool.Fori(0, IMAGES // 2) as i:
                for s in range(2):
                    b = 2 * i + s
                    pool.wait_ge(S("s0_ps"), 2 * b + 2)
                    for r in range(2):
                        m = nc.gpsimd.tensor_tensor(qz[:, s, :, r, :], qkT[:, 0:4, ds(b * SEQ, SEQ)],
                                                    blockones[:, 64 * r:64 * r + 1].unsqueeze(2).to_broadcast([P, 4, SEQ]), ALU.mult)
                    m.then_inc(S("qks_ready"), 1)
                    nc.gpsimd.tensor_tensor(kblk0[:, s, :, :].rearrange("p c (h k) -> p c h k", h=H0),
                                            qkT[:, 4:8, ds(b * SEQ + P, REST)].unsqueeze(2).to_broadcast([P, 4, H0, REST]),
                                            chunkmask.rearrange("p (c h) -> p c h", c=4).unsqueeze(3).to_broadcast([P, 4, H0, REST]), ALU.mult).then_inc(S("qks_ready"), 1)
                    pool.wait_ge(S(f"v0_ld{s}"), 32 * (i + 1))
                    pool.wait_ge(S("pv0_ps"), 2 * b + 2)
                    nc.gpsimd.tensor_tensor(vdiag0[:, s, :, :], vraw0[:, s, :, :], restmask.unsqueeze(2).to_broadcast([P, H0, V0]), ALU.mult).then_inc(S("vdiag0_ready"), 1)
            pool.wait_ge(S("rowsT_ps"), TILES + 2)
            for e in range(2):
                load_expert(nc, S, wraw01[:, e * EXPW:(e + 1) * EXPW], w_gu, w_down, e)
            pool.sem_inc(S("xn2_kept"), 2)
            pool.wait_ge(S("vdiag0_ready"), IMAGES)
            with pool.Fori(0, TILES // 2) as i:
                for s in range(2):
                    t = 2 * i + s
                    pool.wait_ge(S("xn2_ready"), t + 1)
                    nc.gpsimd.tensor_copy(xn2[:, t, :], xn[:, s, :]).then_inc(S("xn2_kept"), 1)
            pool.wait_ge(S("dve_did"), DID["slots_ready"])
            pool.wait_ge(S("xn2_kept"), TILES + 2)
            pool.wait_ge(S("zero_st"), 32)
            for k in range(2):
                for t in range(TILES):
                    nc.gpsimd.indirect_dma_start(xs_d, bass.IndirectOffsetOnAxis(slot[:, k, t:t + 1], 0), xn2[:, t, :], None).then_inc(S("xs_st"), 16)
            pool.wait_ge(S("split_ready"), 2)
            pool.sem_inc(S("wexp_ready"), 2)
            pool.wait_ge(S("xs_st"), 16 * 2 * TILES)
            load_expert(nc, S, wraw, w_gu, w_down, 2)
            for e in range(2, EXPERTS):
                at = (e % 2) * EXPW
                pool.wait_ge(S("wexp_ld"), 32 * (e + 1))
                done = pool.value_load(end_tab[0:1, e - 2:e - 1], min_val=2, max_val=2 * SLOT_TILES + 2)
                pool.wait_ge(S("dn_ps"), done)
                pool.sem_inc(S("passed"), 1)
                nc.gpsimd.tensor_tensor(f32r(whigh[:, at:at + EXPW]), wraw, ones[:, 0:1].to_broadcast([P, EXPW]), ALU.mult).then_inc(S("split_hi"), 1)
                pool.wait_ge(S("split_hi"), e - 1)
                nc.gpsimd.tensor_tensor(f32r(wlow[:, at:at + EXPW]), wraw, whigh[:, at:at + EXPW], ALU.subtract).then_inc(S("wexp_ready"), 1)
                if e + 1 < EXPERTS:
                    pool.wait_ge(S("wexp_ready"), e + 1)
                    load_expert(nc, S, wraw, w_gu, w_down, e + 1)
            pool.wait_ge(S("xs_st"), 16 * 2 * TILES)
            for s in range(2):
                pool.wait_ge(S(f"ys_st{s}"), 16 * (SLOT_TILES // 2 + 1))
            for t in range(TILES):
                for k in range(2):
                    nc.gpsimd.indirect_dma_start(yg[:, k, t, :], None, ys_d, bass.IndirectOffsetOnAxis(slot[:, k, t:t + 1], 0)).then_inc(S(f"yg_ld{t // GT}"), 16)
            pool.wait_ge(S("qkT1_ready"), 5)
            nc.gpsimd.memset(vraw, 0.0).then_inc(S("vraw_zero"), 1)
            with pool.Fori(0, IMAGES // 2) as i:
                for s in range(2):
                    b = 2 * i + s
                    pool.wait_ge(S("qkT1_ready"), b + 5)
                    pool.wait_ge(S("sr_ps"), b + 1)
                    nc.gpsimd.tensor_copy(q1[:, s, :, :], qkT1[:, 0:2, ds(b * SEQ, P)])
                    for g in range(2):
                        nc.gpsimd.tensor_tensor(kblk[:, s, g, :, :], qkT1[:, 2 + g, ds(b * SEQ, SEQ)].unsqueeze(1).to_broadcast([P, HG, SEQ]),
                                                headmask.unsqueeze(2).to_broadcast([P, HG, SEQ]), ALU.mult)
                    for g in range(2):
                        m = nc.gpsimd.tensor_tensor(qblk[:, s, g, :].rearrange("p (h i) -> p h i", h=HG),
                                                    qkT1[:, g, ds(b * SEQ + P, REST)].unsqueeze(1).to_broadcast([P, HG, REST]),
                                                    headmask.unsqueeze(2).to_broadcast([P, HG, REST]), ALU.mult)
                    m.then_inc(S("q1_ready"), 1)
                    pool.wait_ge(S(f"v1_ld{s}"), 32 * (i + 1))
                    pool.wait_ge(S("pv1_ps"), b + 1)
                    nc.gpsimd.tensor_tensor(vdiag[:, s, :, :, :], vraw[:, s, :].rearrange("p (g h v) -> p g h v", g=2, h=HG),
                                            restmask.unsqueeze(1).unsqueeze(3).to_broadcast([P, 2, HG, V1]), ALU.mult).then_inc(S("vdiag_ready"), 1)
            pool.wait_ge(S("xn1_ready"), TILES)
            nc.gpsimd.tensor_tensor(h[:, :, :], h[:, :, :], rowv[:, 1, :].unsqueeze(1).to_broadcast([P, TILES, D]), ALU.add).then_inc(S("h_bias"), 1)
            with pool.Fori(0, GROUPS) as g:
                pool.wait_ge(S("x3_ready"), g + 1)
                nc.gpsimd.tensor_tensor(h[:, ds(g * GT, GT), :], h[:, ds(g * GT, GT), :], rowv[:, 4, :].unsqueeze(1).to_broadcast([P, GT, D]), ALU.add).then_inc(S("h3_ready"), 1)
            pool.wait_ge(S("rowsT_ps"), ROWS_X3 + TILES + 2)
            with pool.Fori(0, GROUPS) as g:
                for n in range(GT):
                    t = g * GT + n
                    pool.wait_ge(S("hg_ps"), t + 1)
                    nc.gpsimd.tensor_copy(xgs[:, n, :], xg[:, t, :]).then_inc(S("xgs_ready"), 1)
            pool.wait_ge(S("hgT_ready"), 2 * TILES + 4)
            with pool.Fori(0, PAIRS // 2) as i:
                for s in range(2):
                    p_ = 2 * i + s
                    pool.wait_ge(S("qkvf_ps"), p_ + 1)
                    nc.gpsimd.tensor_copy(hgp[:, s, :, :, :], hgT[:, :, ds(2 * p_, 2), 0:SEQ]).then_inc(S("hgp_ready"), 1)
            with pool.Fori(0, TILES // 2) as i:
                for s in range(2):
                    t = 2 * i + s
                    pool.wait_ge(S("yf_ps"), t + 1)
                    nc.gpsimd.tensor_copy(sel_s[:, s, :], sel_all[:, t, :]).then_inc(S("sel_ready"), 1)
        @block.scalar
        def _(act):
            act.wait_ge(S("pt_ld1"), 16)
            act.dma_start(h0_img[:, PATCHES:SEQ, :], txt).then_inc(S("h0_st"), 16)
            act.wait_ge(S("fills"), 3)
            act.dma_start(h0_d[IMAGES * SEQ:ROWS, :], zeros[0:ROWS - IMAGES * SEQ, :]).then_inc(S("h0_st"), 16)
            act.dma_start(const[:, :], constants).then_inc(S("w0_ld"), 16)
            act.dma_start(wqkv_sb, w_qkv0).then_inc(S("w0_ld"), 16)
            for s in range(2):
                act.sem_inc(S(f"tok_st{s}"), 32)
            with act.Fori(0, IMAGES // 4) as i:
                for s in range(2):
                    t = 2 * i + s
                    act.wait_ge(S("tok_ready"), t + 3)
                    for r in range(2):
                        act.dma_start(h0_img[ds(2 * t + r, 1), 0:PATCHES, :].rearrange("o n d -> (o n) d"),
                                      h0s[64 * r:64 * r + 64, s, :]).then_inc(S(f"tok_st{s}"), 16)
            act.sem_inc(S("xT_ready"), 2)
            act.sem_inc(S("qkT_ready"), 2)
            act.sem_inc(S("v0_ready"), 1)
            for s in range(2):
                act.sem_inc(S(f"v0_st{s}"), 16)
            act.wait_ge(S("w0_ld"), 32)
            nc.scalar.activation(f32r(w0high), wqkv_sb, ACT.Copy).then_inc(S("act_did"), 1)

            def root0(g):
                act.wait_ge(S("ln_stats"), g + 1)
                nc.scalar.activation(rstd[:, g * GT:(g + 1) * GT], mv[:, g * GT:(g + 1) * GT, 1], ACT.Sqrt).then_inc(S("ln_root"), 1)

            root0(0)

            def keep_qkT(t):
                for a in range(2):
                    act.wait_ge(S("qkT_ps"), 2 * t + a + 5)
                    nc.scalar.activation(qkT[:, 4 * a:4 * a + 4, ds(t * P, P)],
                                         psum[:, 6 + a, :].rearrange("p (k n) -> p k n", k=4), ACT.Copy).then_inc(S("qkT_ready"), 1)

            def keep_xT(t, s):
                act.wait_ge(S("xT_ps"), t + 1)
                nc.scalar.activation(f32r(xTh[:, s, :, :]), psum[:, 5, 0:D].rearrange("p (k n) -> p k n", k=KC), ACT.Copy).then_inc(S("xT_ready"), 1)

            def qkv_step(t, s, i, first=False, last=False):
                if not last:
                    keep_xT(t + 1, 1 - s)
                act.wait_ge(S("qkv_ps"), t + 1)
                act.wait_ge(S(f"v0_st{s}"), 16 * (i + 1))
                act.wait_ge(S("dve_did"), DID["v0_ones"])
                nc.scalar.activation(vst[:, s, :, 0:DH0], psum[:, 4, :].rearrange("p (h v) -> p h v", h=H0), ACT.Copy).then_inc(S("v0_ready"), 1)
                if not first:
                    act.wait_ge(S("ssum_ready"), t)
                nc.scalar.activation(sq.rearrange("p (a n) -> p a n", a=2), psum[:, 2 * s:2 * s + 2, :], ACT.Square).then_inc(S("sq_ready"), 1)
                if not first:
                    keep_qkT(t - 1)
                act.wait_ge(S("ssum_ready"), t + 1)
                nc.scalar.activation(snorm[:, s, :], ssum[:, s, :], ACT.Sqrt).then_inc(S("snorm_ready"), 1)

            keep_xT(0, 0)
            qkv_step(0, 0, 0, first=True)
            qkv_step(1, 1, 0)
            root0(1)
            qkv_step(2, 0, 1)
            qkv_step(3, 1, 1)
            root0(2)
            qkv_step(4, 0, 2)
            with act.Fori(2, TILES // 2 - 1) as i:
                qkv_step(2 * i + 1, 1, i)
                qkv_step(2 * i + 2, 0, i + 1)
            qkv_step(TILES - 1, 1, TILES // 2 - 1, last=True)
            keep_qkT(TILES - 1)
            for s in range(2):
                act.sem_inc(S(f"ao0_st{s}"), 32)

            act.sem_inc(S("p0_ready"), 2)

            def exp0(b, s):
                act.wait_ge(S("pv0_ps"), 2 * b + 2)
                for u in range(2):
                    act.wait_ge(S("s0_ps"), 2 * b + u + 5)
                    m = nc.scalar.activation(pm[:, s, 4 * u:4 * u + 4, :].rearrange("p (a c) i -> p a (c i)", c=2),
                                             psum[:, 2 * u:2 * u + 2, 0:2 * SEQ], ACT.Exp, bias=minus16[:, :], scale=16.0)
                    if u:
                        m = nc.scalar.activation(pr[0:RQ, s, :], psum[0:RQ, 3, 2 * SEQ:3 * SEQ], ACT.Exp, bias=minus16[0:RQ, :], scale=16.0)
                    m.then_inc(S("p0_ready"), 1)

            def store_ao0(b, s):
                act.wait_ge(S("ao0_ready"), 2 * b + 4)
                act.dma_start(ao0_d[ds(b * SEQ, P), :], aom[:, s, :, :].rearrange("p h v -> p (h v)")).then_inc(S(f"ao0_st{s}"), 16)
                act.dma_start(ao0_d[ds(b * SEQ + P, REST), :], aor[0:REST, s, :, :].rearrange("p h v -> p (h v)")).then_inc(S(f"ao0_st{s}"), 16)

            act.dma_start(ao0_d[IMAGES * SEQ:ROWS, 0:D], zeros[0:ROWS - IMAGES * SEQ, :]).then_inc(S("ao0_pad"), 16)
            act.dma_start(ao0_d[IMAGES * SEQ:ROWS, D:INNER], zeros[0:ROWS - IMAGES * SEQ, :]).then_inc(S("ao0_pad"), 16)
            act.wait_ge(S("fills"), 3)
            exp0(0, 0)
            with act.Fori(0, IMAGES // 2 - 1) as i:
                for s in range(2):
                    exp0(2 * i + s + 1, 1 - s)
                    store_ao0(2 * i + s, s)
            exp0(IMAGES - 1, 1)
            store_ao0(IMAGES - 2, 0)
            store_ao0(IMAGES - 1, 1)
            act.sem_inc(S("rowsT_ready"), 2)

            def keep_aT(t, s):
                act.wait_ge(S("rowsT_ps"), t + 3)
                act.wait_ge(S("product_ps"), t + 1)
                nc.scalar.activation(aT[:, s, :, :], psum[:, s, :].rearrange("p (k n) -> p k n", k=4), ACT.Copy).then_inc(S("rowsT_ready"), 1)

            with act.Fori(0, TILES // 2) as i:
                for s in range(2):
                    keep_aT(2 * i + s, s)
            act.wait_ge(S("ln_stats"), ROOT_2 + 1)
            nc.scalar.activation(rstd[:, :], mv[:, :, 1], ACT.Sqrt).then_inc(S("ln_root"), 1)
            with act.Fori(0, TILES // 2) as i:
                for s in range(2):
                    t = 2 * i + s
                    act.wait_ge(S("rowsT_ps"), ROWS_X2 + t + 3)
                    act.wait_ge(S("product_ps"), PRODUCT_GATE + t + 1)
                    nc.scalar.activation(xT[:, s, :, :], psum[:, 4 + s, 0:D].rearrange("p (k n) -> p k n", k=KC), ACT.Copy).then_inc(S("rowsT_ready"), 1)
            act.wait_ge(S("dve_did"), DID["lg_ready"])
            nc.scalar.activation(lg, lg, ACT.Exp).then_inc(S("act_did"), 1)
            act.wait_ge(S("wexp_ld"), 64)
            for e in range(2):
                nc.scalar.activation(f32r(whigh[:, e * EXPW:(e + 1) * EXPW]), wraw01[:, e * EXPW:(e + 1) * EXPW], ACT.Copy).then_inc(S("act_did"), 1)
            act.sem_inc(S("xsT_ready"), 2)
            act.sem_inc(S("sil_ready"), 2)
            act.sem_inc(S("y_ready"), 2)
            for s in range(2):
                act.sem_inc(S(f"ys_st{s}"), 16)

            def keep_xsT(j, s):
                act.wait_ge(S("xsT_ps"), j + 3)
                nc.scalar.activation(f32r(xTh[:, s, :, :]), psum[:, 6, 0:D].rearrange("p (k n) -> p k n", k=KC), ACT.Copy).then_inc(S("xsT_ready"), 1)

            def silu(n, s):
                act.wait_ge(S("gu_ps"), n + 1)
                act.wait_ge(S("hid_ready"), n + 1)
                nc.scalar.activation(sil[:, s, :], psum[:, 2 * s, :], ACT.Silu).then_inc(S("sil_ready"), 1)

            def keep_y(j, s, i):
                act.wait_ge(S("dn_ps"), 2 * j + 4)
                act.wait_ge(S(f"ys_st{s}"), 16 * (i + 1))
                nc.scalar.activation(yst[:, s, :], psum[:, 7, 0:D], ACT.Copy).then_inc(S("y_ready"), 1)
                act.wait_ge(S("y_ready"), j + 3)
                act.dma_start(ys_d[ds(j * P, P), :], yst[:, s, :]).then_inc(S(f"ys_st{s}"), 16)

            keep_xsT(0, 0)
            keep_xsT(1, 1)
            silu(0, 0)
            silu(1, 1)
            with act.Fori(0, SLOT_TILES // 2 - 1) as i:
                silu(4 * i + 2, 0)
                keep_xsT(2 * i + 2, 0)
                silu(4 * i + 3, 1)
                keep_y(2 * i, 0, i)
                silu(4 * i + 4, 0)
                keep_xsT(2 * i + 3, 1)
                silu(4 * i + 5, 1)
                keep_y(2 * i + 1, 1, i)
            silu(2 * SLOT_TILES - 2, 0)
            silu(2 * SLOT_TILES - 1, 1)
            keep_y(SLOT_TILES - 2, 0, SLOT_TILES // 2 - 1)
            keep_y(SLOT_TILES - 1, 1, SLOT_TILES // 2 - 1)
            for s in range(2):
                act.sem_inc(S(f"v1_st{s}"), 16)
            act.sem_inc(S("qkT1_ready"), 2)
            act.sem_inc(S("v1_ready"), 2)

            def root1(g):
                act.wait_ge(S("ln_stats"), ROOT_3 + g + 1)
                nc.scalar.activation(rstd[:, ds(g * GT, GT)], mv[:, ds(g * GT, GT), 1], ACT.Sqrt).then_inc(S("ln_root"), 1)

            def keep_qkT1(t):
                act.wait_ge(S("qkT1_ps"), t + 3)
                nc.scalar.activation(qkT1[:, :, ds(t * P, P)], psum[:, 6, :].rearrange("p (k n) -> p k n", k=4), ACT.Copy).then_inc(S("qkT1_ready"), 1)

            def keep_x1T(t, s):
                act.wait_ge(S("rowsT_ps"), ROWS_X1 + t + 3)
                nc.scalar.activation(xT[:, s, :, :], psum[:, 5, 0:D].rearrange("p (k n) -> p k n", k=KC), ACT.Copy).then_inc(S("rowsT_ready"), 1)

            def qkv1_step(t, s, i, first=False, last=False):
                act.wait_ge(S("qkv1_ps"), t + 1)
                if not last:
                    keep_x1T(t + 1, 1 - s)
                act.wait_ge(S(f"v1_st{s}"), 16 * (i + 1))
                act.wait_ge(S("dve_did"), DID["v1_ones"])
                nc.scalar.activation(vst1[:, s, :, 0:DH1], psum[:, 2 * s + 1, 0:D].rearrange("p (h v) -> p h v", h=H1), ACT.Copy).then_inc(S("v1_ready"), 1)
                act.wait_ge(S("v1_ready"), t + 3)
                act.dma_start(v1_d[ds(t * P, P), :], vst1[:, s, :, :].rearrange("p h v -> p (h v)")).then_inc(S(f"v1_st{s}"), 16)
                if not first:
                    keep_qkT1(t - 1)

            root1(0)
            keep_x1T(0, 0)
            for n in range(GT - 1):
                qkv1_step(n, n % 2, n // 2, first=(n == 0))
            with act.Fori(0, GROUPS - 1) as g:
                root1(g + 1)
                for n in range(GT - 1, 2 * GT - 1):
                    qkv1_step(g * GT + n, n % 2, g * HT + n // 2)
            qkv1_step(TILES - 1, 1, TILES // 2 - 1, last=True)
            keep_qkT1(TILES - 1)
            for s in range(2):
                act.sem_inc(S(f"a1_st{s}"), 16)
                act.sem_inc(S(f"a1r_st{s}"), 32)
            act.sem_inc(S("wT_ready"), 2)
            act.dma_start(ao1_d[IMAGES * SEQ:ROWS, :], zeros[0:ROWS - IMAGES * SEQ, :]).then_inc(S("a1_pad"), 16)

            def exp1(b, s, u):
                act.wait_ge(S("s1_read"), 4 * b + u + 3)
                w = wts[:, s, u // 2, (u % 2) * UNIT:(u % 2 + 1) * UNIT]
                nc.scalar.activation(w, w, ACT.Exp, scale=DH1 ** -0.5).then_inc(S("p1_ready"), 1)

            def keep_wT(b, s, n):
                act.wait_ge(S("wT_ps"), 5 * b + n + 1)
                if n < 4:
                    m = nc.scalar.activation(wT[:, s, 4 * n:4 * n + 4, :], psum[:, 4 + (5 * s + n) % 2, :].rearrange("p (h i) -> p h i", h=4), ACT.Copy)
                else:
                    m = nc.scalar.activation(wTr[0:RQ, s, :, :], psum[0:RQ, 4 + (5 * s + n) % 2, 0:2 * P].rearrange("p (g i) -> p g i", g=2), ACT.Copy)
                m.then_inc(S("wT_ready"), 1)

            def exp_rest(b):
                act.wait_ge(S("mr_ready"), b + 1)
                for g in range(2):
                    m = nc.scalar.activation(wr[0:RQ, g, :], psum[0:RQ, 7, g * SEQ:(g + 1) * SEQ], ACT.Exp, bias=mr[0:RQ, g:g + 1],
                                             scale=DH1 ** -0.5, accum_out=rr[0:RQ, g:g + 1])
                m.then_inc(S("wr_ready"), 1)

            def keep_wrT(b):
                act.wait_ge(S("wrT_ps"), b + 1)
                for n, rows in enumerate((P, REST)):
                    m = nc.scalar.activation(wrT[0:rows, n, :, :], psum[0:rows, 7, n * 2 * RQ:(n + 1) * 2 * RQ].rearrange("p (g i) -> p g i", g=2), ACT.Copy)
                m.then_inc(S("wrT_ready"), 1)

            def store_main(b, s):
                act.wait_ge(S("a1_ready"), b + 1)
                act.dma_start(ao1_d[ds(b * SEQ, P), :], a1m[:, s, :, :].rearrange("p h v -> p (h v)")).then_inc(S(f"a1_st{s}"), 16)

            def store_rest(b, s):
                act.wait_ge(S("a1r_ready"), b + 2)
                for g in range(2):
                    act.dma_start(ao1_d[ds(b * SEQ + P, REST), g * P:(g + 1) * P].rearrange("q (h d) -> h q d", h=HG), a1r[0:RQ, s, g, :]).then_inc(S(f"a1r_st{s}"), 16)

            def image1_act(b, s, first=False, last=False):
                exp1(b, s, 1)
                keep_wT(b, s, 0)
                if not first:
                    store_rest(b - 1, 1 - s)
                exp1(b, s, 2)
                keep_wT(b, s, 1)
                if not first:
                    store_main(b - 1, 1 - s)
                exp1(b, s, 3)
                exp_rest(b)
                keep_wT(b, s, 2)
                if not last:
                    exp1(b + 1, 1 - s, 0)
                keep_wrT(b)
                keep_wT(b, s, 3)
                keep_wT(b, s, 4)

            exp1(0, 0, 0)
            image1_act(0, 0, first=True)
            with act.Fori(0, IMAGES // 2 - 1) as i:
                image1_act(2 * i + 1, 1)
                image1_act(2 * i + 2, 0)
            image1_act(IMAGES - 1, 1, last=True)
            store_rest(IMAGES - 1, 1)
            store_main(IMAGES - 1, 1)

            def keep_a1T(t, s):
                act.wait_ge(S("rowsT_ps"), ROWS_A1 + t + 3)
                act.wait_ge(S("product_ps"), PRODUCT_O1 + t + 1)
                nc.scalar.activation(xT[:, s, :, :], psum[:, s, 0:D].rearrange("p (k n) -> p k n", k=KC), ACT.Copy).then_inc(S("rowsT_ready"), 1)

            def root4(g):
                act.wait_ge(S("ln_stats"), ROOT_4 + g + 1)
                nc.scalar.activation(rg, mvg[:, :, 1], ACT.Sqrt).then_inc(S("ln_root"), 1)

            for n in range(GT):
                keep_a1T(n, n % 2)
            with act.Fori(1, GROUPS) as g:
                for n in range(GT):
                    if n == AHEAD:
                        root4(g - 1)
                    keep_a1T(g * GT + n, n % 2)
            root4(GROUPS - 1)
            with act.Fori(0, TILES // 2) as i:
                for s in range(2):
                    t = 2 * i + s
                    act.wait_ge(S("rowsT_ps"), ROWS_X3 + t + 3)
                    act.wait_ge(S("product_ps"), PRODUCT_ROUTER + t + 1)
                    nc.scalar.activation(x3T[:, s, :, :], psum[:, s, 0:D].rearrange("p (k n) -> p k n", k=KC), ACT.Copy).then_inc(S("rowsT_ready"), 1)
            act.wait_ge(S("h3_ready"), GROUPS)
            act.dma_start(h3_d.rearrange("(t p) d -> p t d", p=P), h[:, :, :]).then_inc(S("h3_st"), 16)
            act.wait_ge(S("dve_did"), DID["lg3_ready"])
            nc.scalar.activation(lg3, lg3, ACT.Exp).then_inc(S("act_did"), 1)
            act.sem_inc(S("hgT_ready"), 4)
            with act.Fori(0, TILES // 2) as i:
                for s in range(2):
                    t = 2 * i + s
                    act.wait_ge(S("hg_ps"), t + 5)
                    for k in range(KC):
                        nc.scalar.activation(hgT[:, k, :, ds(t * GB, GB)].rearrange("p h b -> p b h"),
                                             psum[:, s, k * P:(k + 1) * P].rearrange("p (b h) -> p b h", b=GB), ACT.Copy).then_inc(S("hgT_ready"), 1)
            for s in range(2):
                act.sem_inc(S(f"aof_st{s}"), 32)
            with act.Fori(0, PAIRS // 2) as i:
                for s in range(2):
                    p_ = 2 * i + s
                    act.wait_ge(S("mf_ready"), p_ + 1)
                    act.wait_ge(S("af_ready"), p_ + 1)
                    nc.scalar.activation(ef, psum[:, 2, 0:SEQ], ACT.Exp, bias=mf[:, s:s + 1], scale=DHF ** -0.5, accum_out=rf[:, s:s + 1]).then_inc(S("ef_ready"), 1)
                    act.wait_ge(S("aof_ready"), 2 * p_ + 4)
                    aof_bh = aof_d.rearrange("(b h) d -> b h d", h=HF)
                    act.dma_start(aof_bh[0:P, ds(2 * p_, 2), :], aofm[:, s, :, :]).then_inc(S(f"aof_st{s}"), 16)
                    act.dma_start(aof_bh[P:SEQ, ds(2 * p_, 2), :], aofr[0:REST, s, :, :]).then_inc(S(f"aof_st{s}"), 16)
            out_bs = out.rearrange("s b d -> b s d")
            for s in range(2):
                act.sem_inc(S(f"out_st{s}"), 16)

            def store_group(g, last=False):
                act.wait_ge(S("ln_stats"), ROOT_5 + g + 1)
                nc.scalar.activation(rg, mvg[:, :, 1], ACT.Sqrt).then_inc(S("ln_root"), 1)
                for n in range(GT):
                    t = g * GT + n
                    act.wait_ge(S("o1_ready"), t + 5)
                    if last and n == GT - 1:
                        act.dma_start(out_bs[SEQ - LASTB:SEQ, :, :], o1[0:LASTB * IMAGES, n, :]).then_inc(S(f"out_st{n % 2}"), 16)
                    else:
                        act.dma_start(out_bs[ds(t * GB, GB), :, :], o1[:, n, :]).then_inc(S(f"out_st{n % 2}"), 16)

            with act.Fori(0, GROUPS - 1) as g:
                store_group(g)
            store_group(GROUPS - 1, last=True)
            for s in range(2):
                act.wait_ge(S(f"out_st{s}"), 16 * (TILES // 2 + 1))

        @block.vector
        def _(dve):
            c = Count()

            def step(ins):
                ins.then_inc(S("dve_step"), 1)
                dve.wait_ge(S("dve_step"), c.next())

            def root_tiles(lo, hi, n):
                for t in range(lo, hi):
                    m = nc.vector.bn_aggr(mv[:, t, :], st6[:, t, :])
                step(m)
                step(nc.vector.tensor_scalar(mv[:, lo:hi, 1], mv[:, lo:hi, 1], 1e-5, None, ALU.add))
                dve.sem_inc(S("ln_stats"), 1)
                dve.wait_ge(S("ln_root"), n)
                step(nc.vector.reciprocal(rstd[:, lo:hi], rstd[:, lo:hi]))

            def normed(out_, t):
                return nc.vector.tensor_scalar(out_, h[:, t, :], mv[:, t, 0:1], rstd[:, ds(t, 1)], ALU.subtract, ALU.mult)

            dve.wait_ge(S("tables_ld"), 32)
            step(nc.vector.tensor_tensor(posb, posb, rowv[:, 0, :], ALU.add))
            dve.sem_inc(S("tok_ready"), 2)
            with dve.Fori(0, IMAGES // 4) as i:
                for s in range(2):
                    t = 2 * i + s
                    dve.wait_ge(S("tok_ps"), t + 3)
                    dve.wait_ge(S(f"tok_st{s}"), 32 * (i + 1))
                    nc.vector.tensor_tensor(h0s[:, s, :], psum[:, s, 0:D], posb, ALU.add).then_inc(S("tok_ready"), 1)
            for s in range(2):
                dve.wait_ge(S(f"tok_st{s}"), 32 * (IMAGES // 4 + 1))
                m = nc.vector.memset(vst[:, s, :, DH0:V0], 1.0)
            step(m)
            dve.sem_inc(S("dve_did"), 1)
            dve.wait_ge(S("act_did"), W0_HIGH)
            step(nc.vector.tensor_tensor(f32r(w0low), wqkv_sb, w0high, ALU.subtract))
            dve.sem_inc(S("dve_did"), 1)

            def norm_group(g):
                dve.wait_ge(S(f"h_ld{g}"), 16)
                for t in range(g * GT, (g + 1) * GT):
                    m = nc.vector.bn_stats(st6[:, t, :], h[:, t, :])
                step(m)
                root_tiles(g * GT, (g + 1) * GT, g + 1)

            norm_group(0)
            for t in range(2):
                normed(xn[:, t, :], t).then_inc(S("xn_ready"), 1)
            dve.sem_inc(S("qkn_ready"), 2)
            dve.sem_inc(S("xTl_ready"), 2)

            def low_x0T(t, s):
                dve.wait_ge(S("xT_ready"), t + 3)
                nc.vector.tensor_tensor(f32r(x0Tl[:, s, :, :]), psum[:, 5, 0:D].rearrange("p (k n) -> p k n", k=KC), xTh[:, s, :, :],
                                        ALU.subtract).then_inc(S("xTl_ready"), 1)

            def qk_step(t, s, ahead=2):
                if ahead == 2:
                    dve.wait_ge(S("xT_ps"), t + 1)
                    normed(xn[:, s, :], t + 2).then_inc(S("xn_ready"), 1)
                if ahead:
                    low_x0T(t + 1, 1 - s)
                dve.wait_ge(S("sq_ready"), t + 1)
                nc.vector.tensor_reduce(ssum[:, s, :], sq.rearrange("p (g d) -> p g d", d=DH0), X, ALU.add).then_inc(S("ssum_ready"), 1)
                dve.wait_ge(S("snorm_ready"), t + 1)
                step(nc.vector.tensor_scalar(snorm[:, s, :], snorm[:, s, :], 1e-12, None, ALU.max))
                step(nc.vector.reciprocal(snorm[:, s, :], snorm[:, s, :]))
                dve.wait_ge(S("qkT_ps"), 2 * t + 2)
                nc.vector.tensor_tensor(qkn[:, s, :].rearrange("p (g d) -> p g d", d=DH0),
                                        psum[:, 2 * s:2 * s + 2, :].rearrange("p a (g d) -> p (a g) d", d=DH0),
                                        snorm[:, s, :].unsqueeze(2).to_broadcast([P, 16, DH0]), ALU.mult).then_inc(S("qkn_ready"), 1)

            low_x0T(0, 0)
            for g in range(2):
                for s in range(2):
                    qk_step(2 * g + s, s)
                norm_group(g + 1)
            with dve.Fori(2, TILES // 2 - 1) as i:
                c.enter(i - 2, 4)
                qk_step(2 * i, 0)
                qk_step(2 * i + 1, 1)
                c.leave(TILES // 2 - 3)
            qk_step(TILES - 2, 0, ahead=1)
            qk_step(TILES - 1, 1, ahead=0)
            dve.sem_inc(S("ao0_ready"), 2)

            def stage_kz(b, s):
                nc.vector.tensor_copy(kz[:, s, :, :], qkT[:, 4:8, ds(b * SEQ, P)]).then_inc(S("kz_ready"), 1)

            def divide0(b, s, i, part):
                o_, rows = ((aom, P), (aor, REST))[part]
                dve.wait_ge(S("pv0_ps"), 2 * b + part + 5)
                pv = psum[0:rows, 4 + 2 * part:6 + 2 * part, 0:4 * V0].rearrange("p a (h v) -> p a h v", v=V0)
                rs = rsum[0:rows, s, part, :]
                step(nc.vector.tensor_scalar(rs.rearrange("p (a h) -> p a h", a=2), pv[:, :, :, DH0], 1e-6, None, ALU.max))
                step(nc.vector.reciprocal(rs, rs))
                nc.vector.tensor_tensor(o_[0:rows, s, :, :].rearrange("p (a h) v -> p a h v", a=2), pv[:, :, :, 0:DH0],
                                        rs.rearrange("p (a h) -> p a h", a=2).unsqueeze(3).to_broadcast([rows, 2, 4, DH0]),
                                        ALU.mult).then_inc(S("ao0_ready"), 1)

            def image0_dve(b, s, i, last=False):
                dve.wait_ge(S(f"ao0_st{s}"), 32 * (i + 1))
                divide0(b, s, i, 0)
                if not last:
                    dve.wait_ge(S("s0_ps"), 2 * b + 6)
                    stage_kz(b + 2, s)
                divide0(b, s, i, 1)

            dve.wait_ge(S("qkT_ready"), 2 * TILES + 2)
            for s in range(2):
                stage_kz(s, s)
            with dve.Fori(0, IMAGES // 2 - 1) as i:
                c.enter(i, 8)
                for s in range(2):
                    image0_dve(2 * i + s, s, i)
                c.leave(IMAGES // 2 - 1)
            for s in range(2):
                image0_dve(IMAGES - 2 + s, s, IMAGES // 2 - 1, last=True)
            dve.sem_inc(S("residual_ready"), 2)
            with dve.Fori(0, TILES // 2) as i:
                c.enter(i, 4)
                for s in range(2):
                    t = 2 * i + s
                    dve.wait_ge(S("product_ps"), t + 3)
                    step(nc.vector.tensor_tensor(h[:, t, :], psum[:, 2 + s, 0:D], h[:, t, :], ALU.add))
                    dve.sem_inc(S("residual_ready"), 1)
                    step(nc.vector.bn_stats(st6[:, t, :], h[:, t, :]))
                c.leave(TILES // 2)
            root_tiles(0, TILES, ROOT_2 + 1)
            with dve.Fori(0, TILES // 2) as i:
                for s in range(2):
                    t = 2 * i + s
                    dve.wait_ge(S("rowsT_ps"), ROWS_X2 + t + 1)
                    dve.wait_ge(S("xn2_kept"), t + 1)
                    normed(xn[:, s, :], t).then_inc(S("xn2_ready"), 1)
            dve.wait_ge(S("product_ps"), PRODUCT_GATE + TILES + 2)

            def over8(x, n=TILES):
                return x.unsqueeze(2).to_broadcast([P, n, EXPERTS])

            step(nc.vector.tensor_copy(lg, psum[:, 6, 0:E8].rearrange("p (t e) -> p t e", e=EXPERTS)))
            step(nc.vector.tensor_reduce(r18, lg, X, ALU.max))
            step(nc.vector.tensor_tensor(lg, lg, over8(r18), ALU.subtract))
            dve.sem_inc(S("dve_did"), 1)
            dve.wait_ge(S("act_did"), EXP_EXPERTS)
            step(nc.vector.tensor_reduce(r18, lg, X, ALU.add))
            step(nc.vector.reciprocal(r18, r18))
            step(nc.vector.tensor_tensor(lg, lg, over8(r18), ALU.mult))
            experts = iota[:, 0:EXPERTS].unsqueeze(1).to_broadcast([P, TILES, EXPERTS])
            for k in range(2):
                step(nc.vector.tensor_reduce(val[:, k, :], lg, X, ALU.max))
                step(nc.vector.tensor_tensor(t8, lg, over8(val[:, k, :]), ALU.is_equal))
                step(nc.vector.tensor_scalar(u8, experts, -16.0, None, ALU.add))
                step(nc.vector.tensor_tensor(u8, u8, t8, ALU.mult))
                step(nc.vector.tensor_reduce(s18, u8, X, ALU.min))
                step(nc.vector.tensor_scalar(s18, s18, 16.0, None, ALU.add))
                step(nc.vector.tensor_tensor(oh[:, k, :, :], experts, over8(s18), ALU.is_equal))
                if k == 0:
                    step(nc.vector.scalar_tensor_tensor(out=lg, in0=oh[:, 0, :, :], scalar=-4.0, in1=lg, op0=ALU.mult, op1=ALU.add))
            step(nc.vector.tensor_tensor(s18, val[:, 0, :], val[:, 1, :], ALU.add))
            step(nc.vector.tensor_scalar(s18, s18, 1e-9, None, ALU.max))
            step(nc.vector.reciprocal(s18, s18))
            step(nc.vector.tensor_tensor(gates[:, :, :], val, s18.unsqueeze(1).to_broadcast([P, 2, TILES]), ALU.mult))
            step(nc.vector.tensor_tensor(mask, oh[:, 0, :, :], oh[:, 1, :, :], ALU.add))
            dve.sem_inc(S("dve_did"), 1)
            dve.wait_ge(S("pe_did"), RANKS)
            counts = psum[:, 5, 0:E8].rearrange("p (t e) -> p t e", e=EXPERTS)
            step(nc.vector.tensor_copy(ca, counts))
            x, y = ca, cb
            shift = 1
            while shift < TILES:
                step(nc.vector.tensor_tensor(y[:, shift:, :], x[:, shift:, :], x[:, 0:TILES - shift, :], ALU.add))
                step(nc.vector.tensor_copy(y[:, 0:shift, :], x[:, 0:shift, :]))
                x, y, shift = y, x, 2 * shift
            total = x[:, TILES - 1, :]
            step(nc.vector.tensor_tensor(cmp, total.unsqueeze(2).to_broadcast([P, EXPERTS, TILES]),
                                         q128.unsqueeze(1).to_broadcast([P, EXPERTS, TILES]), ALU.is_gt))
            step(nc.vector.tensor_reduce(nt, cmp, X, ALU.add))
            step(nc.vector.tensor_scalar(nt, nt, 1.0, None, ALU.max))
            step(nc.vector.memset(endf[:, 0:1], 0.0))
            for e in range(EXPERTS):
                step(nc.vector.tensor_tensor(endf[:, e + 1:e + 2], endf[:, e:e + 1], nt[:, e:e + 1], ALU.add))
            step(nc.vector.tensor_tensor(y, x, counts, ALU.subtract))
            step(nc.vector.tensor_tensor(y, psum[:, 7, 0:E8].rearrange("p (t e) -> p t e", e=EXPERTS), y, ALU.add))
            step(nc.vector.scalar_tensor_tensor(out=y, in0=endf[:, 0:EXPERTS].unsqueeze(1).to_broadcast([P, TILES, EXPERTS]),
                                                scalar=float(P), in1=y, op0=ALU.mult, op1=ALU.add))
            for k in range(2):
                step(nc.vector.tensor_tensor(t8, oh[:, k, :, :], y, ALU.mult))
                step(nc.vector.tensor_reduce(posf[:, k, :], t8, X, ALU.add))
            step(nc.vector.tensor_copy(slot[:, :, :], posf))
            dve.sem_inc(S("dve_did"), 1)
            step(nc.vector.tensor_tensor(cmpj, tile_no.unsqueeze(2).to_broadcast([P, SLOT_TILES, EXPERTS]),
                                         endf[:, 1:].unsqueeze(1).to_broadcast([P, SLOT_TILES, EXPERTS]), ALU.is_ge))
            step(nc.vector.tensor_reduce(ej, cmpj, X, ALU.add))
            step(nc.vector.tensor_scalar(ej, ej, float(EXPERTS - 1), None, ALU.min))
            step(nc.vector.tensor_scalar(moe_tab[:, 0, :], ej[0:1, :], 1.0, None, ALU.add))
            step(nc.vector.tensor_scalar(ej2, ej, 1.0, None, ALU.is_ge))
            for e in range(2, EXPERTS):
                step(nc.vector.scalar_tensor_tensor(out=ej2, in0=ej, scalar=float(e), in1=ej2, op0=ALU.is_ge,
                                                    op1=ALU.add if e % 2 else ALU.subtract, **({} if e % 2 else {"reverse1": True})))
            step(nc.vector.tensor_scalar(moe_tab[:, 1, :], ej2[0:1, :], float(EXPW), None, ALU.mult))
            step(nc.vector.tensor_scalar(end_tab[:, :], endf[0:1, 1:], 2.0, 2.0, ALU.mult, ALU.add))
            dve.sem_inc(S("dve_did"), 1)
            for e in range(2):
                dve.wait_ge(S("act_did"), W01_HIGH + e + 1)
                w = slice(e * EXPW, (e + 1) * EXPW)
                nc.vector.tensor_tensor(f32r(wlow[:, w]), wraw01[:, w], whigh[:, w], ALU.subtract).then_inc(S("split_ready"), 1)
            dve.sem_inc(S("hid_ready"), 2)
            dve.sem_inc(S("hidT_ready"), 2)

            def low_xT(j, s):
                dve.wait_ge(S("xsT_ready"), j + 3)
                nc.vector.tensor_tensor(f32r(xTl[:, s, :, :]), psum[:, 6, 0:D].rearrange("p (k n) -> p k n", k=KC), xTh[:, s, :, :],
                                        ALU.subtract).then_inc(S("xTl_ready"), 1)

            def hidden(n, s):
                dve.wait_ge(S("sil_ready"), n + 3)
                dve.wait_ge(S("hidT_ps"), n + 1)
                nc.vector.tensor_tensor(hid[:, s, :], sil[:, s, :], psum[:, 2 * s + 1, :], ALU.mult).then_inc(S("hid_ready"), 1)

            def keep_hidT(n, s):
                dve.wait_ge(S("hidT_ps"), n + 3)
                dve.wait_ge(S("dn_ps"), n + 1)
                t_ = psum[:, 4 + s, :].rearrange("p (k n) -> p k n", k=4)
                step(nc.vector.tensor_copy(f32r(hidTh[:, s, :, :]), t_))
                nc.vector.tensor_tensor(f32r(hidTl[:, s, :, :]), t_, hidTh[:, s, :, :], ALU.subtract).then_inc(S("hidT_ready"), 1)

            low_xT(0, 0)
            low_xT(1, 1)
            hidden(0, 0)
            hidden(1, 1)
            keep_hidT(0, 0)
            hidden(2, 0)
            keep_hidT(1, 1)
            with dve.Fori(0, SLOT_TILES // 2 - 1) as i:
                c.enter(i, 4)
                for j, s in ((2 * i + 1, 0), (2 * i + 2, 1)):
                    low_xT(j + 1, s)
                    hidden(2 * j + 1, 1)
                    keep_hidT(2 * j, 0)
                    hidden(2 * j + 2, 0)
                    keep_hidT(2 * j + 1, 1)
                c.leave(SLOT_TILES // 2 - 1)
            hidden(2 * SLOT_TILES - 1, 1)
            keep_hidT(2 * SLOT_TILES - 2, 0)
            keep_hidT(2 * SLOT_TILES - 1, 1)
            def combine(t, k):
                return nc.vector.scalar_tensor_tensor(out=h[:, t, :], in0=yg[:, k, t, :], scalar=gates[:, k, ds(t, 1)], in1=h[:, t, :],
                                                      op0=ALU.mult, op1=ALU.add)

            def combine_tile(t):
                for k in range(2):
                    step(combine(t, k))
                step(nc.vector.bn_stats(st6[:, t, :], h[:, t, :]))

            def root_group(g):
                root_tiles(g * GT, (g + 1) * GT, ROOT_3 + g + 1)
                dve.wait_ge(S("rowsT_ps"), ROWS_X1 + g * GT + 1)
                normed(xn[:, 0, :], g * GT).then_inc(S("xn1_ready"), 1)
                if g == 0:
                    normed(xn[:, 1, :], 1).then_inc(S("xn1_ready"), 1)

            dve.wait_ge(S("yg_ld0"), 32 * GT)
            for k in range(2):
                for t in range(GT):
                    m = combine(t, k)
                step(m)
            for t in range(GT):
                m = nc.vector.bn_stats(st6[:, t, :], h[:, t, :])
            step(m)
            for s in range(2):
                m = nc.vector.memset(vst1[:, s, :, DH1:V1], 1.0)
            step(m)
            dve.sem_inc(S("dve_did"), 1)
            dve.sem_inc(S("qkr_ready"), 2)
            root_group(0)

            def rope_step(t, s, i, ahead=True):
                if ahead:
                    dve.wait_ge(S("rowsT_ps"), ROWS_X1 + t + 3)
                    normed(xn[:, s, :], t + 2).then_inc(S("xn1_ready"), 1)
                dve.wait_ge(S("qkv1_ps"), t + 1)
                dve.wait_ge(S(f"rp_ld{s}"), 16 * (i + 1))
                dve.wait_ge(S("qkr_ready"), t + 2)
                qk = psum[:, 2 * s, :].rearrange("p (a e n) -> p a e n", a=2, e=2)
                nc.vector.tensor_tensor(ra, qk, rp[:, s, 0:2, :].unsqueeze(1).to_broadcast([P, 2, 2, P]), ALU.mult)
                step(nc.vector.tensor_tensor(rb, qk, rp[:, s, 1:3, :].unsqueeze(1).to_broadcast([P, 2, 2, P]), ALU.mult))
                dve.wait_ge(S("qkT1_ps"), t + 1)
                o_ = qkr[:, s, :, :].rearrange("p (a e) n -> p a e n", a=2)
                step(nc.vector.tensor_tensor(o_[:, :, 0, :], ra[:, :, 0, :], ra[:, :, 1, :], ALU.subtract))
                nc.vector.tensor_tensor(o_[:, :, 1, :], rb[:, :, 0, :], rb[:, :, 1, :], ALU.add).then_inc(S("qkr_ready"), 1)

            for g in range(GROUPS - 1):
                dve.wait_ge(S(f"yg_ld{g + 1}"), 32 * GT)
                combine_tile((g + 1) * GT)
                with dve.Fori(0, HT - 1) as i:
                    c.enter(i, 10)
                    for s in range(2):
                        rope_step(g * GT + 2 * i + s, s, g * HT + i)
                        combine_tile((g + 1) * GT + 2 * i + s + 1)
                    c.leave(HT - 1)
                rope_step((g + 1) * GT - 2, 0, (g + 1) * HT - 1, ahead=False)
                combine_tile((g + 2) * GT - 1)
                root_group(g + 1)
                rope_step((g + 1) * GT - 1, 1, (g + 1) * HT - 1)
            with dve.Fori(0, HT - 1) as i:
                c.enter(i, 4)
                for s in range(2):
                    rope_step(TILES - GT + 2 * i + s, s, (TILES - GT) // 2 + i)
                c.leave(HT - 1)
            for s in range(2):
                rope_step(TILES - 2 + s, s, TILES // 2 - 1, ahead=False)
            dve.sem_inc(S("s1_read"), 2)
            dve.sem_inc(S("a1r_ready"), 1)

            def less_max(b, s, u):
                base = 2 * (u % 2)
                dve.wait_ge(S("s1_ps"), 4 * b + u + 1)
                sc = psum[:, base:base + 2, 0:2 * SEQ].rearrange("p a (h j) -> p a h j", j=SEQ)
                best = max1[:, u % 2, :]
                step(nc.vector.tensor_reduce(best.rearrange("p (a h) -> p a h", a=2), sc, X, ALU.max))
                for at, lo, n in ((FIRST_AT[u % 2], 0, P), (LAST_AT[u % 2], P, REST)):
                    m = nc.vector.tensor_tensor(wts[:, s, u // 2, at:at + 4 * n].rearrange("p (a h j) -> p a h j", a=2, h=2), sc[:, :, :, lo:lo + n],
                                                best.rearrange("p (a h) -> p a h", a=2).unsqueeze(3).to_broadcast([P, 2, 2, n]), ALU.subtract)
                m.then_inc(S("s1_read"), 1)

            def max_rest(b):
                dve.wait_ge(S("sr_ps"), b + 3)
                step(nc.vector.tensor_reduce(mr[0:RQ, :], psum[0:RQ, 7, 0:2 * SEQ].rearrange("p (g j) -> p g j", g=2), X, ALU.max))
                nc.vector.tensor_scalar(mr[0:RQ, :], mr[0:RQ, :], -(DH1 ** -0.5), None, ALU.mult).then_inc(S("mr_ready"), 1)

            def divide_main(b, s, turn):
                dve.wait_ge(S("pv1_ps"), b + 3)
                dve.wait_ge(S(f"a1_st{s}"), 16 * (turn + 1))
                pv = psum[:, 6, 0:H1 * V1].rearrange("p (h v) -> p h v", v=V1)
                step(nc.vector.reciprocal(rs1, pv[:, :, DH1]))
                nc.vector.tensor_tensor(a1m[:, s, :, :], pv[:, :, 0:DH1], rs1.unsqueeze(2).to_broadcast([P, H1, DH1]), ALU.mult).then_inc(S("a1_ready"), 1)

            def divide_rest(b, s, turn):
                dve.wait_ge(S("avr_ps"), b + 1)
                dve.wait_ge(S(f"a1r_st{s}"), 32 * (turn + 1))
                step(nc.vector.reciprocal(rr[0:RQ, :], rr[0:RQ, :]))
                step(nc.vector.tensor_tensor(avr[0:RQ, :, :, :], psum[0:RQ, 7, 0:2 * P].rearrange("p (g h v) -> p g h v", g=2, h=HG),
                                             restmask[0:RQ, :].unsqueeze(1).unsqueeze(3).to_broadcast([RQ, 2, HG, DH1]), ALU.mult))
                step(nc.vector.tensor_reduce(a1r[0:RQ, s, :, :], avr[0:RQ, :, :, :].rearrange("p g h v -> p g v h"), X, ALU.add))
                nc.vector.tensor_tensor(a1r[0:RQ, s, :, :], a1r[0:RQ, s, :, :], rr[0:RQ, :].unsqueeze(2).to_broadcast([RQ, 2, DH1]), ALU.mult).then_inc(S("a1r_ready"), 1)

            def image1_dve(b, s, turn, first=False, last=False):
                less_max(b, s, 2)
                if not first:
                    divide_main(b - 1, 1 - s, turn if s else turn - 1)
                less_max(b, s, 3)
                max_rest(b)
                if not last:
                    less_max(b + 1, 1 - s, 0)
                    less_max(b + 1, 1 - s, 1)
                divide_rest(b, s, turn)

            less_max(0, 0, 0)
            less_max(0, 0, 1)
            image1_dve(0, 0, 0, first=True)
            with dve.Fori(0, IMAGES // 2 - 1) as i:
                c.enter(i, 18)
                image1_dve(2 * i + 1, 1, i)
                image1_dve(2 * i + 2, 0, i + 1)
                c.leave(IMAGES // 2 - 1)
            image1_dve(IMAGES - 1, 1, IMAGES // 2 - 1, last=True)
            divide_main(IMAGES - 1, 1, IMAGES // 2 - 1)
            dve.wait_ge(S("h_bias"), 1)

            def group_root(before, g):
                dve.sem_inc(S("passed"), 1)
                for n in range(GT):
                    m = nc.vector.bn_aggr(mvg[:, n, :], stg[:, n, :])
                step(m)
                step(nc.vector.tensor_scalar(mvg[:, :, 1], mvg[:, :, 1], 1e-5, None, ALU.add))
                dve.sem_inc(S("ln_stats"), 1)
                dve.wait_ge(S("ln_root"), before + g + 1)
                step(nc.vector.reciprocal(rg, rg))

            with dve.Fori(0, GROUPS) as g:
                c.enter(g, 5)
                for n in range(GT):
                    t = g * GT + n
                    dve.wait_ge(S("product_ps"), PRODUCT_O1 + t + 3)
                    nc.vector.tensor_tensor(h[:, t, :], psum[:, 2 + n, 0:D], h[:, t, :], ALU.add).then_inc(S("residual_ready"), 1)
                dve.wait_ge(S("residual_ready"), RESIDUAL_3 + (g + 1) * GT + 2)
                dve.sem_inc(S("passed"), 1)
                for n in range(GT):
                    m = nc.vector.bn_stats(stg[:, n, :], h[:, g * GT + n, :])
                step(m)
                group_root(ROOT_4, g)
                for n in range(GT):
                    m = nc.vector.tensor_scalar(x3[:, g * GT + n, :], h[:, g * GT + n, :], mvg[:, n, 0:1], rg[:, n:n + 1], ALU.subtract, ALU.mult)
                step(m)
                dve.sem_inc(S("x3_ready"), 1)
                c.leave(GROUPS)
            with dve.Fori(0, GROUPS) as g:
                for n in range(GT):
                    t = g * GT + n
                    if n % HT == 0:
                        dve.wait_ge(S(f"xg_ld{n // HT}"), 16 * HT * (g + 2))
                    dve.wait_ge(S("rowsT_ps"), ROWS_X3 + t - 1)
                    nc.vector.tensor_copy(xgs[:, n, :], xg[:, t, :]).then_inc(S("xgs_ready"), 1)
            dve.wait_ge(S("product_ps"), PRODUCT_ROUTER + TILES + 2)

            def over16(x):
                return x.unsqueeze(2).to_broadcast([P, TILES, HF])

            step(nc.vector.tensor_copy(lg3, psum[:, 4, 0:TILES * HF].rearrange("p (t e) -> p t e", e=HF)))
            step(nc.vector.tensor_reduce(rstd[:, :], lg3, X, ALU.max))
            step(nc.vector.tensor_tensor(lg3, lg3, over16(rstd[:, :]), ALU.subtract))
            dve.sem_inc(S("dve_did"), 1)
            dve.wait_ge(S("act_did"), EXP_HEADS)
            step(nc.vector.tensor_reduce(rstd[:, :], lg3, X, ALU.add))
            step(nc.vector.reciprocal(rstd[:, :], rstd[:, :]))
            step(nc.vector.tensor_tensor(lg3, lg3, over16(rstd[:, :]), ALU.mult))
            dve.sem_inc(S("dve_did"), 1)
            dve.wait_ge(S("pe_did"), PROBS_T)
            for rows, lo, n in ((P, 0, 2), (32, 2, 1)):
                def part(x):
                    return x[0:rows, lo * P:(lo + n) * P].rearrange("p (b s) -> p b s", s=IMAGES)

                nb = n * GB
                best = m3[0:rows, lo * GB:lo * GB + nb]
                over = best.unsqueeze(2).to_broadcast([rows, nb, IMAGES])
                images = iota[0:rows, :].unsqueeze(1).to_broadcast([rows, nb, IMAGES])
                step(nc.vector.tensor_copy(part(pT), psum[0:rows, 5, lo * P:(lo + n) * P].rearrange("p (b s) -> p b s", s=IMAGES)))
                step(nc.vector.tensor_reduce(best, part(pT), X, ALU.max))
                step(nc.vector.tensor_tensor(part(pT), part(pT), over, ALU.is_equal))
                step(nc.vector.tensor_scalar(part(uT), images, -float(IMAGES), None, ALU.add))
                step(nc.vector.tensor_tensor(part(uT), part(uT), part(pT), ALU.mult))
                step(nc.vector.tensor_reduce(best, part(uT), X, ALU.min))
                step(nc.vector.tensor_scalar(best, best, float(IMAGES), None, ALU.add))
                step(nc.vector.tensor_tensor(part(oT), images, over, ALU.is_equal))
            dve.sem_inc(S("dve_did"), 1)
            dve.wait_ge(S("pe_did"), CHOICES)
            step(nc.vector.tensor_copy(sel, psum[:, 6, 0:TILES * HF].rearrange("p (t h) -> p t h", h=HF)))
            dve.sem_inc(S("sel_all_ready"), 2)

            def select_tile(t, s):
                dve.wait_ge(S("hg_ps"), t + 3)
                nc.vector.tensor_tensor(selb[:, s, :, :], sel[:, t, :].unsqueeze(1).to_broadcast([P, GB, HF]),
                                        headmask.unsqueeze(2).to_broadcast([P, GB, HF]), ALU.mult).then_inc(S("selb_ready"), 1)

            def keep_selection(t, s):
                dve.wait_ge(S("hg_ps"), t + 5)
                nc.vector.tensor_copy(sel_all[:, t, :], psum[:, 2 + s, 0:P]).then_inc(S("sel_all_ready"), 1)

            select_tile(0, 0)
            with dve.Fori(0, TILES // 2 - 1) as i:
                for s in range(2):
                    select_tile(2 * i + s + 1, 1 - s)
                    keep_selection(2 * i + s, s)
            select_tile(TILES - 1, 1)
            keep_selection(TILES - 2, 0)
            keep_selection(TILES - 1, 1)
            dve.wait_ge(S("bf_ld"), 16)
            dve.sem_inc(S("vf_ready"), 2)
            dve.sem_inc(S("af_ready"), 1)
            dve.sem_inc(S("aof_ready"), 2)

            def bias(p_, x):
                return bf[:, ds(p_, 1), x:x + 1].rearrange("p a b -> p (a b)")

            def add_biases(p_, s):
                dve.wait_ge(S("qkvf_ps"), p_ + 3)
                qkv = psum[:, s, 0:3 * SEQ].rearrange("p (x n) -> p x n", x=3)
                step(nc.vector.tensor_scalar(qf, qkv[:, 0, :], bias(p_, 0), None, ALU.add))
                nc.vector.scalar_tensor_tensor(out=kf, in0=qkv[:, 1, :], scalar=bias(p_, 1), in1=qf, op0=ALU.add, op1=ALU.mult).then_inc(S("kf_ready"), 1)
                nc.vector.tensor_scalar(vf, qkv[:, 2, :], bias(p_, 2), None, ALU.add).then_inc(S("vf_ready"), 1)

            def weigh(p_, s):
                dve.wait_ge(S("attf_ps"), p_ + 1)
                step(nc.vector.tensor_reduce(mf[:, s:s + 1], psum[:, 2, 0:SEQ], X, ALU.max))
                nc.vector.tensor_scalar(mf[:, s:s + 1], mf[:, s:s + 1], -(DHF ** -0.5), None, ALU.mult).then_inc(S("mf_ready"), 1)
                dve.wait_ge(S("ef_ready"), p_ + 1)
                step(nc.vector.reciprocal(rf[:, s:s + 1], rf[:, s:s + 1]))
                dve.wait_ge(S("vf_ready"), p_ + 3)
                dve.wait_ge(S("aof_ps"), 2 * p_ + 2)
                nc.vector.scalar_tensor_tensor(out=af[:, s, :], in0=ef, scalar=rf[:, s:s + 1], in1=vf, op0=ALU.mult, op1=ALU.mult).then_inc(S("af_ready"), 1)

            def add_out_bias(p_, s, i):
                dve.wait_ge(S(f"aof_st{s}"), 32 * (i + 1))
                for n, (o_, rows, bank) in enumerate(((aofm, P, 4), (aofr, REST, 6))):
                    dve.wait_ge(S("aof_ps"), 2 * p_ + n + 5)
                    nc.vector.tensor_tensor(o_[0:rows, s, :, :], psum[0:rows, bank:bank + 2, 0:D],
                                            rowv[0:rows, 2, :].unsqueeze(1).to_broadcast([rows, 2, D]), ALU.add).then_inc(S("aof_ready"), 1)

            def pair_dve(p_, s, i, last=False):
                weigh(p_, s)
                if not last:
                    dve.wait_ge(S("af_ready"), p_ + 2)
                    add_biases(p_ + 1, 1 - s)
                add_out_bias(p_, s, i)

            add_biases(0, 0)
            with dve.Fori(0, PAIRS // 2 - 1) as i:
                c.enter(i, 6)
                pair_dve(2 * i, 0, i)
                pair_dve(2 * i + 1, 1, i)
                c.leave(PAIRS // 2 - 1)
            pair_dve(PAIRS - 2, 0, PAIRS // 2 - 1)
            pair_dve(PAIRS - 1, 1, PAIRS // 2 - 1, last=True)
            dve.sem_inc(S("y_read"), GT)
            dve.sem_inc(S("o1_ready"), 4)
            dve.wait_ge(S("h3b_ld"), 16 * TILES)
            with dve.Fori(0, GROUPS) as g:
                c.enter(g, 4)
                for n in range(GT):
                    dve.wait_ge(S("yf_ps"), g * GT + n + 3)
                    m = nc.vector.bn_stats(stg[:, n, :], psum[:, n, 0:D])
                step(m)
                group_root(ROOT_5, g)
                for s in range(2):
                    dve.wait_ge(S(f"out_st{s}"), 16 * HT * g + 16)
                for n in range(GT):
                    nc.vector.scalar_tensor_tensor(out=o1[:, n, :], in0=psum[:, n, 0:D], scalar=mvg[:, n, 0:1], in1=rowv[:, 3, :],
                                                   op0=ALU.subtract, op1=ALU.mult).then_inc(S("y_read"), 1)
                dve.wait_ge(S("y_read"), (g + 2) * GT)
                for n in range(GT):
                    nc.vector.scalar_tensor_tensor(out=o1[:, n, :], in0=o1[:, n, :], scalar=rg[:, n:n + 1], in1=h3b[:, g * GT + n, :],
                                                   op0=ALU.mult, op1=ALU.add).then_inc(S("o1_ready"), 1)
                c.leave(GROUPS)

        @block.tensor
        def _(pe):
            pe.sem_inc(S("tok_ps"), 2)
            pe.wait_ge(S("wtok_ld"), 16)
            with pe.Fori(0, IMAGES // 4) as i:
                for s in range(2):
                    t = 2 * i + s
                    pe.wait_ge(S(f"pt_ld{s}"), 16 * (i + 1))
                    pe.wait_ge(S("tok_ready"), t + 1)
                    for k in range(PK):
                        m = nc.tensor.matmul(psum[:, s, 0:D], pt[:, s, k, :], wtok_sb[:, k, :], start=(k == 0), stop=(k == PK - 1))
                    m.then_inc(S("tok_ps"), 1)
            pe.wait_ge(S("w0_ld"), 32)
            pe.wait_ge(S("dve_did"), DID["w0low_ready"])
            pe.wait_ge(S("tok_ready"), IMAGES // 2 + 2)
            pe.sem_inc(S("qkT_ps"), 4)

            def qkT_tile(t, s):
                pe.wait_ge(S("qkn_ready"), t + 3)
                for a in range(2):
                    pe.wait_ge(S("qkT_ready"), 2 * t + a + 1)
                    for k in range(4):
                        m = nc.tensor.transpose(psum[:, 6 + a, k * P:(k + 1) * P], qkn[:, s, (4 * a + k) * P:(4 * a + k + 1) * P], ident)
                    m.then_inc(S("qkT_ps"), 1)

            def xT_tile(t, s):
                pe.wait_ge(S("xn_ready"), t + 1)
                for k in range(KC):
                    m = nc.tensor.transpose(psum[:, 5, k * P:(k + 1) * P], xn[:, s, k * P:(k + 1) * P], ident)
                m.then_inc(S("xT_ps"), 1)

            def qkv_tile(t, s, first=False, last=False):
                pe.wait_ge(S("xTl_ready"), t + 3)
                if not last:
                    xT_tile(t + 1, 1 - s)
                pe.wait_ge(S("qkn_ready"), t + 1)
                for a, bank in ((0, 2 * s), (1, 2 * s + 1), (2, 4)):
                    if a == 2:
                        pe.wait_ge(S("v0_ready"), t + 1)
                    for k in range(KC):
                        for n, (x_, w_) in enumerate(((xTh, w0high), (x0Tl, w0high), (xTh, w0low))):
                            m = nc.tensor.matmul(psum[:, bank, :], f32r(x_[:, s, k, :]), f32r(w_[:, k, a * 512:(a + 1) * 512]),
                                                 start=(k == 0 and n == 0), stop=(k == KC - 1 and n == 2))
                m.then_inc(S("qkv_ps"), 1)
                if not first:
                    qkT_tile(t - 1, 1 - s)

            xT_tile(0, 0)
            qkv_tile(0, 0, first=True)
            with pe.Fori(0, TILES // 2 - 1) as i:
                qkv_tile(2 * i + 1, 1)
                qkv_tile(2 * i + 2, 0)
            qkv_tile(TILES - 1, 1, last=True)
            qkT_tile(TILES - 1, 1)
            pe.sem_inc(S("pv0_ps"), 4)
            pe.sem_inc(S("s0_ps"), 4)

            def scores0(b, s, u):
                if u == 0:
                    pe.wait_ge(S("kz_ready"), b + 1)
                pe.wait_ge(S("qks_ready"), 2 * b + u + 1)
                pe.wait_ge(S("p0_ready"), 2 * b + u + 1)
                for r in range(2):
                    m = nc.tensor.matmul(psum[:, 2 * u + r, 0:2 * SEQ], kz[:, s, 2 * u + r, :], qz[:, s, 2 * u + r, :, :].rearrange("p h i -> p (h i)"),
                                         start=True, stop=True)
                if u:
                    for ch in range(4):
                        m = nc.tensor.matmul(psum[0:RQ, 3, 2 * SEQ:3 * SEQ], kblk0[:, s, ch, :], qkT[:, ch, ds(b * SEQ, SEQ)], start=(ch == 0), stop=(ch == 3))
                m.then_inc(S("s0_ps"), 1)

            def values0(s, part):
                lo, n = ((0, P), (P, REST))[part]
                for a in range(2):
                    bank = 4 + 2 * part + a
                    for hd in range(4):
                        nc.tensor.matmul(psum[0:n, bank, hd * V0:(hd + 1) * V0], pm[:, s, 4 * a + hd, lo:lo + n], vm[:, s, 4 * a + hd, :],
                                         start=(hd == 0), stop=False, skip_group_check=True)
                    m = nc.tensor.matmul(psum[0:n, bank, 0:4 * V0], pr[0:RQ, s, lo:lo + n],
                                         vdiag0[0:RQ, s, 4 * a:4 * a + 4, :].rearrange("p h v -> p (h v)"), start=False, stop=True, skip_group_check=True)
                m.then_inc(S("pv0_ps"), 1)

            def image0(b, s, i, last=False):
                if not last:
                    scores0(b + 1, 1 - s, 0)
                pe.wait_ge(S("p0_ready"), 2 * b + 4)
                pe.wait_ge(S("vdiag0_ready"), b + 1)
                pe.wait_ge(S(f"v0_ld{s}"), 32 * (i + 1))
                pe.wait_ge(S("ao0_ready"), 2 * b + 1)
                values0(s, 0)
                if not last:
                    scores0(b + 1, 1 - s, 1)
                pe.wait_ge(S("ao0_ready"), 2 * b + 2)
                values0(s, 1)

            scores0(0, 0, 0)
            scores0(0, 0, 1)
            with pe.Fori(0, IMAGES // 2 - 1) as i:
                image0(2 * i, 0, i)
                image0(2 * i + 1, 1, i)
            image0(IMAGES - 2, 0, IMAGES // 2 - 1)
            image0(IMAGES - 1, 1, IMAGES // 2 - 1, last=True)
            pe.wait_ge(S("weights_ld"), 16 * 3)
            pe.sem_inc(S("rowsT_ps"), 2)
            pe.sem_inc(S("product_ps"), 2)

            def aT_tile(t, s, i):
                pe.wait_ge(S(f"aT_ld{s}"), 16 * (i + 1))
                pe.wait_ge(S("rowsT_ready"), t + 1)
                for k in range(4):
                    m = nc.tensor.transpose(psum[:, s, k * P:(k + 1) * P], aT_in[:, s, k * P:(k + 1) * P], ident)
                m.then_inc(S("rowsT_ps"), 1)

            def o0_tile(t, s):
                pe.wait_ge(S("rowsT_ready"), t + 3)
                pe.wait_ge(S("residual_ready"), t + 1)
                for k in range(4):
                    m = nc.tensor.matmul(psum[:, 2 + s, 0:D], aT[:, s, k, :], wo_sb[:, k, :], start=(k == 0), stop=(k == 3))
                m.then_inc(S("product_ps"), 1)

            aT_tile(0, 0, 0)
            with pe.Fori(0, TILES // 2 - 1) as i:
                aT_tile(2 * i + 1, 1, i)
                o0_tile(2 * i, 0)
                aT_tile(2 * i + 2, 0, i + 1)
                o0_tile(2 * i + 1, 1)
            aT_tile(TILES - 1, 1, TILES // 2 - 1)
            o0_tile(TILES - 2, 0)
            o0_tile(TILES - 1, 1)
            pe.wait_ge(S("weights_ld"), 16 * 3)

            def xT2_tile(t, s):
                pe.wait_ge(S("xn2_ready"), t + 1)
                pe.wait_ge(S("rowsT_ready"), ROWS_X2 + t + 1)
                for k in range(KC):
                    m = nc.tensor.transpose(psum[:, 4 + s, k * P:(k + 1) * P], xn[:, s, k * P:(k + 1) * P], ident)
                m.then_inc(S("rowsT_ps"), 1)

            def gate_tile(t, s):
                pe.wait_ge(S("rowsT_ready"), ROWS_X2 + t + 3)
                for k in range(KC):
                    m = nc.tensor.matmul(psum[:, 6, ds(t * EXPERTS, EXPERTS)], xT[:, s, k, :], wgate_sb[:, k, :], start=(k == 0), stop=(k == KC - 1))
                m.then_inc(S("product_ps"), 1)

            xT2_tile(0, 0)
            with pe.Fori(0, TILES // 2 - 1) as i:
                xT2_tile(2 * i + 1, 1)
                gate_tile(2 * i, 0)
                xT2_tile(2 * i + 2, 0)
                gate_tile(2 * i + 1, 1)
            xT2_tile(TILES - 1, 1)
            gate_tile(TILES - 2, 0)
            gate_tile(TILES - 1, 1)
            pe.wait_ge(S("dve_did"), DID["mask_ready"])
            nc.tensor.matmul(psum[:, 7, 0:E8], tri, mask.rearrange("p t e -> p (t e)"), start=True, stop=True)
            nc.tensor.matmul(psum[:, 5, 0:E8], ones[:, :], mask.rearrange("p t e -> p (t e)"), start=True, stop=True).then_inc(S("pe_did"), 1)
            pe.sem_inc(S("xsT_ps"), 2)
            pe.sem_inc(S("hidT_ps"), 2)
            pe.sem_inc(S("dn_ps"), 2)

            def xsT_tile(j, s, i):
                pe.wait_ge(S(f"xsl_ld{s}"), 16 * (i + 1))
                pe.wait_ge(S("xTl_ready"), TILES + j + 2)
                for k in range(KC):
                    m = nc.tensor.transpose(psum[:, 6, k * P:(k + 1) * P], xsl[:, s, k * P:(k + 1) * P], ident)
                m.then_inc(S("xsT_ps"), 1)

            def gu_half(n, s, half, at):
                pe.wait_ge(S("hid_ready"), n + 1)
                for a in range(2):
                    for k in range(KC):
                        for n, (x_, w_) in enumerate(((xTh, whigh), (xTl, whigh), (xTh, wlow))):
                            m = nc.tensor.matmul(psum[:, 2 * half + a, :], f32r(x_[:, s, k, :]), f32r(w_[:, ds(at + k * 2 * F + a * F + half * 512, 512)]),
                                                 start=(k == 0 and n == 0), stop=(k == KC - 1 and n == 2))
                m.then_inc(S("gu_ps"), 1)

            def hidT_half(n, half):
                pe.wait_ge(S("hid_ready"), n + 3)
                pe.wait_ge(S("hidT_ready"), n + 1)
                for k in range(4):
                    m = nc.tensor.transpose(psum[:, 4 + half, k * P:(k + 1) * P], hid[:, half, k * P:(k + 1) * P], ident)
                m.then_inc(S("hidT_ps"), 1)

            def down_half(n, half, at):
                pe.wait_ge(S("hidT_ready"), n + 3)
                for k in range(4):
                    for n, (x_, w_) in enumerate(((hidTh, whigh), (hidTl, whigh), (hidTh, wlow))):
                        m = nc.tensor.matmul(psum[:, 7, 0:D], f32r(x_[:, half, k, :]), f32r(w_[:, ds(at + KC * 2 * F + (4 * half + k) * D, D)]),
                                             start=(half == 0 and k == 0 and n == 0), stop=(half == 1 and k == 3 and n == 2))
                m.then_inc(S("dn_ps"), 1)

            def expert_of(j):
                return pe.value_load(moe_tab[0:1, 0, ds(j, 1)], min_val=1, max_val=EXPERTS)

            def place_of(j):
                return pe.value_load(moe_tab[0:1, 1, ds(j, 1)], min_val=0, max_val=EXPW)

            def expert_tile(j, s, i, ready, before, at, nxt=True, carry=True):
                pe.wait_ge(S("wexp_ready"), ready)
                pe.sem_inc(S("passed"), 1)
                pe.wait_ge(S("xTl_ready"), TILES + j + 3)
                gu_half(2 * j, s, 0, at)
                hidT_half(2 * j - 1, 1)
                pe.wait_ge(S("y_ready"), j + 1)
                down_half(2 * j - 2, 0, before)
                if nxt:
                    xsT_tile(j + 1, 1 - s, i)
                gu_half(2 * j + 1, s, 1, at)
                following = (expert_of(j + 1), place_of(j + 1)) if nxt and carry else None
                hidT_half(2 * j, 0)
                down_half(2 * j - 1, 1, before)
                return following

            pe.wait_ge(S("dve_did"), DID["tables_ready"])
            xsT_tile(0, 0, 0)
            xsT_tile(1, 1, 0)
            ready, first = expert_of(0), place_of(0)
            pe.wait_ge(S("xTl_ready"), TILES + 3)
            pe.wait_ge(S("wexp_ready"), ready)
            gu_half(0, 0, 0, first)
            gu_half(1, 0, 1, first)
            hidT_half(0, 0)
            LASTJ = SLOT_TILES - 1
            with pe.Fori(0, SLOT_TILES // 2 - 1) as i:
                before, ready, at = place_of(2 * i), expert_of(2 * i + 1), place_of(2 * i + 1)
                ready2, at2 = expert_tile(2 * i + 1, 1, i + 1, ready, before, at)
                expert_tile(2 * i + 2, 0, i + 1, ready2, at, at2, carry=False)
            before, ready, at = place_of(LASTJ - 1), expert_of(LASTJ), place_of(LASTJ)
            expert_tile(LASTJ, 1, 0, ready, before, at, nxt=False)
            hidT_half(2 * LASTJ + 1, 1)
            pe.wait_ge(S("y_ready"), LASTJ + 2)
            down_half(2 * LASTJ, 0, at)
            down_half(2 * LASTJ + 1, 1, at)
            pe.wait_ge(S("weights1_ld"), 32)
            pe.sem_inc(S("qkT1_ps"), 2)

            def qkT1_tile(t, s):
                pe.wait_ge(S("qkr_ready"), t + 3)
                pe.wait_ge(S("qkT1_ready"), t + 2)
                for k in range(4):
                    m = nc.tensor.transpose(psum[:, 6, k * P:(k + 1) * P], qkr[:, s, k, :], ident)
                m.then_inc(S("qkT1_ps"), 1)

            def x1T_tile(t, s):
                pe.wait_ge(S("xn1_ready"), t + 1)
                pe.wait_ge(S("rowsT_ready"), ROWS_X1 + t + 2)
                for k in range(KC):
                    m = nc.tensor.transpose(psum[:, 5, k * P:(k + 1) * P], xn[:, s, k * P:(k + 1) * P], ident)
                m.then_inc(S("rowsT_ps"), 1)

            def qkv1_tile(t, s, first=False, last=False):
                pe.wait_ge(S("rowsT_ready"), ROWS_X1 + t + 3)
                pe.wait_ge(S("qkr_ready"), t + 1)
                pe.wait_ge(S("v1_ready"), t + 1)
                for a, n in ((0, 512), (1, D)):
                    for k in range(KC):
                        m = nc.tensor.matmul(psum[:, 2 * s + a, 0:n], xT[:, s, k, :], wqkv1_sb[:, k, a * 512:a * 512 + n], start=(k == 0), stop=(k == KC - 1))
                m.then_inc(S("qkv1_ps"), 1)
                if not last:
                    x1T_tile(t + 1, 1 - s)
                if not first:
                    qkT1_tile(t - 1, 1 - s)

            x1T_tile(0, 0)
            qkv1_tile(0, 0, first=True)
            with pe.Fori(0, TILES // 2 - 1) as i:
                qkv1_tile(2 * i + 1, 1)
                qkv1_tile(2 * i + 2, 0)
            qkv1_tile(TILES - 1, 1, last=True)
            qkT1_tile(TILES - 1, 1)
            pe.sem_inc(S("pv1_ps"), 2)
            pe.sem_inc(S("sr_ps"), 2)

            def scores1(b, s, u):
                if u == 0:
                    pe.wait_ge(S("q1_ready"), b + 1)
                pe.wait_ge(S("s1_read"), 4 * b + u + 1)
                for r in range(2):
                    lo = 4 * (u % 2) + 2 * r
                    m = nc.tensor.matmul(psum[:, 2 * (u % 2) + r, 0:2 * SEQ], q1[:, s, u // 2, :],
                                         kblk[:, s, u // 2, lo:lo + 2, :].rearrange("p h j -> p (h j)"), start=True, stop=True)
                m.then_inc(S("s1_ps"), 1)

            def transpose1(b, s, n):
                if n < 4:
                    pe.wait_ge(S("p1_ready"), 4 * b + n + 1)
                pe.wait_ge(S("wT_ready"), 5 * b + n + 1)
                bank = 4 + (5 * s + n) % 2
                if n < 4:
                    for hd in range(4):
                        at = FIRST_AT[n % 2] + hd * P
                        m = nc.tensor.transpose(psum[:, bank, hd * P:(hd + 1) * P], wts[:, s, n // 2, at:at + P], ident)
                else:
                    for g in range(2):
                        m = nc.tensor.transpose(psum[0:RQ, bank, g * P:(g + 1) * P], wts[:, s, g, LAST_AT[0]:LAST_AT[0] + RQ], ident)
                m.then_inc(S("wT_ps"), 1)

            def values1(b, s):
                pe.wait_ge(S("wT_ready"), 5 * b + 7)
                pe.wait_ge(S("vdiag_ready"), b + 1)
                for hd in range(H1):
                    nc.tensor.matmul(psum[:, 6, hd * V1:(hd + 1) * V1], wT[:, s, hd, :], v1m[:, s, hd, :], start=(hd == 0), stop=False, skip_group_check=True)
                for g in range(2):
                    m = nc.tensor.matmul(psum[:, 6, g * HG * V1:(g + 1) * HG * V1], wTr[0:RQ, s, g, :],
                                         vdiag[0:RQ, s, g, :, :].rearrange("p h v -> p (h v)"), start=False, stop=(g == 1), skip_group_check=True)
                m.then_inc(S("pv1_ps"), 1)

            def scores_rest(b, s):
                pe.wait_ge(S("a1r_ready"), b + 1)
                for g in range(2):
                    m = nc.tensor.matmul(psum[0:RQ, 7, g * SEQ:(g + 1) * SEQ], qblk[:, s, g, :], qkT1[:, 2 + g, ds(b * SEQ, SEQ)], start=True, stop=True)
                m.then_inc(S("sr_ps"), 1)

            def transpose_rest(b):
                pe.wait_ge(S("wr_ready"), b + 1)
                for n, (rows, lo) in enumerate(((P, 0), (REST, P))):
                    for g in range(2):
                        m = nc.tensor.transpose(psum[0:rows, 7, (2 * n + g) * RQ:(2 * n + g + 1) * RQ], wr[0:RQ, g, lo:lo + rows], ident[0:RQ, 0:RQ])
                m.then_inc(S("wrT_ps"), 1)

            def values_rest(b, s):
                pe.wait_ge(S("wrT_ready"), b + 1)
                for g in range(2):
                    o_ = psum[0:RQ, 7, g * P:(g + 1) * P].rearrange("p (h v) -> p h v", h=HG)
                    nc.tensor.matmul(o_, wrT[:, 0, g, :], v1m[:, s, HG * g:HG * (g + 1), 0:DH1], start=True, stop=False)
                    m = nc.tensor.matmul(o_, wrT[0:REST, 1, g, :],
                                         vraw[0:REST, s, :].rearrange("p (h v) -> p h v", h=H1)[:, HG * g:HG * (g + 1), 0:DH1], start=False, stop=True)
                m.then_inc(S("avr_ps"), 1)

            def image1(b, s, turn, first=False, last=False):
                scores1(b, s, 2)
                transpose1(b, s, 0)
                if not first:
                    values1(b - 1, 1 - s)
                scores1(b, s, 3)
                transpose1(b, s, 1)
                scores_rest(b, s)
                if not last:
                    scores1(b + 1, 1 - s, 0)
                transpose1(b, s, 2)
                transpose_rest(b)
                if not last:
                    scores1(b + 1, 1 - s, 1)
                transpose1(b, s, 3)
                transpose1(b, s, 4)
                pe.wait_ge(S(f"v1_ld{s}"), 32 * (turn + 1))
                values_rest(b, s)

            scores1(0, 0, 0)
            scores1(0, 0, 1)
            image1(0, 0, 0, first=True)
            with pe.Fori(0, IMAGES // 2 - 1) as i:
                image1(2 * i + 1, 1, i)
                image1(2 * i + 2, 0, i + 1)
            image1(IMAGES - 1, 1, IMAGES // 2 - 1, last=True)
            values1(IMAGES - 1, 1)

            def a1T_tile(t, s, i):
                pe.wait_ge(S(f"aT_ld{s}"), ROWS_LD_A1 + 16 * (i + 1))
                pe.wait_ge(S("rowsT_ready"), ROWS_A1 + t + 1)
                for k in range(KC):
                    m = nc.tensor.transpose(psum[:, s, k * P:(k + 1) * P], a1T_in[:, s, k * P:(k + 1) * P], ident)
                m.then_inc(S("rowsT_ps"), 1)

            def o1_tile(g, n):
                t = g * GT + n
                pe.wait_ge(S("rowsT_ready"), ROWS_A1 + t + 3)
                pe.wait_ge(S("residual_ready"), RESIDUAL_3 + t + 3 - GT)
                for k in range(KC):
                    m = nc.tensor.matmul(psum[:, 2 + n, 0:D], xT[:, n % 2, k, :], wo1_sb[:, k, :], start=(k == 0), stop=(k == KC - 1))
                m.then_inc(S("product_ps"), 1)

            with pe.Fori(0, GROUPS) as g:
                a1T_tile(g * GT, 0, g * HT)
                for n in range(1, GT):
                    a1T_tile(g * GT + n, n % 2, g * HT + n // 2)
                    o1_tile(g, n - 1)
                o1_tile(g, GT - 1)
            pe.wait_ge(S("weights_ld"), 16 * 3)

            def x3T_tile(g, n):
                pe.wait_ge(S("xgs_ready"), g * GT + n + 1)
                pe.wait_ge(S("rowsT_ready"), ROWS_X3 + g * GT + n + 1)
                for k in range(KC):
                    m = nc.tensor.transpose(psum[:, n % 2, k * P:(k + 1) * P], xgs[:, n, k * P:(k + 1) * P], ident)
                m.then_inc(S("rowsT_ps"), 1)

            def router_tile(g, n):
                t = g * GT + n
                pe.wait_ge(S("rowsT_ready"), ROWS_X3 + t + 3)
                for k in range(KC):
                    m = nc.tensor.matmul(psum[:, 4, ds(t * HF, HF)], x3T[:, n % 2, k, :], wrout_sb[:, k, :], start=(k == 0), stop=(k == KC - 1))
                m.then_inc(S("product_ps"), 1)

            with pe.Fori(0, GROUPS) as g:
                x3T_tile(g, 0)
                for n in range(1, GT):
                    x3T_tile(g, n)
                    router_tile(g, n - 1)
                router_tile(g, GT - 1)
            pe.wait_ge(S("dve_did"), DID["pr3_ready"])
            pr3 = lg3.rearrange("p t e -> p (t e)")
            for n, cols in enumerate((P, P, 32)):
                m = nc.tensor.transpose(psum[0:cols, 5, n * P:(n + 1) * P], pr3[:, n * P:n * P + cols], ident)
            m.then_inc(S("pe_did"), 1)
            pe.wait_ge(S("dve_did"), DID["oT_ready"])
            for n, rows in enumerate((P, P, 32)):
                m = nc.tensor.transpose(psum[:, 6, n * P:n * P + rows], oT[0:rows, n * P:(n + 1) * P], ident[0:rows, 0:rows])
            m.then_inc(S("pe_did"), 1)
            pe.sem_inc(S("hg_ps"), 4)
            pe.sem_inc(S("qkvf_ps"), 2)
            pe.sem_inc(S("aof_ps"), 4)
            with pe.Fori(0, GROUPS) as g:
                for n in range(GT):
                    t, s = g * GT + n, n % 2
                    pe.wait_ge(S("xgs_ready"), TILES + t + 1)
                    pe.wait_ge(S("selb_ready"), t + 1)
                    pe.wait_ge(S("sel_all_ready"), t + 1)
                    pe.wait_ge(S("hgT_ready"), 2 * t + 2)
                    selm = selb[:, s, :, :].rearrange("p b h -> p (b h)")
                    for k in range(KC):
                        nc.tensor.matmul(psum[:, s, k * P:(k + 1) * P], xgs[:, n, k * P:(k + 1) * P], selm, start=True, stop=True)
                    nc.tensor.transpose(psum[:, 2 + s, 0:P], selm, ident).then_inc(S("hg_ps"), 1)

            def qkvf_pair(p_, s, i):
                pe.wait_ge(S(f"wf_ld{s}"), 16 * (i + 1))
                pe.wait_ge(S("hgp_ready"), p_ + 1)
                pe.wait_ge(S("vf_ready"), p_ + 1)
                for x in range(3):
                    for r in range(2):
                        for k in range(KC):
                            m = nc.tensor.matmul(psum[64 * r:64 * r + 64, s, x * SEQ:(x + 1) * SEQ], wf[:, s, k, x, 64 * r:64 * r + 64], hgp[:, s, k, r, :],
                                                 start=(k == 0), stop=(k == KC - 1))
                m.then_inc(S("qkvf_ps"), 1)

            def pair_pe(p_, s, i, i_next, last=False):
                pe.wait_ge(S("kf_ready"), p_ + 1)
                nc.tensor.matmul(psum[:, 2, 0:SEQ], blockones, kf, start=True, stop=True).then_inc(S("attf_ps"), 1)
                if not last:
                    qkvf_pair(p_ + 1, 1 - s, i_next)
                pe.wait_ge(S(f"wof_ld{s}"), 16 * (i + 1))
                pe.wait_ge(S("af_ready"), p_ + 2)
                pe.wait_ge(S("aof_ready"), 2 * p_ + 2)
                for lo, n, bank in ((0, P, 4), (P, REST, 6)):
                    for r in range(2):
                        m = nc.tensor.matmul(psum[0:n, bank + r, 0:D], af[64 * r:64 * r + 64, s, lo:lo + n], wof[64 * r:64 * r + 64, s, :], start=True, stop=True)
                    m.then_inc(S("aof_ps"), 1)

            qkvf_pair(0, 0, 0)
            with pe.Fori(0, PAIRS // 2 - 1) as i:
                pair_pe(2 * i, 0, i, i)
                pair_pe(2 * i + 1, 1, i, i + 1)
            pair_pe(PAIRS - 2, 0, PAIRS // 2 - 1, PAIRS // 2 - 1)
            pair_pe(PAIRS - 1, 1, PAIRS // 2 - 1, 0, last=True)
            pe.sem_inc(S("yf_ps"), 2)
            with pe.Fori(0, GROUPS) as g:
                for n in range(GT):
                    t = g * GT + n
                    pe.wait_ge(S("y_read"), t + 1)
                    nc.tensor.matmul(psum[:, n, 0:D], ident, xg[:, t, :], start=True, stop=False)
                    if n % HT == 0:
                        pe.wait_ge(S(f"aofl_ld{n // HT}"), 16 * (g + 2))
                    pe.wait_ge(S("sel_ready"), t + 1)
                    nc.tensor.matmul(psum[:, n, 0:D], sel_s[:, n % 2, :], aofl[:, t, :], start=False, stop=True).then_inc(S("yf_ps"), 1)


_OUTS = [((IMAGES, SEQ, D), "float32")]


def shape_constants():
    import numpy as np
    c = np.zeros((P, C_WIDTH), np.float32)
    r = np.arange(P)
    c[:, C_IDENT:C_IDENT + P] = np.eye(P)
    c[:, C_TRI:C_TRI + P] = r[:, None] < r[None, :]
    c[:, C_BLOCK:C_BLOCK + P] = r[:, None] // DHF == r[None, :] // DHF
    c[:, C_HEAD:C_HEAD + 8] = r[:, None] // 16 == np.arange(8)
    c[:, C_IOTA:C_IOTA + 16] = np.arange(16)
    c[:, C_TILE:C_TILE + SLOT_TILES] = np.arange(SLOT_TILES)
    c[:, C_Q128:C_Q128 + TILES] = P * np.arange(TILES)
    c[:, C_REST:C_REST + 8] = (r[:, None] // REST == np.arange(8))
    c[:, C_CHUNK:C_CHUNK + 32] = ((2 * np.arange(4)[:, None] + r[:, None, None] // DH0) == np.arange(8)).reshape(P, 32)
    grid = np.arange(8)
    hp, wp = (g.reshape(-1).astype(np.float32) for g in np.meshgrid(grid, grid, indexing="ij"))
    quarter = D // 4
    factor = np.float32(10000.0) ** (np.arange(quarter, dtype=np.float32) / quarter)
    a, b = hp[:, None] / factor, wp[:, None] / factor
    pos = np.concatenate([np.sin(a), np.cos(a), np.sin(b), np.cos(b)], -1).astype(np.float32)
    pos = np.concatenate([pos, pos])
    freqs = np.exp(np.arange(0, D, 2, dtype=np.float32) * np.float32(-np.log(10000.0) / D))
    ang = (np.arange(ROWS) % SEQ).astype(np.float32)[:, None] * freqs
    cs = np.stack([np.cos(ang), np.sin(ang), np.cos(ang)], 1).astype(np.float32)
    rope = np.ascontiguousarray(cs.reshape(TILES, P, 3, P).transpose(1, 0, 2, 3))
    return c, pos, rope


def layouts(i):
    import numpy as np

    def chunks(w):
        return np.ascontiguousarray(w.reshape(-1, P, w.shape[-1]).transpose(1, 0, 2))

    i = {k: np.asarray(v) for k, v in i.items()}
    c, pos, rope = shape_constants()
    x = i["x"].reshape(IMAGES, 3, 8, 16, 8, 16).transpose(1, 3, 5, 0, 2, 4).reshape(PK, P, 8, P)
    wp = i["L0_tok_Wp"].reshape(D, 16, 16, 3).transpose(3, 1, 2, 0).reshape(768, D)
    even_odd = np.concatenate([np.arange(0, D, 2), np.arange(1, D, 2)])
    qkv1 = np.concatenate([i["L1_attn_wq"][even_odd].T, i["L1_attn_wk"][even_odd].T, i["L1_attn_wv"].T], 1)
    wq = i["L1_ffn_Wq"]
    wkv = i["L1_ffn_Wkv"]
    qkvf = np.stack([wq, wkv[..., :DHF], wkv[..., DHF:]], 2)
    qkvf = qkvf.reshape(PAIRS, 2, KC, P, 3, DHF).transpose(0, 3, 2, 4, 1, 5).reshape(PAIRS, P, KC * 3 * 2 * DHF)
    bf = np.stack([i["L1_ffn_bq"], i["L1_ffn_bkv"][:, :DHF], i["L1_ffn_bkv"][:, DHF:]], 1)
    bf = bf.reshape(PAIRS, 2, 3, DHF).transpose(1, 3, 0, 2).reshape(P, PAIRS * 3)
    rowv = np.stack([i["L0_tok_b"], i["L1_attn_wo_b"], i["L1_ffn_bo"], i["L1_ffn_ln_g"], i["L1_ffn_ln_b"]])
    gu = i["L0_ffn_w_gate_up"].reshape(EXPERTS, KC, P, 2 * F).transpose(0, 2, 1, 3)
    dn = i["L0_ffn_w_down"].reshape(EXPERTS, FK, P, D).transpose(0, 2, 1, 3)
    a = {
        "patches": x.transpose(2, 1, 0, 3), "txt": i["txt"], "pos_table": pos,
        "row_vectors": np.broadcast_to(rowv, (P, 5, D)), "w_tok": chunks(wp),
        "w_qkv0": chunks(np.concatenate([i["L0_attn_Wq"], i["L0_attn_Wkv"]], 1)), "w_o0": chunks(i["L0_attn_Wo"]),
        "w_gate": chunks(i["L0_ffn_w_gate"]), "w_gu": gu.reshape(EXPERTS, P, KC * 2 * F), "w_down": dn.reshape(EXPERTS, P, FK * D),
        "w_qkv1": chunks(qkv1), "w_o1": chunks(i["L1_attn_wo_w"].T), "rope": rope, "w_router": chunks(i["L1_ffn_Wg"]),
        "w_qkvf": qkvf, "b_qkvf": bf, "w_of": i["L1_ffn_Wo"].reshape(PAIRS, P, D), "constants": c,
    }
    return {k: np.ascontiguousarray(v) for k, v in a.items()}


def kernel(**inputs):
    import numpy as _np
    import concourse.bacc as _bacc
    from concourse import mybir as _mybir
    from concourse.bass_utils import run_bass_kernel_spmd as _run

    nc = _bacc.Bacc("TRN2", target_bir_lowering=False, num_devices=1)
    arrays, args = {}, []
    for name, a in layouts(inputs).items():
        arrays[f"in_{name}"] = a
        args.append(nc.dram_tensor(f"in_{name}", a.shape, _mybir.dt.from_np(a.dtype), kind="ExternalInput").ap())
    shape, dtype = _OUTS[0]
    args.append(nc.dram_tensor("out_0", shape, _mybir.dt.from_np(_np.dtype(dtype)), kind="ExternalOutput").ap())
    fusion_kernel(nc, *args)
    r = _run(nc, [arrays], core_ids=[0])
    return r.results[0]["out_0"]
```
